# Optimizing a Trainium2 kernel written in Bass

```python
import numpy as np
import jax
import jax.numpy as jnp

def _softmax(x, axis=-1):
    return jax.nn.softmax(x, axis=axis)
def _gelu(x):
    return jax.nn.gelu(x, approximate=True)
def _silu(x):
    return jax.nn.silu(x)
def _sigmoid(x):
    return jax.nn.sigmoid(x)
def _layernorm(x, axis=-1, eps=1e-5):
    m = jnp.mean(x, axis=axis, keepdims=True)
    v = jnp.var(x, axis=axis, keepdims=True)
    return (x - m) / jnp.sqrt(v + eps)
def _scatter_add(tgt, idx, src, axis=0):
    return tgt.at[idx].add(src)
def _segment_sum(src, seg, n):
    return jax.ops.segment_sum(src, seg, n)

kernel_name = 'mk_conv_preact_d2_conv_nchw128_261b6a'

def setup_inputs(seed: int = 0):
    np.random.seed(seed)
    _w = jnp.asarray
    def _rec_inputs():
        import jax
        import jax.numpy as jnp
        _gk = jax.random.key(seed)
        x = -0.0003929 + 0.9999 * jax.random.normal(jax.random.fold_in(_gk, 1), (8, 128, 128, 128), jnp.float32)
        return x
    x = _rec_inputs()
    def _L0_conv_setup():
        import jax, jax.numpy as jnp
        import numpy as np
        B, DIM, HEADS, H, W = (8, 128, 8, 128, 128)
        EPS_NORM = 1e-12
        BN_EPS = 1e-05

        def _conv(x, w, b=None, pad=0, groups=1):
            out = jax.lax.conv_general_dilated(x, w, window_strides=(1, 1), padding=[(pad, pad), (pad, pad)], dimension_numbers=('NCHW', 'OIHW', 'NCHW'), feature_group_count=groups)
            if b is not None:
                out = out + b[None, :, None, None]
            return out

        def _l2norm_lastdim(t):
            n = jnp.sqrt(jnp.sum(jnp.abs(t) ** 2, axis=-1, keepdims=True))
            return t / jnp.maximum(n, EPS_NORM)

        def _fssa(x, temp_f, w1, b1, bn_gamma, bn_beta, bn_mean, bn_var, w2, b2, projf_w, temp_s, q1_w, q1_b, k1_w, k1_b, v1_w, v1_b, q3_w, q5_w, k3_w, k5_w, v3_w, v5_w, c3_w, c5_w, projs_w):
            b, c, h, w = x.shape
            hd = c // HEADS
            groups = c // 2
            xf = jnp.fft.fft2(x)
            qf = xf.reshape(b, HEADS, hd, h * w)
            qn = _l2norm_lastdim(qf)
            attn_f = jnp.einsum('bhcn,bhdn->bhcd', qn, qn) * temp_f[None]
            attn_f = jax.lax.complex(jax.nn.softmax(attn_f.real, axis=-1), jax.nn.softmax(attn_f.imag, axis=-1))
            out_cplx = jnp.einsum('bhcd,bhdn->bhcn', attn_f, qf)
            out_f = jnp.abs(jnp.fft.ifft2(out_cplx)).reshape(b, c, h, w)
            g = _conv(xf.real, w1, b1)
            g = (g - bn_mean[None, :, None, None]) / jnp.sqrt(bn_var[None, :, None, None] + BN_EPS)
            g = g * bn_gamma[None, :, None, None] + bn_beta[None, :, None, None]
            g = jax.nn.relu(g)
            g = jax.nn.sigmoid(_conv(g, w2, b2))
            out_f_l = jnp.abs(jnp.fft.ifft2(g * xf))
            fsa = _conv(jnp.concatenate([out_f, out_f_l], axis=1), projf_w)

            def qkv(w1x1, b1x1, w3, w5):
                t = _conv(x, w1x1, b1x1)
                return jnp.concatenate([_conv(t, w3, pad=1, groups=groups), _conv(t, w5, pad=2, groups=groups)], axis=1)
            q_s = qkv(q1_w, q1_b, q3_w, q5_w).reshape(b, HEADS, hd, h * w)
            k_s = qkv(k1_w, k1_b, k3_w, k5_w).reshape(b, HEADS, hd, h * w)
            v_s = qkv(v1_w, v1_b, v3_w, v5_w).reshape(b, HEADS, hd, h * w)
            q_s = _l2norm_lastdim(q_s)
            k_s = _l2norm_lastdim(k_s)
            attn_s = jnp.einsum('bhcn,bhdn->bhcd', q_s, k_s) * temp_s[None]
            attn_s = jax.nn.softmax(attn_s, axis=-1)
            out_s = jnp.einsum('bhcd,bhdn->bhcn', attn_s, v_s).reshape(b, c, h, w)
            out_s_l = jnp.concatenate([_conv(x, c3_w, pad=1, groups=groups), _conv(x, c5_w, pad=2, groups=groups)], axis=1)
            ssa = _conv(jnp.concatenate([out_s, out_s_l], axis=1), projs_w)
            return fsa + ssa
        key = jax.random.key(seed)
        ks = iter(jax.random.split(key, 48))
        d = DIM

        def rn(shape, scale=0.02):
            return jax.random.normal(next(ks), shape, jnp.float32) * scale
        inp = {'x': jax.random.normal(next(ks), (B, d, H, W), jnp.float32), 'temp_f': jnp.ones((HEADS, 1, 1), jnp.float32), 'w1': rn((d // 16, d, 1, 1)), 'b1': jnp.zeros((d // 16,), jnp.float32), 'bn_gamma': jnp.ones((d // 16,), jnp.float32), 'bn_beta': jnp.zeros((d // 16,), jnp.float32), 'bn_mean': jnp.zeros((d // 16,), jnp.float32), 'bn_var': jnp.ones((d // 16,), jnp.float32), 'w2': rn((d, d // 16, 1, 1)), 'b2': jnp.zeros((d,), jnp.float32), 'projf_w': rn((d, 2 * d, 1, 1)), 'temp_s': jnp.ones((HEADS, 1, 1), jnp.float32), 'q1_w': rn((d, d, 1, 1)), 'q1_b': jnp.zeros((d,), jnp.float32), 'k1_w': rn((d, d, 1, 1)), 'k1_b': jnp.zeros((d,), jnp.float32), 'v1_w': rn((d, d, 1, 1)), 'v1_b': jnp.zeros((d,), jnp.float32), 'q3_w': rn((d // 2, 2, 3, 3)), 'q5_w': rn((d // 2, 2, 5, 5)), 'k3_w': rn((d // 2, 2, 3, 3)), 'k5_w': rn((d // 2, 2, 5, 5)), 'v3_w': rn((d // 2, 2, 3, 3)), 'v5_w': rn((d // 2, 2, 5, 5)), 'c3_w': rn((d // 2, 2, 3, 3)), 'c5_w': rn((d // 2, 2, 5, 5)), 'projs_w': rn((d, 2 * d, 1, 1))}
        return inp
    _L0_conv_all = _L0_conv_setup()
    _L0_conv_in = {k: v for k, v in _L0_conv_all.items() if k in ('temp_f', 'w1', 'b1', 'bn_gamma', 'bn_beta', 'bn_mean', 'bn_var', 'w2', 'b2', 'projf_w', 'temp_s', 'q1_w', 'q1_b', 'k1_w', 'k1_b', 'v1_w', 'v1_b', 'q3_w', 'q5_w', 'k3_w', 'k5_w', 'v3_w', 'v5_w', 'c3_w', 'c5_w', 'projs_w', )}
    del _L0_conv_all

    def _L1_conv_setup():
        import jax, jax.numpy as jnp
        import numpy as np
        D_MODEL = 128
        OUT_C = 128
        D_STATE = 16
        D_CONV = 4
        EXPAND = 2
        D_INNER = EXPAND * D_MODEL
        DT_RANK = (D_MODEL + 15) // 16
        key = jax.random.key(seed)
        ks = jax.random.split(key, 8)
        B, H, W = (16, 64, 64)
        x = jax.random.normal(ks[0], (B, D_MODEL, H, W), jnp.float32)
        s = 0.02
        W_in = jax.random.normal(ks[1], (D_MODEL, 2 * D_INNER), jnp.float32) * s
        conv_w = jax.random.normal(ks[2], (D_INNER, D_CONV), jnp.float32) * D_CONV ** (-0.5)
        conv_b = jnp.zeros((D_INNER,), jnp.float32)
        W_xproj = jax.random.normal(ks[3], (D_INNER, DT_RANK + 2 * D_STATE), jnp.float32) * s
        W_dt = jax.random.normal(ks[4], (DT_RANK, D_INNER), jnp.float32) * DT_RANK ** (-0.5)
        b_dt = jnp.full((D_INNER,), float(np.log(np.expm1(0.01))), jnp.float32)
        A_log = jnp.log(jnp.tile(jnp.arange(1, D_STATE + 1, dtype=jnp.float32), (D_INNER, 1)))
        D_param = jnp.ones((D_INNER,), jnp.float32)
        W_out = jax.random.normal(ks[5], (D_INNER, OUT_C), jnp.float32) * s
        return {'x': x, 'W_in': W_in, 'conv_w': conv_w, 'conv_b': conv_b, 'W_xproj': W_xproj, 'W_dt': W_dt, 'b_dt': b_dt, 'A_log': A_log, 'D_param': D_param, 'W_out': W_out}
    _L1_conv_all = _L1_conv_setup()
    _L1_conv_in = {k: v for k, v in _L1_conv_all.items() if k in ('W_in', 'conv_w', 'conv_b', 'W_xproj', 'W_dt', 'b_dt', 'A_log', 'D_param', 'W_out', )}
    del _L1_conv_all

    return {
        "x": x,
        "L0_conv_temp_f": _L0_conv_in["temp_f"],
        "L0_conv_w1": _L0_conv_in["w1"],
        "L0_conv_b1": _L0_conv_in["b1"],
        "L0_conv_bn_gamma": _L0_conv_in["bn_gamma"],
        "L0_conv_bn_beta": _L0_conv_in["bn_beta"],
        "L0_conv_bn_mean": _L0_conv_in["bn_mean"],
        "L0_conv_bn_var": _L0_conv_in["bn_var"],
        "L0_conv_w2": _L0_conv_in["w2"],
        "L0_conv_b2": _L0_conv_in["b2"],
        "L0_conv_projf_w": _L0_conv_in["projf_w"],
        "L0_conv_temp_s": _L0_conv_in["temp_s"],
        "L0_conv_q1_w": _L0_conv_in["q1_w"],
        "L0_conv_q1_b": _L0_conv_in["q1_b"],
        "L0_conv_k1_w": _L0_conv_in["k1_w"],
        "L0_conv_k1_b": _L0_conv_in["k1_b"],
        "L0_conv_v1_w": _L0_conv_in["v1_w"],
        "L0_conv_v1_b": _L0_conv_in["v1_b"],
        "L0_conv_q3_w": _L0_conv_in["q3_w"],
        "L0_conv_q5_w": _L0_conv_in["q5_w"],
        "L0_conv_k3_w": _L0_conv_in["k3_w"],
        "L0_conv_k5_w": _L0_conv_in["k5_w"],
        "L0_conv_v3_w": _L0_conv_in["v3_w"],
        "L0_conv_v5_w": _L0_conv_in["v5_w"],
        "L0_conv_c3_w": _L0_conv_in["c3_w"],
        "L0_conv_c5_w": _L0_conv_in["c5_w"],
        "L0_conv_projs_w": _L0_conv_in["projs_w"],
        "L1_conv_W_in": _L1_conv_in["W_in"],
        "L1_conv_conv_w": _L1_conv_in["conv_w"],
        "L1_conv_conv_b": _L1_conv_in["conv_b"],
        "L1_conv_W_xproj": _L1_conv_in["W_xproj"],
        "L1_conv_W_dt": _L1_conv_in["W_dt"],
        "L1_conv_b_dt": _L1_conv_in["b_dt"],
        "L1_conv_A_log": _L1_conv_in["A_log"],
        "L1_conv_D_param": _L1_conv_in["D_param"],
        "L1_conv_W_out": _L1_conv_in["W_out"],
    }

def reference(x, L0_conv_temp_f, L0_conv_w1, L0_conv_b1, L0_conv_bn_gamma, L0_conv_bn_beta, L0_conv_bn_mean, L0_conv_bn_var, L0_conv_w2, L0_conv_b2, L0_conv_projf_w, L0_conv_temp_s, L0_conv_q1_w, L0_conv_q1_b, L0_conv_k1_w, L0_conv_k1_b, L0_conv_v1_w, L0_conv_v1_b, L0_conv_q3_w, L0_conv_q5_w, L0_conv_k3_w, L0_conv_k5_w, L0_conv_v3_w, L0_conv_v5_w, L0_conv_c3_w, L0_conv_c5_w, L0_conv_projs_w, L1_conv_W_in, L1_conv_conv_w, L1_conv_conv_b, L1_conv_W_xproj, L1_conv_W_dt, L1_conv_b_dt, L1_conv_A_log, L1_conv_D_param, L1_conv_W_out):
    import jax
    import jax.numpy as jnp
    def _L0_conv_ref(x, temp_f, w1, b1, bn_gamma, bn_beta, bn_mean, bn_var, w2, b2, projf_w, temp_s, q1_w, q1_b, k1_w, k1_b, v1_w, v1_b, q3_w, q5_w, k3_w, k5_w, v3_w, v5_w, c3_w, c5_w, projs_w):
        import jax, jax.numpy as jnp
        import numpy as np
        B, DIM, HEADS, H, W = (8, 128, 8, 128, 128)
        EPS_NORM = 1e-12
        BN_EPS = 1e-05

        def _conv(x, w, b=None, pad=0, groups=1):
            out = jax.lax.conv_general_dilated(x, w, window_strides=(1, 1), padding=[(pad, pad), (pad, pad)], dimension_numbers=('NCHW', 'OIHW', 'NCHW'), feature_group_count=groups)
            if b is not None:
                out = out + b[None, :, None, None]
            return out

        def _l2norm_lastdim(t):
            n = jnp.sqrt(jnp.sum(jnp.abs(t) ** 2, axis=-1, keepdims=True))
            return t / jnp.maximum(n, EPS_NORM)

        def _fssa(x, temp_f, w1, b1, bn_gamma, bn_beta, bn_mean, bn_var, w2, b2, projf_w, temp_s, q1_w, q1_b, k1_w, k1_b, v1_w, v1_b, q3_w, q5_w, k3_w, k5_w, v3_w, v5_w, c3_w, c5_w, projs_w):
            b, c, h, w = x.shape
            hd = c // HEADS
            groups = c // 2
            xf = jnp.fft.fft2(x)
            qf = xf.reshape(b, HEADS, hd, h * w)
            qn = _l2norm_lastdim(qf)
            attn_f = jnp.einsum('bhcn,bhdn->bhcd', qn, qn) * temp_f[None]
            attn_f = jax.lax.complex(jax.nn.softmax(attn_f.real, axis=-1), jax.nn.softmax(attn_f.imag, axis=-1))
            out_cplx = jnp.einsum('bhcd,bhdn->bhcn', attn_f, qf)
            out_f = jnp.abs(jnp.fft.ifft2(out_cplx)).reshape(b, c, h, w)
            g = _conv(xf.real, w1, b1)
            g = (g - bn_mean[None, :, None, None]) / jnp.sqrt(bn_var[None, :, None, None] + BN_EPS)
            g = g * bn_gamma[None, :, None, None] + bn_beta[None, :, None, None]
            g = jax.nn.relu(g)
            g = jax.nn.sigmoid(_conv(g, w2, b2))
            out_f_l = jnp.abs(jnp.fft.ifft2(g * xf))
            fsa = _conv(jnp.concatenate([out_f, out_f_l], axis=1), projf_w)

            def qkv(w1x1, b1x1, w3, w5):
                t = _conv(x, w1x1, b1x1)
                return jnp.concatenate([_conv(t, w3, pad=1, groups=groups), _conv(t, w5, pad=2, groups=groups)], axis=1)
            q_s = qkv(q1_w, q1_b, q3_w, q5_w).reshape(b, HEADS, hd, h * w)
            k_s = qkv(k1_w, k1_b, k3_w, k5_w).reshape(b, HEADS, hd, h * w)
            v_s = qkv(v1_w, v1_b, v3_w, v5_w).reshape(b, HEADS, hd, h * w)
            q_s = _l2norm_lastdim(q_s)
            k_s = _l2norm_lastdim(k_s)
            attn_s = jnp.einsum('bhcn,bhdn->bhcd', q_s, k_s) * temp_s[None]
            attn_s = jax.nn.softmax(attn_s, axis=-1)
            out_s = jnp.einsum('bhcd,bhdn->bhcn', attn_s, v_s).reshape(b, c, h, w)
            out_s_l = jnp.concatenate([_conv(x, c3_w, pad=1, groups=groups), _conv(x, c5_w, pad=2, groups=groups)], axis=1)
            ssa = _conv(jnp.concatenate([out_s, out_s_l], axis=1), projs_w)
            return fsa + ssa
        return _fssa(x, temp_f, w1, b1, bn_gamma, bn_beta, bn_mean, bn_var, w2, b2, projf_w, temp_s, q1_w, q1_b, k1_w, k1_b, v1_w, v1_b, q3_w, q5_w, k3_w, k5_w, v3_w, v5_w, c3_w, c5_w, projs_w)

    def _L1_conv_ref(x, W_in, conv_w, conv_b, W_xproj, W_dt, b_dt, A_log, D_param, W_out):
        import jax, jax.numpy as jnp
        import numpy as np
        D_MODEL = 128
        OUT_C = 128
        D_STATE = 16
        D_CONV = 4
        EXPAND = 2
        D_INNER = EXPAND * D_MODEL
        DT_RANK = (D_MODEL + 15) // 16
        b, c, h, w = x.shape
        u = x.transpose(0, 2, 3, 1).reshape(b, h * w, c)
        xz = u @ W_in
        xs, z = jnp.split(xz, 2, axis=-1)
        xt = xs.transpose(0, 2, 1)
        xt = jax.lax.conv_general_dilated(xt, conv_w[:, None, :], (1,), [(D_CONV - 1, 0)], feature_group_count=D_INNER) + conv_b[None, :, None]
        xc = jax.nn.silu(xt.transpose(0, 2, 1))
        dbl = xc @ W_xproj
        dt, Bm, Cm = jnp.split(dbl, [DT_RANK, DT_RANK + D_STATE], axis=-1)
        delta = jax.nn.softplus(dt @ W_dt + b_dt)
        A = -jnp.exp(A_log)

        def step(hs, inp):
            d_t, B_t, C_t, u_t = inp
            dA = jnp.exp(d_t[:, :, None] * A)
            h_new = dA * hs + (d_t * u_t)[:, :, None] * B_t[:, None, :]
            y_t = jnp.einsum('bdn,bn->bd', h_new, C_t)
            return (h_new, y_t)
        xs_scan = (delta.transpose(1, 0, 2), Bm.transpose(1, 0, 2), Cm.transpose(1, 0, 2), xc.transpose(1, 0, 2))
        h0 = jnp.zeros((b, D_INNER, D_STATE), delta.dtype)
        _, ys = jax.lax.scan(step, h0, xs_scan)
        y = ys.transpose(1, 0, 2) + xc * D_param
        y = y * jax.nn.silu(z)
        out = y @ W_out
        out = out.reshape(b, h, w, OUT_C).transpose(0, 3, 2, 1)
        return out

    def _gn(v, G=32, eps=1e-5):
        B_, C_, H_, W_ = v.shape
        g = v.reshape(B_, G, C_ // G, H_, W_)
        m = jnp.mean(g, axis=(2, 3, 4), keepdims=True)
        s = jnp.var(g, axis=(2, 3, 4), keepdims=True)
        return ((g - m) / jnp.sqrt(s + eps)).reshape(v.shape)

    def _ln_c(v, eps=1e-6):
        m = jnp.mean(v, axis=1, keepdims=True)
        s = jnp.var(v, axis=1, keepdims=True)
        return (v - m) / jnp.sqrt(s + eps)

    def _ln_t(v, eps=1e-5):
        m = jnp.mean(v, axis=-1, keepdims=True)
        s = jnp.var(v, axis=-1, keepdims=True)
        return (v - m) / jnp.sqrt(s + eps)

    def _to_tokens(v):
        B_, C_, H_, W_ = v.shape
        return v.reshape(B_, C_, H_ * W_).transpose(0, 2, 1)
    def _from_tokens(t, like):
        B_, C_, H_, W_ = like.shape
        return t.transpose(0, 2, 1).reshape(B_, C_, H_, W_)

    x = x + _L0_conv_ref(_gn(x), L0_conv_temp_f, L0_conv_w1, L0_conv_b1, L0_conv_bn_gamma, L0_conv_bn_beta, L0_conv_bn_mean, L0_conv_bn_var, L0_conv_w2, L0_conv_b2, L0_conv_projf_w, L0_conv_temp_s, L0_conv_q1_w, L0_conv_q1_b, L0_conv_k1_w, L0_conv_k1_b, L0_conv_v1_w, L0_conv_v1_b, L0_conv_q3_w, L0_conv_q5_w, L0_conv_k3_w, L0_conv_k5_w, L0_conv_v3_w, L0_conv_v5_w, L0_conv_c3_w, L0_conv_c5_w, L0_conv_projs_w)
    x = x + _L1_conv_ref(_gn(x), L1_conv_W_in, L1_conv_conv_w, L1_conv_conv_b, L1_conv_W_xproj, L1_conv_W_dt, L1_conv_b_dt, L1_conv_A_log, L1_conv_D_param, L1_conv_W_out)
    return x


_drawn_inputs = setup_inputs


def setup_inputs(seed=0):
    import zlib

    import numpy as np

    out = dict(_drawn_inputs(seed))
    spreads = {'L0_conv_temp_f': (1.0, 0.2),
     'L0_conv_b1': (0.0, 0.1),
     'L0_conv_bn_gamma': (1.0, 0.2),
     'L0_conv_bn_beta': (0.0, 0.1),
     'L0_conv_bn_mean': (0.0, 0.1),
     'L0_conv_bn_var': (1.0, 0.2),
     'L0_conv_b2': (0.0, 0.1),
     'L0_conv_temp_s': (1.0, 0.2),
     'L0_conv_q1_b': (0.0, 0.1),
     'L0_conv_k1_b': (0.0, 0.1),
     'L0_conv_v1_b': (0.0, 0.1),
     'L1_conv_conv_b': (0.0, 0.1),
     'L1_conv_b_dt': (-4.600165843963623, 0.2),
     'L1_conv_D_param': (1.0, 0.2)}
    factors = {}
    for name, (base, spread) in spreads.items():
        noise = np.random.default_rng([zlib.crc32(name.encode()), seed]).standard_normal(out[name].shape)
        drawn = base * np.exp(spread * noise) if base else spread * noise
        out[name] = jnp.asarray(drawn.astype(out[name].dtype))
    for name, factor in factors.items():
        out[name] = (out[name] * factor).astype(out[name].dtype)
    return out
```

```python
from contextlib import ExitStack
import numpy as np
import concourse.bass as bass
from concourse import mybir

F32 = mybir.dt.float32
BF16 = mybir.dt.bfloat16
ALU = mybir.AluOpType
ACT = mybir.ActivationFunctionType
AX = mybir.AxisListType

P = 128
HW = 16384
HALF = 65
UG, JG = 13, 8
NUG = HALF // UG
T5 = 25
INNER = [5 * i + j for i in (1, 2, 3) for j in (1, 2, 3)]
WP = P + 4
TAPS = T5 * P


def constants():
    i = np.arange(P)
    cos, sin = (f(2 * np.pi * (np.outer(i, i) % P) / P) for f in (np.cos, np.sin))
    wt = np.where((i[:HALF] == 0) | (i[:HALF] == 64), 1.0, 2.0)[:, None] / HW
    o64 = np.arange(64)
    head = (i[:, None] // 16 == i // 16) * 1.0
    valid = np.zeros((T5, 8, P))
    for t in range(T5):
        dh, dw = t // 5 - 2, t % 5 - 2
        for n, h in enumerate((0, 1, 64, 64, 64, 64, 126, 127)):
            valid[t, n] = (0 <= h + dh < P) * ((0 <= i + dw) & (i + dw < P))
    spread = np.zeros((9, UG, UG * JG + 1))
    for u in range(UG):
        spread[8, u, UG * JG] = 1
        for j in range(JG):
            spread[j, u, u * JG + j] = 1
    parts = {
        "fwd": np.concatenate([cos[:, :HALF], sin[:, 1:64]], 1),
        "cs": np.concatenate([cos, -sin], 1), "sc": np.concatenate([sin, cos], 1),
        "back": np.concatenate([wt * cos[:HALF], wt * sin[:HALF]], 1),
        "eye": np.eye(P), "ones": np.ones((P, P)),
        "head": head, "head64": ((i[:, None] // 16) % 4 == o64 // 16),
        "four": (i[:, None] // 4 == i // 4) / 4,
        "mixc": head * np.cos(2 * np.pi * np.outer(i, i) / 16) / 16, "mixs": head * np.sin(2 * np.pi * np.outer(i, i) / 16) / 16,
        "mixi": head * (i % 16 == 0) / 16,
        "shift": (i[:, None] == 64 + o64), "valid": valid.reshape(T5, -1),
        "heads": (np.arange(8)[:, None] == i // 16), "rep8": (np.arange(8)[:, None] == np.arange(UG * JG) % JG),
        "mpair": (i[:, None] // 2 == o64), "mgroup": (i[:, None] % 64 == o64),
        "spread": spread.reshape(9, -1), "tap": np.broadcast_to(np.eye(T5).reshape(1, -1), (P, T5 * T5)),
    }
    at, cols = {}, 0
    for k, v in parts.items():
        at[k] = (cols, v.shape[0], v.shape[1])
        cols += v.shape[1]
    packed = np.zeros((P, cols), np.float32)
    for k, v in parts.items():
        packed[:v.shape[0], at[k][0]:at[k][0] + v.shape[1]] = v
    return packed, at


def shifts():
    i = np.arange(P)
    t = i[None, None, :] - i[:, None, None] + i[None, :, None] / P
    whole = t == np.round(t)
    safe = np.where(whole, 0.5, t)
    series = (np.exp(2j * np.pi * safe) - 1) / (np.exp(2j * np.pi * safe / P) - 1) / P
    d = np.where(whole, (t % P == 0) * (1.0 + 0j), series)
    return np.concatenate([d.real, d.imag], 2).astype(np.float32)


class Count:

    def __init__(self, sem, per):
        self.sem, self.per = sem, per

    def at(self, b, n):
        return b * self.per + self.per + n


def layer0(nc, B, x, table, shift_d, w, wts, y_d, of_d, x1, gn2):
    _, at = constants()
    ctx = ExitStack()
    with ctx:
        sb = lambda name, shape, dt=F32: ctx.enter_context(nc.sbuf_tensor(name, shape, dt))
        sem = lambda name: ctx.enter_context(nc.semaphore(name))
        counters = []

        def count(name, per):
            counters.append(Count(sem(name), per))
            return counters[-1]

        setup_from = at["mpair"][0]
        ncols = at["tap"][0] + at["tap"][2]
        ctab = sb("ctab", [P, setup_from])
        xpad = sb("xpad", [P, WP, WP])
        xpad_flat = xpad[:, :, :].rearrange("p h w -> p (h w)")
        region = sb("region", [P, 17408])
        work = sb("work", [P, 11264])
        k = {n: ctab[:r, c0:c0 + n_] for n, (c0, r, n_) in at.items() if c0 < setup_from}
        stab = xpad_flat[:, 0:ncols - setup_from]
        ks = {n: stab[:r, c0 - setup_from:c0 - setup_from + n_] for n, (c0, r, n_) in at.items() if c0 >= setup_from}
        valid = k["valid"].rearrange("t (r n) -> t r n", n=P)
        XR = region[:, 0:P * HALF].rearrange("p (c u) -> p c u", u=HALF)
        XI = region[:, P * HALF:2 * P * HALF].rearrange("p (c u) -> p c u", u=HALF)
        WA = region[:, 0:9 * P].rearrange("p (t o) -> p t o", o=P)
        cut = [9 * P + i * TAPS for i in range(6)]
        WB, WV, WC, UU, MM = (region[:, cut[i]:cut[i + 1]] for i in range(5))

        pt = sb("pt", [P, 4, P])
        v1 = sb("v1", [P, P])
        w1t = sb("w1t", [P, JG])
        gate_w = sb("gate_w", [UG * JG + 1, UG, P])
        gate_sb = sb("gate_sb", [UG * JG, 2])
        temps = sb("temps", [P, 2])
        vtap = sb("vtap", [P, T5, T5])
        bias_ab = sb("bias_ab", [T5, 2, P])
        bias_v = sb("bias_v", [T5, P])
        small = sb("small", [P, 64])
        stats = sb("stats", [P, 32, 6])
        mix_t = sb("mix_t", [P, 3, P])
        relu_r = sb("relu_r", [P, NUG, P])
        A8 = sb("A8", [P, HALF, JG])
        B8 = sb("B8", [P, HALF, JG])
        norms = sb("norms", [P, 2, 32])

        wk = lambda o, n: work[:, o:o + n]
        xh = wk(0, 4096).rearrange("p (s c w) -> p s c w", s=2, w=P)
        AB = wk(4096, 1024).rearrange("p (s c u) -> p s c u", s=2, u=P)
        T8 = wk(5120, 1024).rearrange("p (w j) -> p w j", j=JG)
        gates = wk(0, UG * P).rearrange("p (u c) -> p u c", c=P)
        Z = wk(2048, 2048).rearrange("p (s c n) -> p s c n", s=2, c=4)
        Yb = wk(4096, 1024).rearrange("p (s c w) -> p s c w", s=2, w=P)
        rows = wk(6144, 256)
        diag = wk(6400, 256)
        sq = [wk(6656 + P * i, P) for i in range(6)]
        rowbuf = wk(0, 512)
        turned = wk(512, 512)
        shifted = wk(1024, 1024)
        sq2 = [wk(2048 + 512 * i, 512) for i in range(2)]
        kbuf = [wk(7424 + 1024 * i, 1024) for i in range(2)]
        kbuf3 = [v_.rearrange("p (j n) -> p j n", j=4) for v_ in kbuf]
        OF = region[:, 0:HW].rearrange("p (a h) -> p a h", h=P)
        qa = [wk(512 * i, 512) for i in range(2)]
        tt = [wk(1024 + 512 * i, 512).rearrange("p (j o) -> p j o", o=P) for i in range(2)]
        of = [wk(2048 + 512 * i, 512) for i in range(2)]
        sqa = [wk(3072 + 512 * i, 512) for i in range(2)]
        ych = [wk(4096 + 512 * i, 512) for i in range(2)]
        xch = [wk(5120 + 512 * i, 512) for i in range(2)]
        x1c = [wk(7424 + 512 * i, 512) for i in range(2)]
        afull = wk(8448, P)
        ap_ = wk(8576, P)
        sparse = wk(0, T5 * 64).rearrange("p (t o) -> p t o", o=64)
        btap = wk(1600, T5 * T5).rearrange("p (t s) -> p t s", s=T5)
        wq = wk(2304, P)
        w5 = wk(2432, T5)
        w2 = wk(2464, 50).rearrange("p (i t) -> p i t", i=2)
        bcol = wk(2520, 1)
        wproj = wk(2528, 256)
        w1n = wk(2784, P)
        w2b = wk(2912, P)
        par8 = wk(3040, 8)
        tin = wk(3048, 2)

        bk = [ctx.enter_context(nc.psum_tensor(f"bk{i}", [P, 512], F32)) for i in range(8)]

        setup = ExitStack()
        s_ld = setup.enter_context(nc.semaphore("s_setup_load"))
        s_pe = setup.enter_context(nc.semaphore("s_setup_pe"))
        s_ve = setup.enter_context(nc.semaphore("s_setup_dve"))
        s_go = setup.enter_context(nc.semaphore("s_setup_next"))
        s_wr = setup.enter_context(nc.semaphore("s_setup_store"))
        s_link = setup.enter_context(nc.semaphore("s_setup_link"))
        s_sq = setup.enter_context(nc.semaphore("s_setup_sqrt"))
        qk = [("q", 0), ("k", 64)]

        def put(dst, src):
            return lambda sp: sp.dma_start(dst, src, allow_slow_non_contiguous=True).then_inc(s_ld, 16)

        conv_flat = lambda a: a.rearrange("o i a b -> (o i) (a b)")
        W5 = w5.rearrange("p (a b) -> p a b", b=5)
        table_loads = [put(ctab[:, :], table[:, 0:setup_from]), put(stab, table[:, setup_from:])]
        small_loads = [
            put(w1n[0:8, :], w["w1"].rearrange("o i a b -> o (i a b)")),
            put(w2b[0:8, :], w["w2"].rearrange("o i a b -> (i a b) o")), put(w2b[8:9, :], w["b2"].unsqueeze(0)),
            *(put(par8[0:8, n:n + 1], w[name].unsqueeze(1)) for n, name in enumerate(("b1", "bn_gamma", "bn_beta", "bn_mean", "bn_var"))),
            put(tin[0:8, 0:1], w["temp_f"].rearrange("h a b -> h (a b)")), put(tin[0:8, 1:2], w["temp_s"].rearrange("h a b -> h (a b)")),
            put(v1[:, :], w["v1_w"].rearrange("o i a b -> o (i a b)")),
        ]
        flats = [w["projf_w"].rearrange("o i a b -> o (i a b)"), w["projs_w"].rearrange("o i a b -> o (i a b)")]
        WBt = WB.rearrange("p (t o) -> p t o", o=P)
        WAfull = UU.rearrange("p (t o) -> p t o", o=P)
        WVt = WV.rearrange("p (t m) -> p t m", m=P)
        WCt = WC.rearrange("p (t m) -> p t m", m=P)

        block = setup.enter_context(nc.Block())
        loads_done, pe_done, ve_done, go = [0], [0], [0], [0]

        plan = []
        plan.append(("first", table_loads + small_loads))
        for n in range(2):
            plan.append((f"proj{n}", [put(wproj, flats[n])]))
        for nm, off in qk:
            for size in (3, 5):
                ld = [put(wq, w[nm + "1_w"].rearrange("o i a b -> o (i a b)")), put(bcol, w[nm + "1_b"].unsqueeze(1))]
                if size == 5:
                    ld.append(put(w5, conv_flat(w[nm + "5_w"])))
                else:
                    ld += [put(W5[:, 1 + a, 1:4], w[nm + "3_w"].rearrange("o i a b -> (o i) a b")[:, a, :]) for a in range(3)]
                plan.append((f"qk {off} {size}", ld))
        for n, nm in enumerate("vc"):
            ld = [put(w2[64:128, :, :], w[nm + "5_w"].rearrange("o i a b -> o i (a b)"))]
            ld += [put(w2[0:64, i, :].rearrange("p (a b) -> p a b", b=5)[:, 1 + a, 1:4], w[nm + "3_w"][:, i, a, :]) for i in range(2) for a in range(3)]
            if n == 0:
                ld.append(put(bcol, w["v1_b"].unsqueeze(1)))
            plan.append((f"vc {n}", ld))
        ld_at, total = [], 0
        for _, ld in plan:
            total += len(ld)
            ld_at.append(total * 16)
        NSTEP = len(plan)

        @block.sync
        def _(sp):
            for n, (_, loads) in enumerate(plan):
                sp.wait_ge(s_go, n + 1)
                for ld in loads:
                    ld(sp)
            sp.wait_ge(s_go, NSTEP + 1)
            for n, dst in enumerate((UU, WB, WV, WC)):
                sp.dma_start(wts[:, n * TAPS:(n + 1) * TAPS], dst).then_inc(s_wr, 16)
            sp.wait_ge(s_wr, 64)

        @block.tensor
        def _(pe):
            c = [0]

            def after(n):
                pe.wait_ge(s_ve, n)

            ve = iter(range(1, 1000))
            for n, (name, _) in enumerate(plan):
                pe.wait_ge(s_ld, ld_at[n])
                if name == "first":
                    after(next(ve))
                    nc.tensor.matmul(bk[0][0:UG * JG, 0:2], k["rep8"], par8[0:8, 6:8], start=True, stop=True)
                    nc.tensor.matmul(bk[1][:, 0:2], k["heads"], tin[0:8, :], start=True, stop=True)
                    nc.tensor.transpose(bk[2][:, 0:8], w1n[0:8, :], k["eye"][0:8, 0:8])
                    for u in range(UG):
                        m = nc.tensor.matmul(bk[3 + u // 4][0:UG * JG + 1, (u % 4) * P:(u % 4 + 1) * P], ks["spread"].rearrange("p (u m) -> p u m", u=UG)[:, u, :], w2b[0:9, :], start=True, stop=True)
                    m.then_inc(s_pe, 1)
                elif name.startswith("proj"):
                    for i in range(2):
                        m = nc.tensor.transpose(bk[i][:, 0:P], wproj[:, i * P:(i + 1) * P], k["eye"])
                    m.then_inc(s_pe, 1)
                elif name.startswith("qk"):
                    after(next(ve))
                    for t in range(0, T5, 8):
                        e = min(T5, t + 8)
                        nc.tensor.matmul(bk[t // 8][:, 0:(e - t) * 64], wq, sparse[:, t:e, :], start=True, stop=True)
                    for t in range(T5):
                        m = nc.tensor.matmul(bk[4][0:T5, 0:64], btap[:, t, :], sparse[:, t, :], start=(t == 0), stop=(t == T5 - 1))
                    m.then_inc(s_pe, 1)
                if name != "" and not name.startswith("vc"):
                    after(next(ve))

        @block.vector
        def _(dve):
            done = [0]

            def did(op):
                done[0] += 1
                op.then_inc(s_ve, 1)

            s_ch = [0]

            def link(op):
                s_ch[0] += 1
                op.then_inc(s_link, 1)
                dve.wait_ge(s_link, s_ch[0])

            link(nc.vector.memset(w5, 0.0))
            nc.vector.memset(w2, 0.0).then_inc(s_go, 1)
            npe = iter(range(1, 1000))
            for n, (name, _) in enumerate(plan):
                dve.wait_ge(s_ld, ld_at[n])
                if name == "first":
                    g = lambda i: par8[0:8, i:i + 1]
                    link(nc.vector.tensor_scalar(g(5), g(4), 1e-5, None, ALU.add))
                    dve.wait_ge(s_sq, 1)
                    link(nc.vector.reciprocal(g(5), g(5)))
                    link(nc.vector.tensor_tensor(g(6), g(1), g(5), ALU.mult))
                    link(nc.vector.tensor_tensor(g(7), g(0), g(3), ALU.subtract))
                    link(nc.vector.tensor_tensor(g(7), g(7), g(6), ALU.mult))
                    did(nc.vector.tensor_tensor(g(7), g(7), g(2), ALU.add))
                    dve.wait_ge(s_pe, next(npe))
                    nc.vector.tensor_copy(gate_sb[:, :], bk[0][0:UG * JG, 0:2])
                    nc.vector.tensor_copy(temps[:, :], bk[1][:, 0:2])
                    nc.vector.tensor_copy(w1t[:, :], bk[2][:, 0:8])
                    for i in range(4):
                        m = min(4, UG - 4 * i)
                        link(nc.vector.tensor_copy(gate_w[:, 4 * i:4 * i + m, :], bk[3 + i][0:UG * JG + 1, 0:m * P]))
                    link(nc.vector.memset(relu_r[:, :, :], 1.0))
                    did(nc.vector.memset(B8[:, :, :], 0.0))
                    nc.vector.memset(norms[:, 0, 0:1], 0.0).then_inc(s_go, 1)
                elif name.startswith("proj"):
                    dve.wait_ge(s_pe, next(npe))
                    s = int(name[4:])
                    link(nc.vector.tensor_copy(pt[:, 2 * s, :], bk[0][:, 0:P]))
                    did(nc.vector.tensor_copy(pt[:, 2 * s + 1, :], bk[1][:, 0:P]))
                    nc.vector.memset(norms[:, 0, 1:2], 0.0).then_inc(s_go, 1)
                elif name.startswith("qk"):
                    _, off, size = name.split()
                    off = int(off)
                    link(nc.vector.tensor_tensor(btap, ks["tap"].rearrange("p (t s) -> p t s", s=T5), bcol.unsqueeze(1).broadcast_to([P, T5, T5]), ALU.mult))
                    did(nc.vector.tensor_tensor(sparse, ks["mpair"].unsqueeze(1).broadcast_to([P, T5, 64]), w5.unsqueeze(2).broadcast_to([P, T5, 64]), ALU.mult))
                    dve.wait_ge(s_pe, next(npe))
                    dst = WBt if size == "5" else WAfull
                    for i in range(4):
                        m = min(8, T5 - 8 * i)
                        link(nc.vector.tensor_copy(dst[:, 8 * i:8 * i + m, off:off + 64], bk[i][:, 0:m * 64].rearrange("p (t o) -> p t o", o=64)))
                    did(nc.vector.tensor_copy(bias_ab[:, int(size == "5"), off:off + 64], bk[4][0:T5, 0:64]))
                    dve.wait_ge(s_ve, done[0])
                    nc.vector.memset(w5, 0.0).then_inc(s_go, 1)
                else:
                    s = int(name[3:])
                    for i in range(2):
                        dst = (WVt, WCt)[s].rearrange("p t (g i) -> p t g i", i=2)[:, :, :, i]
                        link(nc.vector.tensor_tensor(dst, ks["mgroup"].unsqueeze(1).broadcast_to([P, T5, 64]), w2[:, i, :].unsqueeze(2).broadcast_to([P, T5, 64]), ALU.mult))
                    if s == 0:
                        link(nc.vector.tensor_tensor(vtap[:, :, :], ks["tap"].rearrange("p (t s) -> p t s", s=T5), bcol.unsqueeze(1).broadcast_to([P, T5, T5]), ALU.mult))
                    nc.vector.memset(w2, 0.0).then_inc(s_go, 1)

        @block.scalar
        def _(act):
            act.wait_ge(s_ld, ld_at[0])
            act.wait_ge(s_link, 2)
            nc.scalar.activation(par8[0:8, 5:6], par8[0:8, 5:6], ACT.Sqrt).then_inc(s_sq, 1)

        setup.close()
        TAPAT = [(t // 5, t % 5) for t in range(T5)]
        NK = 32
        sxp = [sem(f"s_x_rows_{i}") for i in range(4)]
        sxh = [sem(f"s_columns_{i}") for i in range(2)]
        syc = [sem(f"s_y_chunk_{i}") for i in range(2)]
        sxc = [sem(f"s_x_chunk_{i}") for i in range(2)]
        s_yst = [sem(f"s_y_stored_{i}") for i in range(2)]
        s_x1st = [sem(f"s_x1_stored_{i}") for i in range(2)]
        s_wl = sem("s_weights_loaded")
        s_gst = sem("s_gn_stored")
        LINKS = 106
        v = count("s_dve_link", LINKS)
        a = count("s_act_small", 7)
        m_ = count("s_pe_small", 10)
        s_xn = count("s_x_normalised", 4)
        s_xhn = count("s_columns_normalised", 8)
        s_s1 = count("s_stage1", NK)
        s_ab = count("s_stage1_copied", NK)
        s_s2 = count("s_stage2", NK)
        s_xr = count("s_real_copied", NK)
        s_xi = count("s_imag_copied", NK)
        s_gram = count("s_gram", 1)
        s_t8 = count("s_hidden", 2)
        s_t8c = count("s_hidden_copied", 2)
        s_h1 = count("s_hidden_stage1", 2)
        s_h1c = count("s_hidden_stage1_copied", 2)
        s_h2 = count("s_hidden_stage2", NUG)
        s_rel = count("s_relu", NUG)
        s_gl = count("s_gate_logits", NUG)
        s_sig = count("s_sigmoid", 2 * 4 * NUG // 2)
        s_gx = count("s_gated", 2 * NUG)
        s_i1 = count("s_inverse1", 2 * NK)
        s_z = count("s_inverse1_copied", 2 * NK)
        s_i2 = count("s_inverse2", NK)
        s_abs = count("s_abs", NK)
        s_ca = count("s_conv3", NK)
        s_cb = count("s_conv5", NK)
        s_ae = count("s_conv3_copied", 2 * NK)
        s_be = count("s_conv5_copied", 2 * NK)
        s_ta = count("s_transposed3", NK)
        s_tb = count("s_transposed5", NK)
        s_tae = count("s_transposed3_copied", NK)
        s_tbe = count("s_transposed5_copied", NK)
        s_ga = count("s_gram3", NK)
        s_gb = count("s_gram5", NK)
        s_u = count("s_u_taps", 7)
        s_uc = count("s_u_copied", 7)
        s_m = count("s_m_taps", 7)
        s_mc = count("s_m_copied", 7)
        s_bv = count("s_v_bias", 1)
        s_bvc = count("s_v_bias_copied", 1)
        s_row = count("s_rows_taken", NK)
        s_tr = count("s_rows_turned", NK)
        s_trc = count("s_rows_turned_copied", NK)
        s_sh = count("s_rows_shifted", NK)
        s_shr = count("s_shifted_real_copied", NK)
        s_shi = count("s_shifted_imag_copied", NK)
        s_o = count("s_heads_mixed", NK)
        s_os = count("s_heads_squared", 2 * NK)
        s_oa = count("s_heads_added", NK)
        s_of = count("s_heads_root", NK)
        s_kl = [sem(f"s_shift_loaded_{i}") for i in range(2)]
        s_ofst = sem("s_heads_stored")
        sof = [sem(f"s_heads_chunk_{i}") for i in range(2)]
        s_vc = count("s_conv_out", NK)
        s_x1 = count("s_x1_ready", NK)
        s_bn = count("s_x1_stats", NK)
        s_edge = sem("s_edges_cleared")
        VL = {}
        block = ctx.enter_context(nc.Block())

        def credit(eng, *cs):
            for c in cs:
                eng.sem_inc(c.sem, c.per)

        rows4 = lambda h: bass.ds(h, 4)

        def window(kk, dh, dw):
            return xpad[:, bass.ds(kk * 4 + dh, 4), dw:dw + P]

        def chunk_loop(eng, body):
            body(0, 0, 0)
            with eng.Fori(0, NK // 2 - 1) as i:
                body(i * 2 + 1, 1, 2)
                body(i * 2 + 2, 0, 2)
            body(NK - 1, 1, 4)

        col = lambda i, n=1: small[:, i:i + n]
        xview = lambda b: x[bass.ds(b, 1), :, :, :]

        @block.vector
        def _(dve):
            credit(dve, v, s_shi, s_xhn, s_xi, s_h1c, s_gx, s_tae, s_tbe, s_bvc, s_oa, s_x1, s_bn)
            V = nc.vector
            n0 = [0]
            for part in (xpad[:, 0:2, :], xpad[:, WP - 2:WP, :], xpad[:, :, 0:2], xpad[:, :, WP - 2:WP]):
                V.memset(part, 0.0).then_inc(s_edge, 1)
                n0[0] += 1
                dve.wait_ge(s_edge, n0[0])
            with dve.Fori(0, B) as b:
                n, pn, an = [0], [0], [0]

                def link(op):
                    n[0] += 1
                    op.then_inc(v.sem, 1)
                    dve.wait_ge(v.sem, v.at(b, n[0]))

                def mark(name):
                    VL[name] = n[0]

                def pe_done():
                    pn[0] += 1
                    dve.wait_ge(m_.sem, m_.at(b, pn[0]))

                def act_done():
                    an[0] += 1
                    dve.wait_ge(a.sem, a.at(b, an[0]))

                def group_norm(name, st):
                    V.memset(col(20), 0.0)
                    link(V.bn_aggr(col(0, 2), st))
                    mark(name + "_mean")
                    pe_done()
                    link(V.tensor_tensor(col(2), col(0), bk[7][:, 0:1], ALU.subtract))
                    link(V.tensor_tensor(col(3), col(2), col(2), ALU.mult))
                    link(V.tensor_tensor(col(3), col(3), col(1), ALU.add))
                    link(V.tensor_copy(col(7), bk[7][:, 0:1]))
                    mark(name + "_var")
                    pe_done()
                    link(V.tensor_scalar(col(6), bk[7][:, 1:2], 1e-5, None, ALU.add))
                    mark(name + "_root")
                    act_done()
                    link(V.reciprocal(col(4), col(6)))
                    link(V.tensor_tensor(col(5), col(7), col(4), ALU.mult))
                    link(V.tensor_scalar(col(5), col(5), -1.0, None, ALU.mult))
                    mark(name + "_done")

                dve.wait_ge(s_gst, b * 16 + 16)
                for i in range(4):
                    dve.wait_ge(sxp[i], b * 16 + 16)
                    for r in range(8):
                        h = 2 + 32 * i + 4 * r
                        V.bn_stats(stats[:, 8 * i + r, :], xpad[:, h:h + 4, 2:2 + P]).then_inc(v.sem, 1)
                        n[0] += 1
                dve.wait_ge(v.sem, v.at(b, n[0]))
                group_norm("gn", stats[:, :, :])
                link(V.tensor_scalar(diag[:, 0:P], k["eye"], col(4), None, ALU.mult))
                link(V.tensor_scalar(diag[:, P:], k["eye"], col(5), None, ALU.mult))
                mark("gn_rows")
                pe_done()
                link(V.tensor_copy(rows, bk[7][:, 0:256]))

                def xi_copy(t):
                    dve.wait_ge(s_s2.sem, s_s2.at(b, t + 1))
                    V.tensor_copy(XI[:, 4 * t:4 * t + 4, :], bk[4 + t % 2][:, 0:4 * HALF].rearrange("p (c u) -> p c u", u=HALF)).then_inc(s_xi.sem, 1)

                def columns(i):
                    dve.wait_ge(sxh[i % 2], b * 128 + 32 * (i // 2) + 32)
                    t_ = xh[:, i % 2, :, :]
                    link(V.tensor_tensor(t_, t_, rows[:, 16 * i:16 * i + 16].unsqueeze(2).broadcast_to([P, 16, P]), ALU.mult))
                    V.tensor_tensor(t_, t_, rows[:, P + 16 * i:P + 16 * i + 16].unsqueeze(2).broadcast_to([P, 16, P]), ALU.add).then_inc(s_xhn.sem, 1)

                columns(0)
                columns(1)
                for i in range(8):
                    for t in range(4 * i, 4 * i + 4):
                        xi_copy(t)
                    if i + 2 < 8:
                        columns(i + 2)

                def softmax(name, width, mask):
                    L = sq[1][:, 0:width]
                    link(V.tensor_tensor(L, L, mask, ALU.mult))
                    link(V.tensor_scalar(sq[2][:, 0:width], mask, 1e30, -1e30, ALU.mult, ALU.add))
                    link(V.tensor_tensor(L, L, sq[2][:, 0:width], ALU.add))
                    link(V.reduce_max(col(15), L, AX.X))
                    link(V.tensor_scalar(col(15), col(15), -1.0, None, ALU.mult))
                    mark(name + "_max")
                    act_done()
                    link(V.reciprocal(col(17), col(16)))

                def roots(name, w_):
                    mark(name + "_root")
                    for _ in range(w_):
                        act_done()
                    link(V.tensor_scalar(col(10, w_), col(10, w_), 1e-12, None, ALU.max))
                    link(V.reciprocal(col(12, w_), col(10, w_)))

                for hf in range(2):
                    dve.wait_ge(s_h1.sem, s_h1.at(b, hf + 1))
                    src = bk[2 + hf][:, :].rearrange("p (j u) -> p u j", j=4)
                    link(V.tensor_copy(A8[:, :, 4 * hf:4 * hf + 4], src[:, 0:HALF, :]))
                    V.tensor_copy(B8[:, 1:64, 4 * hf:4 * hf + 4], src[:, HALF:, :]).then_inc(s_h1c.sem, 1)
                dve.wait_ge(s_gram.sem, s_gram.at(b, 1))
                G = bk[6]
                for i in range(2):
                    link(V.tensor_copy(sq[i], G[:, (2 * i + 1) * P:(2 * i + 2) * P]))
                for o, op in ((2, ALU.subtract), (3, ALU.add)):
                    link(V.tensor_tensor(sq[o], G[:, 0:P], sq[0], op))
                    link(V.tensor_tensor(sq[4], G[:, 2 * P:3 * P], sq[1], op))
                    link(V.scalar_tensor_tensor(sq[o], sq[o], 2.0, sq[4], ALU.mult, ALU.add))
                link(V.tensor_tensor(sq[3], sq[3], k["eye"], ALU.mult))
                link(V.reduce_sum(col(8), sq[3], AX.X))
                roots("f", 1)
                link(V.tensor_scalar(diag[:, 0:P], k["eye"], col(12), None, ALU.mult))
                mark("f_rows")
                pe_done()
                link(V.tensor_tensor(col(14), col(12), temps[:, 0:1], ALU.mult))
                link(V.scalar_tensor_tensor(sq[1], sq[2], col(14), bk[7][:, 0:P], ALU.mult, ALU.mult))
                softmax("f", P, k["head"])
                link(V.tensor_scalar(sq[0], sq[0], col(17), None, ALU.mult))
                mark("f_soft")
                pe_done()
                link(V.tensor_copy(mix_t[:, 0, :], bk[7][:, 0:P]))
                link(V.tensor_tensor(mix_t[:, 1, :], bk[7][:, P:2 * P], k["mixi"], ALU.add))
                link(V.tensor_scalar(mix_t[:, 2, :], mix_t[:, 1, :], -1.0, None, ALU.mult))
                mark("f_mix")
                for g in range(NUG):
                    dve.wait_ge(s_sig.sem, s_sig.at(b, 4 * g + 4))
                    for X in (XR, XI):
                        part = X[:, :, g * UG:(g + 1) * UG]
                        V.tensor_tensor(part, part, gates.rearrange("p u c -> p c u"), ALU.mult).then_inc(s_gx.sem, 1)

                def body(kk, par, vrow):
                    dve.wait_ge(s_sh.sem, s_sh.at(b, kk + 1))
                    dve.wait_ge(s_o.sem, s_o.at(b, kk))
                    V.tensor_copy(shifted[:, 512:], bk[2][:, :]).then_inc(s_shi.sem, 1)
                    dve.wait_ge(s_os.sem, s_os.at(b, 2 * kk + 2))
                    V.tensor_tensor(sq2[0], sq2[0], sq2[1], ALU.add).then_inc(s_oa.sem, 1)

                chunk_loop(dve, body)

                def body(kk, par, vrow):
                    first = isinstance(kk, int) and kk == 0
                    if not first:
                        tcopy(kk - 1, 1)
                    tcopy(kk, 0)

                def tcopy(kk, s):
                    ready, done, used = ((s_ta, s_tae, s_ga), (s_tb, s_tbe, s_gb))[s]
                    dve.wait_ge(ready.sem, ready.at(b, kk + 1))
                    dve.wait_ge(used.sem, used.at(b, kk))
                    V.tensor_copy(tt[s], bk[2 + s][:, :].rearrange("p (j o) -> p j o", o=P)).then_inc(done.sem, 1)

                chunk_loop(dve, body)
                tcopy(NK - 1, 1)
                dve.wait_ge(s_gb.sem, s_gb.at(b, NK))
                dve.wait_ge(s_ae.sem, s_ae.at(b, 2 * NK))
                dve.wait_ge(s_be.sem, s_be.at(b, 2 * NK))
                pe_done()
                link(V.reduce_sum(col(8, 2), norms[:, :, :], AX.X))
                roots("s", 2)
                for s in range(2):
                    link(V.tensor_scalar(sq[4][:, 64 * s:64 * s + 64], k["ones"][:, 0:64], col(12 + s), None, ALU.mult))
                mark("s_rows")
                pe_done()
                link(V.tensor_tensor(col(14), bk[5][:, 0:1], temps[:, 1:2], ALU.mult))
                link(V.tensor_scalar(sq[1][:, 0:64], bk[4][:, 0:64], col(14), None, ALU.mult))
                link(V.tensor_tensor(sq[1][:, 0:64], sq[1][:, 0:64], bk[5][:, 64:P], ALU.mult))
                softmax("s", 64, k["head64"])
                link(V.memset(afull, 0.0))
                for s in range(2):
                    r = slice(64 * s, 64 * s + 64)
                    link(V.tensor_scalar(afull[r, r], sq[0][r, 0:64], small[r, 17:18], None, ALU.mult))
                mark("s_soft")
                pe_done()
                link(V.tensor_copy(ap_, bk[5][:, 0:P]))
                mark("s_mix")
                dve.wait_ge(s_bv.sem, s_bv.at(b, 1))
                V.tensor_copy(bias_v[:, :], bk[6][0:T5, 0:P]).then_inc(s_bvc.sem, 1)

                def body(kk, par, vrow):
                    dve.wait_ge(s_vc.sem, s_vc.at(b, kk + 1))
                    dve.wait_ge(sxc[par], b * (8 * NK) + (kk - par) * 8 + 16)
                    dve.wait_ge(s_x1st[par], b * (8 * NK) + (kk - par) * 8 + 16)
                    dve.wait_ge(s_bn.sem, s_bn.at(b, kk - 1))
                    V.tensor_tensor(x1c[par], bk[6 + par][:, :], xch[par], ALU.add).then_inc(s_x1.sem, 1)
                    dve.wait_ge(s_x1.sem, s_x1.at(b, kk + 1))
                    V.bn_stats(stats[:, bass.ds(kk, 1), :], x1c[par]).then_inc(s_bn.sem, 1)

                chunk_loop(dve, body)
                dve.wait_ge(s_bn.sem, s_bn.at(b, NK))
                group_norm("gn2", stats[:, :, :])
                assert n[0] == LINKS, n

        @block.sync
        def _(sp):
            with sp.Fori(0, B) as b:
                sp.wait_ge(s_vc.sem, s_vc.at(b, 0))
                sp.wait_ge(s_bn.sem, s_bn.at(b, 0))
                for i in range(4):
                    sp.dma_start(xpad[:, 2 + 32 * i:34 + 32 * i, 2:2 + P], x[bass.ds(b, 1), :, 32 * i:32 * i + 32, :].rearrange("a c h w -> (a c) h w")).then_inc(sxp[i], 16)
                for s in range(2):
                    sp.wait_ge(s_x1st[s], b * (8 * NK) + 16)
                for i in range(8):
                    if i >= 2:
                        sp.wait_ge(s_s1.sem, s_s1.at(b, 4 * (i - 1)))
                    for hf in range(2):
                        c0 = 16 * i + 8 * hf
                        sp.dma_start(xh[:, i % 2, 8 * hf:8 * hf + 8, :], x[bass.ds(b, 1), c0:c0 + 8, :, :].rearrange("a c h w -> h (a c) w")).then_inc(sxh[i % 2], 16)
                for g in range(NK):
                    sp.wait_ge(s_abs.sem, s_abs.at(b, g + 1))
                    sp.dma_start(y_d[bass.ds(b, 1), 4 * g:4 * g + 4, :, :].rearrange("a c h w -> h (a c) w"), Yb[:, g % 2, :, :]).then_inc(s_yst[g % 2], 16)

                def body(kk, par, vrow):
                    sp.wait_ge(s_sh.sem, s_sh.at(b, kk - 1))
                    sp.dma_start(kbuf3[par], shift_d[:, rows4(kk * 4), :]).then_inc(s_kl[par], 16)

                chunk_loop(sp, body)
                sp.wait_ge(s_of.sem, s_of.at(b, NK))
                sp.dma_start(of_d[bass.ds(b, 1), :, :].rearrange("a c n -> (a c) n"), region[:, 0:HW]).then_inc(s_ofst, 16)
                sp.wait_ge(s_ofst, b * 16 + 16)
                inner = wts[:, 0:TAPS].rearrange("p (i j o) -> p i j o", i=5, j=5)
                for i in range(3):
                    sp.dma_start(WA[:, 3 * i:3 * i + 3, :], inner[:, 1 + i, 1:4, :]).then_inc(s_wl, 16)
                for n, dst in enumerate((WB, WV, WC)):
                    sp.dma_start(dst, wts[:, (n + 1) * TAPS:(n + 2) * TAPS]).then_inc(s_wl, 16)
                sp.wait_ge(s_yst[0], b * (8 * NK) + 8 * NK)
                sp.wait_ge(s_yst[1], b * (8 * NK) + 8 * NK)

                def body(kk, par, vrow):
                    first = isinstance(kk, int) and kk == 0
                    if not first:
                        store(kk - 1, 1 - par)
                    sp.wait_ge(s_vc.sem, s_vc.at(b, kk - 1))
                    sp.wait_ge(s_x1.sem, s_x1.at(b, kk - 1))
                    sp.dma_start(ych[par], y_d[bass.ds(b, 1), :, rows4(kk * 4), :].rearrange("a c h w -> (a c) (h w)")).then_inc(syc[par], 16)
                    sp.dma_start(of[par], of_d[bass.ds(b, 1), :, bass.ds(kk * 512, 512)].rearrange("a c n -> (a c) n")).then_inc(sof[par], 16)
                    sp.dma_start(xch[par], x[bass.ds(b, 1), :, rows4(kk * 4), :].rearrange("a c h w -> (a c) (h w)")).then_inc(sxc[par], 16)

                def store(kk, par):
                    sp.wait_ge(s_x1.sem, s_x1.at(b, kk + 1))
                    sp.dma_start(x1[bass.ds(b, 1), :, bass.ds(kk * 512, 512)].rearrange("a c n -> (a c) n"), x1c[par]).then_inc(s_x1st[par], 16)

                chunk_loop(sp, body)
                sp.wait_ge(v.sem, v.at(b, LINKS))
                store(NK - 1, 1)
                sp.dma_start(gn2[bass.ds(b, 1), :, :].rearrange("a c n -> (a c) n"), col(4, 2)).then_inc(s_gst, 16)
            sp.wait_ge(s_gst, 16 * B + 16)
            for s in range(2):
                sp.wait_ge(s_x1st[s], B * (8 * NK) + 16)

        @block.tensor
        def _(pe):
            credit(pe, s_tr, s_sh, m_, s_s1, s_s2, s_gram, s_t8, s_h1, s_h2, s_gl, s_i1, s_i2, s_ca, s_cb, s_ta, s_tb, s_ga, s_gb, s_u, s_m, s_bv, s_o, s_vc)
            mm = lambda *args, **kw: nc.tensor.matmul(*args, skip_group_check=True, **kw)

            with pe.Fori(0, B) as b:
                n = [0]

                def small_mm(wait, *ops):
                    pe.wait_ge(v.sem, v.at(b, wait))
                    for o, l, r in ops:
                        x_ = mm(o, l, r, start=True, stop=True)
                    n[0] += 1
                    x_.then_inc(m_.sem, 1)

                small_mm(VL["gn_mean"], (bk[7][:, 0:1], k["four"], col(0)))
                small_mm(VL["gn_var"], (bk[7][:, 1:2], k["four"], col(3)))
                small_mm(VL["gn_rows"], (bk[7][:, 0:256], k["ones"], diag))

                def stage1(t):
                    pe.wait_ge(s_xhn.sem, s_xhn.at(b, t // 4 + 1))
                    pe.wait_ge(s_ab.sem, s_ab.at(b, t - 1))
                    for c in range(4):
                        m = mm(bk[t % 2][:, c * P:(c + 1) * P], xh[:, t // 4 % 2, 4 * (t % 4) + c, :], k["fwd"], start=True, stop=True)
                    m.then_inc(s_s1.sem, 1)

                def stage2(t):
                    pe.wait_ge(s_ab.sem, s_ab.at(b, t + 1))
                    pe.wait_ge(s_xr.sem, s_xr.at(b, t - 1))
                    pe.wait_ge(s_xi.sem, s_xi.at(b, t - 1))
                    A, Bm = AB[:, t % 2, :, 0:HALF], AB[:, t % 2, :, HALF:]
                    for o, (ca, cb_) in ((bk[2 + t % 2], (k["cs"][:, 0:P], k["cs"][:, P:])), (bk[4 + t % 2], (k["sc"][:, 0:P], k["cs"][:, 0:P]))):
                        o3 = o[:, 0:4 * HALF].rearrange("p (c u) -> p c u", u=HALF)
                        mm(o3, ca, A, start=True, stop=False)
                        m = mm(o3[:, :, 1:64], cb_, Bm, start=False, stop=True)
                    m.then_inc(s_s2.sem, 1)

                stage1(0)
                for t in range(NK):
                    if t + 1 < NK:
                        stage1(t + 1)
                    stage2(t)
                pe.wait_ge(s_xr.sem, s_xr.at(b, NK))
                pe.wait_ge(s_xi.sem, s_xi.at(b, NK))
                for i, (X, us) in enumerate(((XR, range(1, 64)), (XI, range(1, 64)), (XR, (0, 64)), (XI, (0, 64)))):
                    for u in us:
                        m = mm(bk[6][:, i * P:(i + 1) * P], X[:, :, u], X[:, :, u], start=(u == us[0]), stop=(u == us[-1]))
                m.then_inc(s_gram.sem, 1)
                pe.wait_ge(s_xn.sem, s_xn.at(b, 4))
                for hf in range(2):
                    for c in range(64 * hf, 64 * hf + 64):
                        m = mm(bk[hf][:, (c % 64) * JG:(c % 64 + 1) * JG], xpad[:, 2:2 + P, 2 + c], w1t[:, :], start=True, stop=True)
                    m.then_inc(s_t8.sem, 1)
                for hf in range(2):
                    pe.wait_ge(s_t8c.sem, s_t8c.at(b, 2))
                    for j in range(4 * hf, 4 * hf + 4):
                        m = mm(bk[2 + hf][:, (j % 4) * P:(j % 4 + 1) * P], T8[:, :, j], k["fwd"], start=True, stop=True)
                    m.then_inc(s_h1.sem, 1)
                pe.wait_ge(s_h1c.sem, s_h1c.at(b, 2))
                for g in range(NUG):
                    u0 = g * UG
                    o = bk[g // 4][0:UG * JG, (g % 4) * P:(g % 4 + 1) * P]
                    mm(o, A8[:, u0:u0 + UG, :].rearrange("p u j -> p (u j)"), k["cs"][:, 0:P], start=True, stop=False)
                    mm(o, B8[:, u0:u0 + UG, :].rearrange("p u j -> p (u j)"), k["cs"][:, P:], start=False, stop=True).then_inc(s_h2.sem, 1)
                small_mm(VL["f_rows"], (bk[7][:, 0:P], k["ones"], diag[:, 0:P]))
                pe.wait_ge(v.sem, v.at(b, VL["f_soft"]))
                mm(bk[7][:, 0:P], sq[0], k["mixc"], start=True, stop=True)
                mm(bk[7][:, P:2 * P], sq[0], k["mixs"], start=True, stop=True).then_inc(m_.sem, 1)
                gate_flat = gate_w[:, :, :].rearrange("p u c -> p (u c)")
                for g in range(NUG):
                    pe.wait_ge(s_rel.sem, s_rel.at(b, g + 1))
                    pe.wait_ge(s_sig.sem, s_sig.at(b, 4 * g))
                    for i in range(4):
                        e = min(UG * P, (i + 1) * 512)
                        m = mm(bk[2 + i][:, 0:e - i * 512], relu_r[0:UG * JG + 1, g, :], gate_flat[:, i * 512:e], start=True, stop=True)
                    m.then_inc(s_gl.sem, 1)
                pe.wait_ge(s_gx.sem, s_gx.at(b, 2 * NUG))

                def inverse1(p):
                    pe.wait_ge(s_z.sem, s_z.at(b, p - 1))
                    if p < 2:
                        pe.wait_ge(s_rel.sem, s_rel.at(b, NUG))
                    for c in range(2):
                        o = bk[p % 2][0:HALF, c * 256:(c + 1) * 256]
                        mm(o, XR[:, 2 * p + c, :], k["cs"], start=True, stop=False)
                        m = mm(o, XI[:, 2 * p + c, :], k["sc"], start=False, stop=True)
                    m.then_inc(s_i1.sem, 1)

                def inverse2(t):
                    pe.wait_ge(s_z.sem, s_z.at(b, 2 * t + 2))
                    pe.wait_ge(s_abs.sem, s_abs.at(b, t - 1))
                    mm(bk[2 + t % 2][:, :], k["back"][:, 0:P], Z[0:HALF, t % 2, :, 0:P], start=True, stop=False)
                    mm(bk[2 + t % 2][:, :], k["back"][:, P:], Z[0:HALF, t % 2, :, P:], start=False, stop=True).then_inc(s_i2.sem, 1)

                inverse1(0)
                inverse1(1)
                for t in range(NK):
                    if t + 1 < NK:
                        inverse1(2 * t + 2)
                        inverse1(2 * t + 3)
                    inverse2(t)

                def turn(kk):
                    pe.wait_ge(s_row.sem, s_row.at(b, kk + 1))
                    pe.wait_ge(s_trc.sem, s_trc.at(b, kk))
                    for j in range(4):
                        m = nc.tensor.transpose(bk[0][:, j * P:(j + 1) * P], rowbuf[:, j * P:(j + 1) * P], k["eye"])
                    m.then_inc(s_tr.sem, 1)

                def body(kk, par, vrow):
                    last = isinstance(kk, int) and kk == NK - 1
                    pe.wait_ge(s_trc.sem, s_trc.at(b, kk + 1))
                    pe.wait_ge(s_kl[par], b * (8 * NK) + (kk - par) * 8 + 16)
                    pe.wait_ge(s_shr.sem, s_shr.at(b, kk))
                    pe.wait_ge(s_shi.sem, s_shi.at(b, kk))
                    for j in range(4):
                        for s in range(2):
                            m = mm(bk[1 + s][:, j * P:(j + 1) * P], turned[:, j * P:(j + 1) * P], kbuf3[par][:, j, s * P:(s + 1) * P], start=True, stop=True)
                    m.then_inc(s_sh.sem, 1)
                    if not last:
                        turn(kk + 1)
                    pe.wait_ge(s_shr.sem, s_shr.at(b, kk + 1))
                    pe.wait_ge(s_shi.sem, s_shi.at(b, kk + 1))
                    pe.wait_ge(s_os.sem, s_os.at(b, 2 * kk))
                    re, im = shifted[:, 0:512], shifted[:, 512:]
                    mm(bk[3][:, :], mix_t[:, 0, :], re, start=True, stop=False)
                    mm(bk[3][:, :], mix_t[:, 2, :], im, start=False, stop=True)
                    mm(bk[4][:, :], mix_t[:, 0, :], im, start=True, stop=False)
                    mm(bk[4][:, :], mix_t[:, 1, :], re, start=False, stop=True).then_inc(s_o.sem, 1)

                pe.wait_ge(s_abs.sem, s_abs.at(b, NK))
                turn(0)
                chunk_loop(pe, body)
                pe.wait_ge(s_os.sem, s_os.at(b, 2 * NK))
                pe.wait_ge(s_wl, b * 96 + 96)
                pe.wait_ge(s_i2.sem, s_i2.at(b, NK))
                pe.wait_ge(s_abs.sem, s_abs.at(b, NK))
                mm(bk[4][:, 0:64], relu_r[:, 0, :], B8[:, 0, :].unsqueeze(1).broadcast_to([P, 8, JG]), start=True, stop=True).then_inc(m_.sem, 1)
                WBt_ = WB.rearrange("p (t o) -> p t o", o=P)

                def gram(kk, s):
                    done, ready = ((s_ga, s_tae), (s_gb, s_tbe))[s]
                    pe.wait_ge(ready.sem, ready.at(b, kk + 1))
                    for j in range(4):
                        m = mm(bk[4][64 * s:64 * s + 64, 0:64], tt[s][:, j, 0:64], tt[s][:, j, 64:P], start=False, stop=True)
                    m.then_inc(done.sem, 1)

                def flip(kk, s):
                    done, copied, read = ((s_ta, s_ae, s_tae), (s_tb, s_be, s_tbe))[s]
                    pe.wait_ge(copied.sem, copied.at(b, 2 * kk + 1))
                    pe.wait_ge(read.sem, read.at(b, kk))
                    for j in range(4):
                        m = nc.tensor.transpose(bk[2 + s][:, j * P:(j + 1) * P], qa[s][:, j * P:(j + 1) * P], k["eye"])
                    m.then_inc(done.sem, 1)

                def body(kk, par, vrow):
                    first = isinstance(kk, int) and kk == 0
                    pe.wait_ge(s_ae.sem, s_ae.at(b, 2 * kk))
                    for n_, t in enumerate(INNER):
                        mm(bk[0][:, :], WA[:, n_, :], window(kk, *TAPAT[t]), start=(n_ == 0), stop=False)
                    mm(bk[0][:, :], bias_ab[:, 0, :], valid[:, vrow:vrow + 4, :], start=False, stop=True).then_inc(s_ca.sem, 1)
                    if not first:
                        flip(kk - 1, 1)
                        gram(kk - 1, 0)
                    pe.wait_ge(s_be.sem, s_be.at(b, 2 * kk))
                    for t in range(T5):
                        mm(bk[1][:, :], WBt_[:, t, :], window(kk, *TAPAT[t]), start=(t == 0), stop=False)
                    mm(bk[1][:, :], bias_ab[:, 1, :], valid[:, vrow:vrow + 4, :], start=False, stop=True).then_inc(s_cb.sem, 1)
                    if not first:
                        gram(kk - 1, 1)
                    flip(kk, 0)

                chunk_loop(pe, body)
                flip(NK - 1, 1)
                gram(NK - 1, 0)
                gram(NK - 1, 1)
                pe.wait_ge(v.sem, v.at(b, VL["s_rows"]))
                for s in range(2):
                    o = bk[5][64 * s:64 * s + 64, :]
                    mm(o[:, 0:1], k["eye"][:, 0:64], col(12 + s), start=True, stop=True)
                    m = mm(o[:, 64:P], sq[4][:, 64 * s:64 * s + 64], k["shift"], start=True, stop=True)
                m.then_inc(m_.sem, 1)
                small_mm(VL["s_soft"], (bk[5][:, 0:P], afull, pt[:, 2, :]))
                pe.wait_ge(v.sem, v.at(b, VL["s_mix"]))
                WVt_, WCt_ = (W.rearrange("p (t o) -> p t o", o=P) for W in (WV, WC))
                UT = UU.rearrange("p (t o) -> p t o", o=P)
                for i in range(7):
                    e = min(T5, 4 * i + 4)
                    pe.wait_ge(s_uc.sem, s_uc.at(b, i - 1))
                    for t in range(4 * i, e):
                        m = mm(bk[i % 2][:, (t % 4) * P:(t % 4 + 1) * P], WVt_[:, t, :], ap_, start=True, stop=True)
                    m.then_inc(s_u.sem, 1)
                for i in range(7):
                    e = min(T5, 4 * i + 4)
                    pe.wait_ge(s_uc.sem, s_uc.at(b, i + 1))
                    pe.wait_ge(s_mc.sem, s_mc.at(b, i - 1))
                    mm(bk[2 + i % 2][:, 0:(e - 4 * i) * P], v1[:, :], UU[:, 4 * i * P:e * P], start=True, stop=False)
                    for t in range(4 * i, e):
                        m = mm(bk[2 + i % 2][:, (t % 4) * P:(t % 4 + 1) * P], WCt_[:, t, :], pt[:, 3, :], start=False, stop=True)
                    m.then_inc(s_m.sem, 1)
                for t in range(T5):
                    m = mm(bk[6][0:T5, 0:P], vtap[:, t, :], UT[:, t, :], start=(t == 0), stop=(t == T5 - 1))
                m.then_inc(s_bv.sem, 1)
                pe.wait_ge(s_bvc.sem, s_bvc.at(b, 1))
                pe.wait_ge(s_mc.sem, s_mc.at(b, 7))
                MT = MM.rearrange("p (t o) -> p t o", o=P)

                def body(kk, par, vrow):
                    o = bk[6 + par][:, :]
                    pe.wait_ge(s_x1.sem, s_x1.at(b, kk - 1))
                    for t in range(T5):
                        mm(o, MT[:, t, :], window(kk, *TAPAT[t]), start=(t == 0), stop=False)
                    mm(o, bias_v[:, :], valid[:, vrow:vrow + 4, :], start=False, stop=False)
                    pe.wait_ge(syc[par], b * (8 * NK) + (kk - par) * 8 + 16)
                    mm(o, pt[:, 1, :], ych[par], start=False, stop=False)
                    pe.wait_ge(sof[par], b * (8 * NK) + (kk - par) * 8 + 16)
                    mm(o, pt[:, 0, :], of[par], start=False, stop=True).then_inc(s_vc.sem, 1)

                chunk_loop(pe, body)
                small_mm(VL["gn2_mean"], (bk[7][:, 0:1], k["four"], col(0)))
                small_mm(VL["gn2_var"], (bk[7][:, 1:2], k["four"], col(3)))
                assert n[0] + 3 == m_.per

        @block.scalar
        def _(act):
            credit(act, a, s_row, s_trc, s_shr, s_xn, s_ab, s_xr, s_t8c, s_rel, s_sig, s_z, s_abs, s_ae, s_be, s_uc, s_mc, s_os, s_of)
            cp = lambda o, i, f=ACT.Copy, **kw: nc.scalar.activation(o, i, f, **kw)
            with act.Fori(0, B) as b:
                n = [0]

                def small_act(wait, o, i, f, **kw):
                    act.wait_ge(v.sem, v.at(b, wait))
                    n[0] += 1
                    cp(o, i, f, **kw).then_inc(a.sem, 1)

                small_act(VL["gn_root"], col(6), col(6), ACT.Sqrt)
                act.wait_ge(v.sem, v.at(b, VL["gn_done"]))
                def normalise(i):
                    part = xpad[:, 2 + 32 * i:34 + 32 * i, 2:2 + P]
                    cp(part, part, ACT.Identity, bias=col(5), scale=col(4)).then_inc(s_xn.sem, 1)

                for t in range(NK):
                    act.wait_ge(s_s1.sem, s_s1.at(b, t + 1))
                    act.wait_ge(s_s2.sem, s_s2.at(b, t - 1))
                    cp(AB[:, t % 2, :, :].rearrange("p c u -> p (c u)"), bk[t % 2][:, :]).then_inc(s_ab.sem, 1)
                    if t > 0:
                        act.wait_ge(s_s2.sem, s_s2.at(b, t))
                        cp(XR[:, 4 * t - 4:4 * t, :], bk[2 + (t - 1) % 2][:, 0:4 * HALF].rearrange("p (c u) -> p c u", u=HALF)).then_inc(s_xr.sem, 1)
                    if t % 8 == 4:
                        normalise(t // 8)
                act.wait_ge(s_s2.sem, s_s2.at(b, NK))
                cp(XR[:, P - 4:P, :], bk[2 + (NK - 1) % 2][:, 0:4 * HALF].rearrange("p (c u) -> p c u", u=HALF)).then_inc(s_xr.sem, 1)
                for hf in range(2):
                    act.wait_ge(s_t8.sem, s_t8.at(b, hf + 1))
                    cp(T8[:, 64 * hf:64 * hf + 64, :], bk[hf][:, :].rearrange("p (w j) -> p w j", j=JG)).then_inc(s_t8c.sem, 1)
                for g in range(NUG):
                    act.wait_ge(s_h2.sem, s_h2.at(b, min(NUG, 4 * (g // 4) + 4)))
                    cp(relu_r[0:UG * JG, g, :], bk[g // 4][0:UG * JG, (g % 4) * P:(g % 4 + 1) * P], ACT.Relu, bias=gate_sb[:, 1:2], scale=gate_sb[:, 0:1]).then_inc(s_rel.sem, 1)
                small_act(VL["f_root"], col(10), col(8), ACT.Sqrt)
                small_act(VL["f_max"], sq[0], sq[1], ACT.Exp, bias=col(15), accum_out=col(16))
                for g in range(NUG):
                    act.wait_ge(s_gl.sem, s_gl.at(b, g + 1))
                    act.wait_ge(s_gx.sem, s_gx.at(b, 2 * g))
                    for i in range(4):
                        e = min(UG, 4 * i + 4)
                        cp(gates[:, 4 * i:e, :], bk[2 + i][:, 0:(e - 4 * i) * P].rearrange("p (u c) -> p u c", c=P), ACT.Sigmoid).then_inc(s_sig.sem, 1)

                def zcopy(p):
                    act.wait_ge(s_i1.sem, s_i1.at(b, p + 1))
                    act.wait_ge(s_i2.sem, s_i2.at(b, p // 2 - 1))
                    cp(Z[0:HALF, p // 2 % 2, 2 * (p % 2):2 * (p % 2) + 2, :], bk[p % 2][0:HALF, :].rearrange("p (c n) -> p c n", c=2)).then_inc(s_z.sem, 1)

                for t in range(NK + 1):
                    if t < NK:
                        zcopy(2 * t)
                        zcopy(2 * t + 1)
                    if t > 0:
                        g = t - 1
                        act.wait_ge(s_i2.sem, s_i2.at(b, g + 1))
                        if g >= 2:
                            act.wait_ge(s_yst[g % 2], b * (8 * NK) + 16 * (g // 2))
                        cp(Yb[:, g % 2, :, :], bk[2 + g % 2][:, :].rearrange("p (c w) -> p c w", c=4), ACT.Abs).then_inc(s_abs.sem, 1)

                def take_rows(kk):
                    act.wait_ge(s_tr.sem, s_tr.at(b, kk))
                    cp(rowbuf.rearrange("p (j w) -> p j w", j=4), window(kk, 2, 2)).then_inc(s_row.sem, 1)

                act.wait_ge(s_i2.sem, s_i2.at(b, NK))
                act.wait_ge(s_gx.sem, s_gx.at(b, 2 * NUG))
                act.wait_ge(s_xn.sem, s_xn.at(b, 4))
                take_rows(0)

                def body(kk, par, vrow):
                    act.wait_ge(s_tr.sem, s_tr.at(b, kk + 1))
                    act.wait_ge(s_sh.sem, s_sh.at(b, kk))
                    cp(turned, bk[0][:, :]).then_inc(s_trc.sem, 1)
                    if not (isinstance(kk, int) and kk == NK - 1):
                        take_rows(kk + 1)
                    act.wait_ge(s_sh.sem, s_sh.at(b, kk + 1))
                    act.wait_ge(s_o.sem, s_o.at(b, kk))
                    cp(shifted[:, 0:512], bk[1][:, :]).then_inc(s_shr.sem, 1)
                    act.wait_ge(s_o.sem, s_o.at(b, kk + 1))
                    act.wait_ge(s_of.sem, s_of.at(b, kk))
                    for s in range(2):
                        cp(sq2[s], bk[3 + s][:, :], ACT.Square).then_inc(s_os.sem, 1)
                    act.wait_ge(s_oa.sem, s_oa.at(b, kk + 1))
                    cp(OF[:, :, bass.ds(kk * 4, 4)], sq2[0].rearrange("p (j a) -> p a j", j=4), ACT.Sqrt).then_inc(s_of.sem, 1)

                chunk_loop(act, body)
                def body(kk, par, vrow):
                    for s, (ready, done, read) in enumerate(((s_ca, s_ae, s_ta), (s_cb, s_be, s_tb))):
                        act.wait_ge(ready.sem, ready.at(b, kk + 1))
                        act.wait_ge(read.sem, read.at(b, kk))
                        cp(qa[s], bk[s][:, :]).then_inc(done.sem, 1)
                        act.wait_ge(done.sem, done.at(b, 2 * kk))
                        cp(sqa[s], bk[s][:, :], ACT.Square, accum_out=norms[:, s, bass.ds(kk, 1)]).then_inc(done.sem, 1)

                act.wait_ge(s_yst[0], b * (8 * NK) + 8 * NK)
                act.wait_ge(s_yst[1], b * (8 * NK) + 8 * NK)
                chunk_loop(act, body)
                for s in range(2):
                    small_act(VL["s_root"], col(10 + s), col(8 + s), ACT.Sqrt)
                small_act(VL["s_max"], sq[0][:, 0:64], sq[1][:, 0:64], ACT.Exp, bias=col(15), accum_out=col(16))
                for i in range(7):
                    e = min(T5, 4 * i + 4)
                    act.wait_ge(s_u.sem, s_u.at(b, i + 1))
                    cp(UU[:, 4 * i * P:e * P], bk[i % 2][:, 0:(e - 4 * i) * P]).then_inc(s_uc.sem, 1)
                for i in range(7):
                    e = min(T5, 4 * i + 4)
                    act.wait_ge(s_m.sem, s_m.at(b, i + 1))
                    cp(MM[:, 4 * i * P:e * P], bk[2 + i % 2][:, 0:(e - 4 * i) * P]).then_inc(s_mc.sem, 1)

                small_act(VL["gn2_root"], col(6), col(6), ACT.Sqrt)
                assert n[0] == a.per

        @block.gpsimd
        def _(pool):
            for s in s_x1st:
                pool.sem_inc(s, 16)
            pool.sem_inc(s_gst, 16)


class Counter:

    def __init__(self, sem, per, ahead=1):
        self.sem, self.per, self.ahead = sem, per, ahead

    def at(self, chunk, n):
        return chunk * self.per + self.ahead * self.per + n


def layer1(nc, x1, gn2, W_in, conv_w, conv_b, W_xproj, W_dt, b_dt, A_log, D_param, W_out, out, B):
    CH = 512
    NCH = HW // CH
    N = 16
    R = 8
    G = 4
    NG = N // G
    RC = 512
    K4 = 4
    ctx = ExitStack()
    with ctx:
        sb = lambda name, shape, dt=F32: ctx.enter_context(nc.sbuf_tensor(name, shape, dt))
        pb = lambda name, shape: ctx.enter_context(nc.psum_tensor(name, shape, F32))
        sem = lambda name: ctx.enter_context(nc.semaphore(name))

        w_in = sb("w_in", [P, 4 * P])
        w_conv = sb("w_conv", [P, 2, K4])
        v_convb = sb("v_convb", [P, 2])
        w_bc = sb("w_bc", [P, 2, 3 * 2 * N])
        w_xdt = sb("w_xdt", [P, 2, R])
        w_dt = sb("w_dt", [R, 2 * P])
        v_bdt = sb("v_bdt", [P, 2])
        v_alog = sb("v_alog", [P, 2, N])
        v_aexp = sb("v_aexp", [P, 2, N])
        v_a = sb("v_a", [P, 2, N])
        v_d = sb("v_d", [P, 2])
        w_out = sb("w_out", [P, 2, P])
        ident = sb("ident", [P, P])
        pick = sb("pick", [96, 2 * N, P], BF16)
        gnb = sb("gnb", [P, 2])
        xin = sb("xin", [P, 2, CH])
        xn = sb("xn", [P, CH])
        xs = sb("xs", [P, 2, K4 - 1 + CH])
        conv = sb("conv", [P, 2, CH])
        silu_z = sb("silu_z", [P, 2, 2, CH])
        xc = sb("xc", [P, 2, 2, CH])
        delta = sb("delta", [P, 2, 2, CH])
        du = sb("du", [P, 2, 2, CH])
        parts = sb("parts", [96, 2, CH], BF16)
        rest = sb("rest", [96, CH])
        dt8 = sb("dt8", [R, CH])
        lin = conv
        soft = sb("soft", [P, 2, CH])
        mid = soft[0:96, 0, 0:CH // 2].bitcast(BF16)
        da = sb("da", [P, 4, NG, CH + 1])
        hid = sb("hid", [P, 4, NG, CH + 1])
        carry = sb("carry", [P, 2, N])
        cs = sb("cs", [P, 2, NG, CH])
        y = sb("y", [P, 2, CH])
        img = sb("img", [P, P, P])
        img_flat = img[:, :, :].rearrange("p i j -> p (i j)")
        rbuf = sb("rbuf", [P, 2, RC])

        bb = pb("bb", [P, 2, CH])
        cb = pb("cb", [P, CH])
        yp = pb("yp", [P, 2, CH])
        pj = [pb(f"pj{i}", [P, CH]) for i in range(3)]

        s_w = sem("s_weights_loaded")
        s_cst = sem("s_constants_built")
        s_ap = sem("s_a_ready")
        s_gn = sem("s_gn_loaded")
        s_reset = sem("s_state_reset")
        s_x = [sem(f"s_x_loaded_{q}") for q in range(2)]
        s_xn = Counter(sem("s_xn_ready"), 1, 2)
        s_inp = Counter(sem("s_inproj_done"), 4)
        s_xs = Counter(sem("s_xs_ready"), 2)
        s_conv = Counter(sem("s_conv_step"), 9)
        s_silu = Counter(sem("s_silu_done"), 4)
        s_xp = Counter(sem("s_xproj_done"), 2)
        s_hi = Counter(sem("s_hi_ready"), 2)
        s_rest = Counter(sem("s_rest_ready"), 1)
        s_mid = Counter(sem("s_mid_ready"), 2)
        s_low = Counter(sem("s_low_ready"), 1)
        s_dt = Counter(sem("s_dtproj_done"), 2)
        s_lin = Counter(sem("s_lin_ready"), 2)
        s_neg = Counter(sem("s_neg_ready"), 2)
        s_exp = Counter(sem("s_softexp_ready"), 2)
        s_ln = Counter(sem("s_softln_ready"), 2)
        s_delta = Counter(sem("s_delta_ready"), 2)
        s_du = Counter(sem("s_du_ready"), 2, 2)
        s_da = Counter(sem("s_da_ready"), 2 * G, 2)
        s_bb = Counter(sem("s_b_spread"), 2 * G, 2)
        s_cb = Counter(sem("s_c_spread"), N, 2)
        s_cs = Counter(sem("s_c_copied"), N)
        s_m1 = Counter(sem("s_input_ready"), 4 * G, 2)
        s_c0 = Counter(sem("s_carry_in"), 2 * G)
        s_scan = Counter(sem("s_scanned"), 2 * G)
        s_cout = Counter(sem("s_carry_out"), 2 * G)
        s_hc = Counter(sem("s_hc_ready"), 2 * G)
        s_ysum = Counter(sem("s_y_summed"), 2 * G)
        s_yd = Counter(sem("s_y_skip"), 2)
        s_yg = Counter(sem("s_y_gated"), 2, 2)
        s_op = Counter(sem("s_outproj_done"), 1)
        s_img = Counter(sem("s_image_written"), 1, 2)
        s_r = [sem(f"s_residual_loaded_{r}") for r in range(2)]
        s_add = sem("s_residual_added")
        s_st = sem("s_stored")
        block = ctx.enter_context(nc.Block())

        def chunks(eng, body, image_start, image_end):
            with eng.Fori(0, B) as b:
                image_start(b)
                body(None, b * NCH, 0, b, 0, b * (NCH // 2))
                with eng.Fori(0, NCH // 2 - 1) as i:
                    c = b * NCH + i * 2
                    body(c, c + 1, 1, b, i * 2 + 1, b * (NCH // 2) + i)
                    body(c + 1, c + 2, 0, b, i * 2 + 2, b * (NCH // 2) + i + 1)
                c = b * NCH + NCH - 2
                body(c, c + 1, 1, b, NCH - 1, b * (NCH // 2) + NCH // 2 - 1)
                body(c + 1, None, 0, b, NCH, None)
                image_end(b)

        def credit(eng, *counters):
            for s in counters:
                eng.sem_inc(s.sem, s.per * s.ahead)

        NR = HW // RC

        @block.sync
        def _(sp):
            for dst, src in (
                (w_in[:, :], W_in), (w_conv[:, :, :], conv_w.rearrange("(h p) k -> p h k", p=P)),
                (v_convb[:, :], conv_b.rearrange("(h p) -> p h", p=P)),
                (w_xdt[:, :, :], W_xproj[:, 0:R].rearrange("(h p) r -> p h r", p=P)),
                (w_dt[:, :], W_dt), (v_bdt[:, :], b_dt.rearrange("(h p) -> p h", p=P)),
                (v_alog[:, :, :], A_log.rearrange("(h p) n -> p h n", p=P)),
                (v_d[:, :], D_param.rearrange("(h p) -> p h", p=P)),
                (w_out[:, :, :], W_out.rearrange("(h p) o -> p h o", p=P)),
                *((w_bc[:, :, 2 * N * j:2 * N * (j + 1)], W_xproj[:, R:].rearrange("(h p) r -> p h r", p=P)) for j in range(3)),
            ):
                sp.dma_start(dst, src, allow_slow_non_contiguous=True).then_inc(s_w, 16)

            def start(b):
                sp.wait_ge(s_xn.sem, s_xn.at(b * NCH, 0))
                sp.dma_start(gnb[:, :], gn2[bass.ds(b, 1), :, :].rearrange("a p t -> p (a t)")).then_inc(s_gn, 16)

            def body(core, front, q, b, k, m):
                if front is None:
                    return
                sp.wait_ge(s_xn.sem, s_xn.at(front, -1))
                sp.dma_start(xin[:, q, :], x1[bass.ds(b, 1), :, bass.ds(k * CH, CH)].rearrange("a p n -> p (a n)")).then_inc(s_x[q], 16)

            def end(b):
                for r in range(NR + 1):
                    if r:
                        sp.wait_ge(s_add, b * NR + r + 2)
                        sp.dma_start(out[bass.ds(b, 1), :, (r - 1) * RC:r * RC].rearrange("a p n -> p (a n)"), img_flat[:, (r - 1) * RC:r * RC]).then_inc(s_st, 16)
                    if r == NR:
                        break
                    sp.dma_start(rbuf[:, r % 2, :], x1[bass.ds(b, 1), :, r * RC:(r + 1) * RC].rearrange("a p n -> p (a n)")).then_inc(s_r[r % 2], 16)

            sp.sem_inc(s_st, 16)
            chunks(sp, body, start, end)
            sp.wait_ge(s_st, 16 * (NR * B + 1))

        @block.tensor
        def _(pe):
            credit(pe, s_inp, s_xp, s_dt, s_bb, s_cb, s_ysum, s_op)
            pe.wait_ge(s_w, 16 * 12)
            pe.wait_ge(s_cst, 5)

            def front_a(f, q):
                pe.wait_ge(s_xn.sem, s_xn.at(f, 1))
                for i in range(4):
                    if i < 2:
                        pe.wait_ge(s_lin.sem, s_lin.at(f, i - 1))
                    if i == 2:
                        pe.wait_ge(s_img.sem, s_img.at(f, -1))
                    if i == 3:
                        pe.wait_ge(s_xs.sem, s_xs.at(f, 1))
                    nc.tensor.matmul(pj[i % 3][:, :], w_in[:, i * P:(i + 1) * P], xn[:, :], start=True, stop=True).then_inc(s_inp.sem, 1)

            def front_b(f, q):
                pe.wait_ge(s_xs.sem, s_xs.at(f, 2))
                pe.wait_ge(s_silu.sem, s_silu.at(f, 4))
                for h in range(2):
                    m = nc.tensor.matmul(pj[1][0:96, :], w_bc[:, h, :], xc[:, q, h, :], start=(h == 0), stop=(h == 1))
                m.then_inc(s_xp.sem, 1)
                for h in range(2):
                    m = nc.tensor.matmul(pj[2][0:R, :], w_xdt[:, h, :], xc[:, q, h, :], start=(h == 0), stop=(h == 1))
                m.then_inc(s_xp.sem, 1)

            def front_c(f, q):
                pe.wait_ge(s_hi.sem, s_hi.at(f, 2))
                pe.wait_ge(s_rest.sem, s_rest.at(f, 1))
                for h in range(2):
                    nc.tensor.matmul(pj[h][:, :], w_dt[:, h * P:(h + 1) * P], dt8[:, :], start=True, stop=True).then_inc(s_dt.sem, 1)

            def spread_b(c, q, u):
                pe.wait_ge(s_m1.sem, s_m1.at(c, 2 * u))
                for j in range(2):
                    m = nc.tensor.matmul(bb[:, j, :], pick[:, 2 * u + j, :], parts[:, q, :], start=True, stop=True)
                m.then_inc(s_bb.sem, 1)

            def spread_c(c, q, n):
                pe.wait_ge(s_cs.sem, s_cs.at(c, n))
                nc.tensor.matmul(cb[:, :], pick[:, N + n, :], parts[:, q, :], start=True, stop=True).then_inc(s_cb.sem, 1)

            def sum_y(c, g):
                for h in range(2):
                    if g == 0:
                        pe.wait_ge(s_yd.sem, s_yd.at(c, h - 1))
                    pe.wait_ge(s_hc.sem, s_hc.at(c, 2 * g + h + 1))
                    for n in range(NG):
                        m = nc.tensor.matmul(yp[:, h, :], ident[:, :], hid[:, (2 * g + h) % 4, n, 1:], start=(g == 0 and n == 0), stop=(g == G - 1 and n == NG - 1), skip_group_check=True)
                    m.then_inc(s_ysum.sem, 1)

            def body(c, f, qf, b, k, m):
                q = 1 - qf
                if c is not None:
                    pe.wait_ge(s_low.sem, s_low.at(c, 1))
                    pe.wait_ge(s_mid.sem, s_mid.at(c, 2))
                for g in range(G):
                    if c is not None:
                        spread_b(c, q, 2 * g)
                        for n in range(2):
                            spread_c(c, q, NG * g + n)
                        spread_b(c, q, 2 * g + 1)
                        for n in range(2, NG):
                            spread_c(c, q, NG * g + n)
                    if f is not None and g < 3:
                        (front_a, front_b, front_c)[g](f, qf)
                    if c is not None and g > 0:
                        sum_y(c, g - 1)
                if c is not None:
                    sum_y(c, G - 1)
                    if f is not None:
                        pe.wait_ge(s_hi.sem, s_hi.at(f, 2))
                    for h in range(2):
                        pe.wait_ge(s_yg.sem, s_yg.at(c, h + 1))
                        m = nc.tensor.matmul(pj[2][:, :], w_out[:, h, :], y[:, h, :], start=(h == 0), stop=(h == 1))
                    m.then_inc(s_op.sem, 1)

            chunks(pe, body, lambda b: None, lambda b: None)

        @block.scalar
        def _(act):
            credit(act, s_xn, s_xs, s_silu, s_hi, s_mid, s_lin, s_exp, s_ln, s_da, s_cs, s_img)
            act.wait_ge(s_w, 16 * 12)
            nc.scalar.activation(v_aexp[:, :, :], v_alog[:, :, :], ACT.Exp).then_inc(s_ap, 1)
            act.wait_ge(s_ap, 2)
            act.wait_ge(s_cst, 5)

            def exps(c, q, g):
                for h in range(2):
                    act.wait_ge(s_scan.sem, s_scan.at(c, 2 * g + h - 3))
                    if g == 0:
                        act.wait_ge(s_delta.sem, s_delta.at(c, h + 1))
                    for n in range(NG):
                        m = nc.scalar.activation(da[:, (2 * g + h) % 4, n, 1:], delta[:, q, h, :], ACT.Exp, scale=v_a[:, h, NG * g + n:NG * g + n + 1])
                        if n == NG - 1:
                            m.then_inc(s_da.sem, 1)
                        copy_c(c, g, h, n)

            def copy_c(c, g, h, n):
                if n % 2:
                    s = NG * g + 2 * h + n // 2
                    if s % NG == 0:
                        act.wait_ge(s_hc.sem, s_hc.at(c, 2 * (g - 1)))
                    act.wait_ge(s_cb.sem, s_cb.at(c, s + 1))
                    nc.scalar.activation(cs[:, g % 2, s % NG, :], cb[:, :], ACT.Copy).then_inc(s_cs.sem, 1)

            def front_a(f, q, m):
                act.wait_ge(s_x[q], m * 16 + 16)
                act.wait_ge(s_inp.sem, s_inp.at(f, 0))
                nc.scalar.activation(xn[:, :], xin[:, q, :], ACT.Identity, bias=gnb[:, 1:2], scale=gnb[:, 0:1]).then_inc(s_xn.sem, 1)
                for h in range(2):
                    act.wait_ge(s_inp.sem, s_inp.at(f, h + 1))
                    act.wait_ge(s_conv.sem, s_conv.at(f, 0))
                    nc.scalar.activation(xs[:, h, K4 - 1:], pj[h][:, :], ACT.Copy).then_inc(s_xs.sem, 1)

            def front_b(f, q, m):
                for h in range(2):
                    act.wait_ge(s_inp.sem, s_inp.at(f, h + 3))
                    act.wait_ge(s_yg.sem, s_yg.at(f, -2))
                    nc.scalar.activation(silu_z[:, q, h, :], pj[(2 + h) % 3][:, :], ACT.Silu).then_inc(s_silu.sem, 1)
                for h in range(2):
                    act.wait_ge(s_conv.sem, s_conv.at(f, 4 * h + 4))
                    nc.scalar.activation(xc[:, q, h, :], conv[:, h, :], ACT.Silu).then_inc(s_silu.sem, 1)
                act.wait_ge(s_xp.sem, s_xp.at(f, 1))
                act.wait_ge(s_cb.sem, s_cb.at(f, -N))
                act.wait_ge(s_bb.sem, s_bb.at(f, -2 * G))
                nc.scalar.activation(parts[:, q, :], pj[1][0:96, :], ACT.Copy).then_inc(s_hi.sem, 1)
                act.wait_ge(s_xp.sem, s_xp.at(f, 2))
                act.wait_ge(s_dt.sem, s_dt.at(f, 0))
                nc.scalar.activation(dt8[:, :], pj[2][0:R, :], ACT.Copy).then_inc(s_hi.sem, 1)
                act.wait_ge(s_rest.sem, s_rest.at(f, 1))
                act.wait_ge(s_hi.sem, s_hi.at(f, 1))
                nc.scalar.activation(parts[32:64, q, :], rest[32:64, :], ACT.Copy).then_inc(s_mid.sem, 1)
                act.wait_ge(s_delta.sem, s_delta.at(f, 0))
                nc.scalar.activation(mid[64:96, :], rest[64:96, :], ACT.Copy).then_inc(s_mid.sem, 1)

            def front_c(f, q, m):
                for h in range(2):
                    act.wait_ge(s_dt.sem, s_dt.at(f, h + 1))
                    act.wait_ge(s_delta.sem, s_delta.at(f, h - 1))
                    nc.scalar.activation(lin[:, h, :], pj[h][:, :], ACT.Identity, bias=v_bdt[:, h:h + 1]).then_inc(s_lin.sem, 1)
                for h in range(2):
                    act.wait_ge(s_neg.sem, s_neg.at(f, h + 1))
                    nc.scalar.activation(soft[:, h, :], soft[:, h, :], ACT.Exp).then_inc(s_exp.sem, 1)
                for h in range(2):
                    act.wait_ge(s_exp.sem, s_exp.at(f, h + 1))
                    nc.scalar.activation(soft[:, h, :], soft[:, h, :], ACT.Ln, bias=1.0).then_inc(s_ln.sem, 1)

            def body(c, f, qf, b, k, m):
                q = 1 - qf
                for g in range(G):
                    if c is not None:
                        exps(c, q, g)
                    if f is not None and g < 3:
                        (front_a, front_b, front_c)[g](f, qf, m)
                if c is not None:
                    act.wait_ge(s_op.sem, s_op.at(c, 1))
                    act.wait_ge(s_st, b * (NR * 16) + 16)
                    nc.scalar.activation(img[:, :, bass.ds((k - 1) * 4, 4)], pj[2][:, :].rearrange("p (j i) -> p i j", j=4), ACT.Copy).then_inc(s_img.sem, 1)

            def start(b):
                act.wait_ge(s_gn, b * 16 + 16)

            chunks(act, body, start, lambda b: None)

        @block.vector
        def _(dve):
            credit(dve, s_conv, s_rest, s_low, s_neg, s_delta, s_m1, s_c0, s_scan, s_cout, s_yd)
            dve.sem_inc(s_reset, 2)
            nc.vector.memset(ident[:, :], 0.0).then_inc(s_cst, 1)
            nc.vector.memset(da[:, :, :, 0:1], 0.0).then_inc(s_cst, 1)
            dve.wait_ge(s_ap, 1)
            nc.vector.tensor_scalar(v_a[:, :, :], v_aexp[:, :, :], -1.0, None, ALU.mult).then_inc(s_ap, 1)
            dve.wait_ge(s_w, 16 * 12)
            dve.wait_ge(s_cst, 5)

            def front_a(f, q):
                for h in range(2):
                    dve.wait_ge(s_xs.sem, s_xs.at(f, h + 1))
                    dve.wait_ge(s_silu.sem, s_silu.at(f, 0))
                    nc.vector.tensor_scalar(conv[:, h, :], xs[:, h, K4 - 1:], w_conv[:, h, K4 - 1:K4], v_convb[:, h:h + 1], ALU.mult, ALU.add).then_inc(s_conv.sem, 1)
                    for t in range(K4 - 2, -1, -1):
                        dve.wait_ge(s_conv.sem, s_conv.at(f, 4 * h + K4 - 1 - t))
                        nc.vector.scalar_tensor_tensor(conv[:, h, :], xs[:, h, t:t + CH], w_conv[:, h, t:t + 1], conv[:, h, :], ALU.mult, ALU.add).then_inc(s_conv.sem, 1)
                dve.wait_ge(s_conv.sem, s_conv.at(f, 8))
                nc.vector.tensor_copy(xs[:, :, 0:K4 - 1], xs[:, :, CH:CH + K4 - 1]).then_inc(s_conv.sem, 1)

            def front_b(f, q):
                dve.wait_ge(s_hi.sem, s_hi.at(f, 1))
                dve.wait_ge(s_mid.sem, s_mid.at(f, 0))
                dve.wait_ge(s_low.sem, s_low.at(f, 0))
                nc.vector.tensor_tensor(rest[:, :], pj[1][0:96, :], parts[:, q, :], ALU.subtract).then_inc(s_rest.sem, 1)

            def front_c(f, q):
                dve.wait_ge(s_mid.sem, s_mid.at(f, 2))
                nc.vector.tensor_tensor(parts[64:96, q, :], rest[64:96, :], mid[64:96, :], ALU.subtract).then_inc(s_low.sem, 1)
                for h in range(2):
                    dve.wait_ge(s_lin.sem, s_lin.at(f, h + 1))
                    dve.wait_ge(s_low.sem, s_low.at(f, 1))
                    nc.vector.scalar_tensor_tensor(soft[:, h, :], lin[:, h, :], -1.0, lin[:, h, :], ALU.mult, ALU.min).then_inc(s_neg.sem, 1)

            def front_d(f, q):
                for h in range(2):
                    dve.wait_ge(s_ln.sem, s_ln.at(f, h + 1))
                    dve.wait_ge(s_da.sem, s_da.at(f, -2 * G))
                    dve.wait_ge(s_du.sem, s_du.at(f, -2))
                    nc.vector.scalar_tensor_tensor(delta[:, q, h, :], lin[:, h, :], 0.0, soft[:, h, :], ALU.max, ALU.add).then_inc(s_delta.sem, 1)

            def inputs(c, q, g):
                for u in range(2 * g, 2 * g + 2):
                    dve.wait_ge(s_bb.sem, s_bb.at(c, u + 1))
                    for h in range(2):
                        slot = (2 * g + h) % 4
                        if u % 2 == 0:
                            dve.wait_ge(s_ysum.sem, s_ysum.at(c, 2 * g + h - 3))
                        if g == 0 and u == 0:
                            dve.wait_ge(s_du.sem, s_du.at(c, h + 1))
                        o = hid[:, slot, 2 * (u % 2):2 * (u % 2) + 2, 1:]
                        nc.vector.tensor_tensor(o, bb[:, :, :], du[:, q, h, :].unsqueeze(1).broadcast_to([P, 2, CH]), ALU.mult).then_inc(s_m1.sem, 1)

            def scans(c, q, g):
                for h in range(2):
                    slot = (2 * g + h) % 4
                    st = carry[:, h, NG * g:NG * (g + 1)].unsqueeze(2)
                    dve.wait_ge(s_cout.sem, s_cout.at(c, 2 * g + h - 2 * G + 1))
                    nc.vector.tensor_copy(hid[:, slot, :, 0:1], st).then_inc(s_c0.sem, 1)
                    dve.wait_ge(s_c0.sem, s_c0.at(c, 2 * g + h + 1))
                    dve.wait_ge(s_m1.sem, s_m1.at(c, 4 * g + 4))
                    dve.wait_ge(s_da.sem, s_da.at(c, 2 * g + h + 1))
                    flat = hid[:, slot, :, :].rearrange("p n t -> p (n t)")
                    nc.vector.tensor_tensor_scan(flat, da[:, slot, :, :].rearrange("p n t -> p (n t)"), flat, 0.0, ALU.mult, ALU.add).then_inc(s_scan.sem, 1)
                    dve.wait_ge(s_scan.sem, s_scan.at(c, 2 * g + h + 1))
                    nc.vector.tensor_copy(st, hid[:, slot, :, CH:CH + 1]).then_inc(s_cout.sem, 1)

            def body(c, f, qf, b, k, m):
                q = 1 - qf
                for g in range(G):
                    if c is not None:
                        inputs(c, q, g)
                        scans(c, q, g)
                    if f is not None:
                        (front_a, front_b, front_c, front_d)[g](f, qf)
                if c is not None:
                    for h in range(2):
                        dve.wait_ge(s_ysum.sem, s_ysum.at(c, 2 * G - 1 + h))
                        dve.wait_ge(s_op.sem, s_op.at(c, 0))
                        nc.vector.scalar_tensor_tensor(y[:, h, :], xc[:, q, h, :], v_d[:, h:h + 1], yp[:, h, :], ALU.mult, ALU.add).then_inc(s_yd.sem, 1)

            def start(b):
                dve.wait_ge(s_cout.sem, s_cout.at(b * NCH, 0))
                dve.wait_ge(s_conv.sem, s_conv.at(b * NCH, 0))
                nc.vector.memset(carry[:, :, :], 0.0).then_inc(s_reset, 1)
                nc.vector.memset(xs[:, :, 0:K4 - 1], 0.0).then_inc(s_reset, 1)
                dve.wait_ge(s_reset, b * 2 + 4)

            chunks(dve, body, start, lambda b: None)

        @block.gpsimd
        def _(pool):
            credit(pool, s_du, s_hc, s_yg)
            pool.sem_inc(s_add, 2)
            pool.wait_ge(s_cst, 2)
            nc.gpsimd.affine_select(out=ident[:, :], in_=ident[:, :], compare_op=ALU.not_equal, fill=1.0, base=0, pattern=[[-1, P]], channel_multiplier=1).then_inc(s_cst, 1)
            nc.gpsimd.memset(pick[:, :, :], 0.0).then_inc(s_cst, 1)
            pool.wait_ge(s_cst, 4)
            for j in range(3):
                part = pick[32 * j:32 * (j + 1), :, :]
                m = nc.gpsimd.affine_select(out=part, in_=part, compare_op=ALU.not_equal, fill=1.0, base=0, pattern=[[-1, 2 * N], [0, P]], channel_multiplier=1)
            m.then_inc(s_cst, 1)

            def body(c, f, qf, b, k, m):
                q = 1 - qf
                for g in range(G):
                    if c is not None:
                        pool.wait_ge(s_cs.sem, s_cs.at(c, NG * (g + 1)))
                        for h in range(2):
                            pool.wait_ge(s_cout.sem, s_cout.at(c, 2 * g + h + 1))
                            slot = (2 * g + h) % 4
                            nc.gpsimd.tensor_tensor(hid[:, slot, :, 1:], hid[:, slot, :, 1:], cs[:, g % 2, :, :], ALU.mult).then_inc(s_hc.sem, 1)
                if f is not None:
                    for h in range(2):
                        pool.wait_ge(s_delta.sem, s_delta.at(f, h + 1))
                        pool.wait_ge(s_silu.sem, s_silu.at(f, h + 3))
                        pool.wait_ge(s_m1.sem, s_m1.at(f, -4 * G))
                        nc.gpsimd.tensor_tensor(du[:, qf, h, :], delta[:, qf, h, :], xc[:, qf, h, :], ALU.mult).then_inc(s_du.sem, 1)
                if c is not None:
                    for h in range(2):
                        pool.wait_ge(s_yd.sem, s_yd.at(c, h + 1))
                        nc.gpsimd.tensor_tensor(y[:, h, :], y[:, h, :], silu_z[:, q, h, :], ALU.mult).then_inc(s_yg.sem, 1)

            def end(b):
                pool.wait_ge(s_img.sem, s_img.at(b * NCH + NCH - 1, 1))
                for r in range(NR):
                    part = img_flat[:, r * RC:(r + 1) * RC]
                    pool.wait_ge(s_r[r % 2], b * (8 * NR) + 16 * (r // 2 + 1))
                    nc.gpsimd.tensor_tensor(part, part, rbuf[:, r % 2, :], ALU.add).then_inc(s_add, 1)

            chunks(pool, body, lambda b: None, end)


_L0 = ['temp_f', 'w1', 'b1', 'bn_gamma', 'bn_beta', 'bn_mean', 'bn_var', 'w2', 'b2', 'projf_w', 'temp_s', 'q1_w', 'q1_b', 'k1_w', 'k1_b', 'v1_w', 'v1_b', 'q3_w', 'q5_w', 'k3_w', 'k5_w', 'v3_w', 'v5_w', 'c3_w', 'c5_w', 'projs_w']
_L1 = ["W_in", "conv_w", "conv_b", "W_xproj", "W_dt", "b_dt", "A_log", "D_param", "W_out"]


def build(nc, x, out, table, shift_d, l0, l1):
    B = x.shape[0]

    def scratch(name, shape):
        return nc.dram_tensor(name, shape, F32, kind="Internal").ap()

    x1, gn2 = scratch("x1", (B, P, HW)), scratch("gn2", (B, P, 2))
    layer0(nc, B, x, table, shift_d, l0, scratch("kernels", (P, 4 * TAPS)), scratch("gated", (B, P, P, P)),
           scratch("heads", (B, P, HW)), x1, gn2)
    layer1(nc, x1, gn2, *(l1[n] for n in _L1), out.rearrange("b c i j -> b c (i j)"), B)


def kernel(**inputs):
    import numpy as _np
    import concourse.bacc as _bacc
    from concourse import mybir as _mybir
    from concourse.bass_utils import run_bass_kernel_spmd as _run

    nc = _bacc.Bacc("TRN2", target_bir_lowering=False, num_devices=1, dynamic_dma_scratch_size=1024)
    arrays, aps = {}, {}

    def feed(name, a):
        a = _np.ascontiguousarray(a)
        arrays[f"in_{name}"] = a
        aps[name] = nc.dram_tensor(f"in_{name}", a.shape, _mybir.dt.from_np(a.dtype), kind="ExternalInput").ap()

    for name, a in inputs.items():
        feed(name, a)
    feed("table", constants()[0])
    feed("shift_d", shifts())
    x = inputs["x"]
    out = nc.dram_tensor("out", x.shape, _mybir.dt.float32, kind="ExternalOutput").ap()
    build(nc, aps["x"], out, aps["table"], aps["shift_d"], {n: aps["L0_conv_" + n] for n in _L0}, {n: aps["L1_conv_" + n] for n in _L1})
    r = _run(nc, [arrays], core_ids=[0])
    return r.results[0]["out"]
```

```python
from contextlib import ExitStack
import numpy as np
import concourse.bass as bass
from concourse import mybir

F32 = mybir.dt.float32
BF16 = mybir.dt.bfloat16
F16 = mybir.dt.float16
ALU = mybir.AluOpType
ACT = mybir.ActivationFunctionType
AX = mybir.AxisListType

P = 128
HW = 16384
HALF = 65
UG, JG = 13, 8
NUG = HALF // UG
T5 = 25
INNER = [5 * i + j for i in (1, 2, 3) for j in (1, 2, 3)]
WP = P + 4
TAPS = T5 * P
XSCALE, WMAX = 128.0, 16384.0


def constants():
    i = np.arange(P)
    cos, sin = (f(2 * np.pi * (np.outer(i, i) % P) / P) for f in (np.cos, np.sin))
    wt = np.where((i[:HALF] == 0) | (i[:HALF] == 64), 1.0, 2.0)[:, None] / HW
    o64 = np.arange(64)
    head = (i[:, None] // 16 == i // 16) * 1.0
    valid = np.zeros((T5, 8, P))
    for t in range(T5):
        dh, dw = t // 5 - 2, t % 5 - 2
        for n, h in enumerate((0, 1, 64, 64, 64, 64, 126, 127)):
            valid[t, n] = (0 <= h + dh < P) * ((0 <= i + dw) & (i + dw < P))
    spread = np.zeros((9, UG, UG * JG + 1))
    for u in range(UG):
        spread[8, u, UG * JG] = 1
        for j in range(JG):
            spread[j, u, u * JG + j] = 1
    parts = {
        "fwd": np.concatenate([cos[:, :HALF], sin[:, 1:64]], 1),
        "cs": np.concatenate([cos, -sin], 1), "sc": np.concatenate([sin, cos], 1),
        "back": np.concatenate([wt * cos[:HALF], wt * sin[:HALF]], 1),
        "eye": np.eye(P), "ones": np.ones((P, P)),
        "head": head, "head64": ((i[:, None] // 16) % 4 == o64 // 16),
        "four": (i[:, None] // 4 == i // 4) / 4,
        "mixc": head * np.cos(2 * np.pi * np.outer(i, i) / 16) / 16, "mixs": head * np.sin(2 * np.pi * np.outer(i, i) / 16) / 16,
        "mixi": head * (i % 16 == 0) / 16,
        "shift": (i[:, None] == 64 + o64), "valid": valid.reshape(T5, -1),
        "heads": (np.arange(8)[:, None] == i // 16), "rep8": (np.arange(8)[:, None] == np.arange(UG * JG) % JG),
        "mpair": (i[:, None] // 2 == o64), "mgroup": (i[:, None] % 64 == o64),
        "spread": spread.reshape(9, -1), "tap": np.broadcast_to(np.eye(T5).reshape(1, -1), (P, T5 * T5)),
    }
    at, cols = {}, 0
    for k, v in parts.items():
        at[k] = (cols, v.shape[0], v.shape[1])
        cols += v.shape[1]
    packed = np.zeros((P, cols), np.float32)
    for k, v in parts.items():
        packed[:v.shape[0], at[k][0]:at[k][0] + v.shape[1]] = v
    return packed, at


def shifts():
    i = np.arange(P)
    t = i[None, None, :] - i[:, None, None] + i[None, :, None] / P
    whole = t == np.round(t)
    safe = np.where(whole, 0.5, t)
    series = (np.exp(2j * np.pi * safe) - 1) / (np.exp(2j * np.pi * safe / P) - 1) / P
    d = np.where(whole, (t % P == 0) * (1.0 + 0j), series)
    return np.concatenate([d.real, d.imag], 2).astype(np.float32)


class Count:

    def __init__(self, sem, per):
        self.sem, self.per = sem, per

    def at(self, b, n):
        return b * self.per + self.per + n


def layer0(nc, B, x, table, shift_d, w, wts, y_d, of_d, x1, gn2):
    _, at = constants()
    ctx = ExitStack()
    with ctx:
        sb = lambda name, shape, dt=F32: ctx.enter_context(nc.sbuf_tensor(name, shape, dt))
        sem = lambda name: ctx.enter_context(nc.semaphore(name))
        counters = []

        def count(name, per):
            counters.append(Count(sem(name), per))
            return counters[-1]

        setup_from = at["mpair"][0]
        ncols = at["tap"][0] + at["tap"][2]
        ctab = sb("ctab", [P, setup_from])
        xpad = sb("xpad", [P, WP, WP])
        xpad_flat = xpad[:, :, :].rearrange("p h w -> p (h w)")
        region = sb("region", [P, 17408])
        work = sb("work", [P, 11264])
        k = {n: ctab[:r, c0:c0 + n_] for n, (c0, r, n_) in at.items() if c0 < setup_from}
        stab = xpad_flat[:, 0:ncols - setup_from]
        ks = {n: stab[:r, c0 - setup_from:c0 - setup_from + n_] for n, (c0, r, n_) in at.items() if c0 >= setup_from}
        valid = k["valid"].rearrange("t (r n) -> t r n", n=P)
        XR = region[:, 0:P * HALF].rearrange("p (c u) -> p c u", u=HALF)
        XI = region[:, P * HALF:2 * P * HALF].rearrange("p (c u) -> p c u", u=HALF)
        halves = lambda v, n: v.bitcast(F16).rearrange("p (s t o) -> p s t o", s=2, t=n)
        pixels16 = xpad[:, :, :].bitcast(F16).rearrange("p h (w s) -> p h s w", s=2)
        WA = halves(region[:, 0:9 * P], 9)
        cut = [9 * P + i * TAPS for i in range(6)]
        WB, WV, WC, UU, MM = (region[:, cut[i]:cut[i + 1]] for i in range(5))
        M16 = halves(UU, T5)

        pt = sb("pt", [P, 4, P])
        v1 = sb("v1", [P, P])
        floor = sb("floor", [P, 1])
        w1t = sb("w1t", [P, JG])
        gate_w = sb("gate_w", [UG * JG + 1, UG, P])
        gate_sb = sb("gate_sb", [UG * JG, 2])
        temps = sb("temps", [P, 2])
        vtap = sb("vtap", [P, T5, T5])
        bias_ab = sb("bias_ab", [T5, 2, P])
        bias_v = sb("bias_v", [T5, P])
        small = sb("small", [P, 64])
        stats = sb("stats", [P, 32, 6])
        mix_t = sb("mix_t", [P, 3, P])
        relu_r = sb("relu_r", [P, NUG, P])
        A8 = sb("A8", [P, HALF, JG])
        B8 = sb("B8", [P, HALF, JG])
        norms = sb("norms", [P, 2, 32])

        wk = lambda o, n: work[:, o:o + n]
        xh = wk(0, 4096).rearrange("p (s c w) -> p s c w", s=2, w=P)
        AB = wk(4096, 1024).rearrange("p (s c u) -> p s c u", s=2, u=P)
        T8 = wk(5120, 1024).rearrange("p (w j) -> p w j", j=JG)
        gates = wk(0, UG * P).rearrange("p (u c) -> p u c", c=P)
        Z = wk(2048, 2048).rearrange("p (s c n) -> p s c n", s=2, c=4)
        Yb = wk(4096, 1024).rearrange("p (s c w) -> p s c w", s=2, w=P)
        rows = wk(6144, 256)
        diag = wk(6400, 256)
        sq = [wk(6656 + P * i, P) for i in range(6)]
        rowbuf = wk(0, 512)
        turned = wk(512, 512)
        shifted = wk(1024, 1024)
        sq2 = [wk(2048 + 512 * i, 512) for i in range(2)]
        kbuf = [wk(7424 + 1024 * i, 1024) for i in range(2)]
        kbuf3 = [v_.rearrange("p (j n) -> p j n", j=4) for v_ in kbuf]
        high = [wk(3072 + 256 * i, 256).bitcast(F16) for i in range(2)]
        OF = region[:, 0:HW].rearrange("p (a h) -> p a h", h=P)
        qa = [wk(512 * i, 512) for i in range(2)]
        tt = [wk(1024 + 512 * i, 512).rearrange("p (j o) -> p j o", o=P) for i in range(2)]
        pt_scaled = wk(6144, 2 * P).rearrange("p (i o) -> p i o", i=2)
        of = [wk(2048 + 512 * i, 512) for i in range(2)]
        sqa = [wk(3072 + 512 * i, 512) for i in range(2)]
        ych = [wk(4096 + 512 * i, 512) for i in range(2)]
        xch = [wk(5120 + 512 * i, 512) for i in range(2)]
        x1c = [wk(7424 + 512 * i, 512) for i in range(2)]
        afull = wk(8448, P)
        ap_ = wk(8576, P)
        sparse = wk(0, T5 * 64).rearrange("p (t o) -> p t o", o=64)
        btap = wk(1600, T5 * T5).rearrange("p (t s) -> p t s", s=T5)
        wq = wk(2304, P)
        w5 = wk(2432, T5)
        w2 = wk(2464, 50).rearrange("p (i t) -> p i t", i=2)
        bcol = wk(2520, 1)
        wproj = wk(2528, 256)
        w1n = wk(2784, P)
        w2b = wk(2912, P)
        par8 = wk(3040, 8)
        tin = wk(3048, 2)

        bk = [ctx.enter_context(nc.psum_tensor(f"bk{i}", [P, 512], F32)) for i in range(8)]

        setup = ExitStack()
        s_ld = setup.enter_context(nc.semaphore("s_setup_load"))
        s_pe = setup.enter_context(nc.semaphore("s_setup_pe"))
        s_ve = setup.enter_context(nc.semaphore("s_setup_dve"))
        s_go = setup.enter_context(nc.semaphore("s_setup_next"))
        s_wr = setup.enter_context(nc.semaphore("s_setup_store"))
        s_link = setup.enter_context(nc.semaphore("s_setup_link"))
        s_sq = setup.enter_context(nc.semaphore("s_setup_sqrt"))
        qk = [("q", 0), ("k", 64)]

        def put(dst, src):
            return lambda sp: sp.dma_start(dst, src, allow_slow_non_contiguous=True).then_inc(s_ld, 16)

        conv_flat = lambda a: a.rearrange("o i a b -> (o i) (a b)")
        W5 = w5.rearrange("p (a b) -> p a b", b=5)
        table_loads = [put(ctab[:, :], table[:, 0:setup_from]), put(stab, table[:, setup_from:])]
        small_loads = [
            put(w1n[0:8, :], w["w1"].rearrange("o i a b -> o (i a b)")),
            put(w2b[0:8, :], w["w2"].rearrange("o i a b -> (i a b) o")), put(w2b[8:9, :], w["b2"].unsqueeze(0)),
            *(put(par8[0:8, n:n + 1], w[name].unsqueeze(1)) for n, name in enumerate(("b1", "bn_gamma", "bn_beta", "bn_mean", "bn_var"))),
            put(tin[0:8, 0:1], w["temp_f"].rearrange("h a b -> h (a b)")), put(tin[0:8, 1:2], w["temp_s"].rearrange("h a b -> h (a b)")),
            put(v1[:, :], w["v1_w"].rearrange("o i a b -> o (i a b)")),
        ]
        flats = [w["projf_w"].rearrange("o i a b -> o (i a b)"), w["projs_w"].rearrange("o i a b -> o (i a b)")]
        WBt = WB.rearrange("p (t o) -> p t o", o=P)
        WAfull = UU.rearrange("p (t o) -> p t o", o=P)
        WVt = WV.rearrange("p (t m) -> p t m", m=P)
        WCt = WC.rearrange("p (t m) -> p t m", m=P)

        block = setup.enter_context(nc.Block())
        loads_done, pe_done, ve_done, go = [0], [0], [0], [0]

        plan = []
        plan.append(("first", table_loads + small_loads))
        for n in range(2):
            plan.append((f"proj{n}", [put(wproj, flats[n])]))
        for nm, off in qk:
            for size in (3, 5):
                ld = [put(wq, w[nm + "1_w"].rearrange("o i a b -> o (i a b)")), put(bcol, w[nm + "1_b"].unsqueeze(1))]
                if size == 5:
                    ld.append(put(w5, conv_flat(w[nm + "5_w"])))
                else:
                    ld += [put(W5[:, 1 + a, 1:4], w[nm + "3_w"].rearrange("o i a b -> (o i) a b")[:, a, :]) for a in range(3)]
                plan.append((f"qk {off} {size}", ld))
        for n, nm in enumerate("vc"):
            ld = [put(w2[64:128, :, :], w[nm + "5_w"].rearrange("o i a b -> o i (a b)"))]
            ld += [put(w2[0:64, i, :].rearrange("p (a b) -> p a b", b=5)[:, 1 + a, 1:4], w[nm + "3_w"][:, i, a, :]) for i in range(2) for a in range(3)]
            if n == 0:
                ld.append(put(bcol, w["v1_b"].unsqueeze(1)))
            plan.append((f"vc {n}", ld))
        ld_at, total = [], 0
        for _, ld in plan:
            total += len(ld)
            ld_at.append(total * 16)
        NSTEP = len(plan)

        @block.sync
        def _(sp):
            for n, (_, loads) in enumerate(plan):
                sp.wait_ge(s_go, n + 1)
                for ld in loads:
                    ld(sp)
            sp.wait_ge(s_go, NSTEP + 2)
            for n, dst in enumerate((MM, UU, WV, WC)):
                sp.dma_start(wts[:, n * TAPS:(n + 1) * TAPS], dst).then_inc(s_wr, 16)
            sp.wait_ge(s_wr, 64)

        @block.tensor
        def _(pe):
            c = [0]

            def after(n):
                pe.wait_ge(s_ve, n)

            ve = iter(range(1, 1000))
            for n, (name, _) in enumerate(plan):
                pe.wait_ge(s_ld, ld_at[n])
                if name == "first":
                    after(next(ve))
                    nc.tensor.matmul(bk[0][0:UG * JG, 0:2], k["rep8"], par8[0:8, 6:8], start=True, stop=True)
                    nc.tensor.matmul(bk[1][:, 0:2], k["heads"], tin[0:8, :], start=True, stop=True)
                    nc.tensor.transpose(bk[2][:, 0:8], w1n[0:8, :], k["eye"][0:8, 0:8])
                    for u in range(UG):
                        m = nc.tensor.matmul(bk[3 + u // 4][0:UG * JG + 1, (u % 4) * P:(u % 4 + 1) * P], ks["spread"].rearrange("p (u m) -> p u m", u=UG)[:, u, :], w2b[0:9, :], start=True, stop=True)
                    m.then_inc(s_pe, 1)
                elif name.startswith("proj"):
                    for i in range(2):
                        m = nc.tensor.transpose(bk[i][:, 0:P], wproj[:, i * P:(i + 1) * P], k["eye"])
                    m.then_inc(s_pe, 1)
                elif name.startswith("qk"):
                    after(next(ve))
                    for t in range(0, T5, 8):
                        e = min(T5, t + 8)
                        nc.tensor.matmul(bk[t // 8][:, 0:(e - t) * 64], wq, sparse[:, t:e, :], start=True, stop=True)
                    for t in range(T5):
                        m = nc.tensor.matmul(bk[4][0:T5, 0:64], btap[:, t, :], sparse[:, t, :], start=(t == 0), stop=(t == T5 - 1))
                    m.then_inc(s_pe, 1)
                if name != "" and not name.startswith("vc"):
                    after(next(ve))
            after(next(ve))
            nc.tensor.matmul(bk[0][0:1, 0:P], small[:, 40:41], k["eye"], start=True, stop=True).then_inc(s_pe, 1)
            after(next(ve))
            nc.tensor.matmul(bk[1][:, 0:1], k["ones"][0:1, :], small[0:1, 42:43], start=True, stop=True).then_inc(s_pe, 1)

        @block.vector
        def _(dve):
            done = [0]

            def did(op):
                done[0] += 1
                op.then_inc(s_ve, 1)

            s_ch = [0]

            def link(op):
                s_ch[0] += 1
                op.then_inc(s_link, 1)
                dve.wait_ge(s_link, s_ch[0])

            link(nc.vector.memset(w5, 0.0))
            nc.vector.memset(w2, 0.0).then_inc(s_go, 1)
            npe = iter(range(1, 1000))
            for n, (name, _) in enumerate(plan):
                dve.wait_ge(s_ld, ld_at[n])
                if name == "first":
                    g = lambda i: par8[0:8, i:i + 1]
                    link(nc.vector.tensor_scalar(g(5), g(4), 1e-5, None, ALU.add))
                    dve.wait_ge(s_sq, 1)
                    link(nc.vector.reciprocal(g(5), g(5)))
                    link(nc.vector.tensor_tensor(g(6), g(1), g(5), ALU.mult))
                    link(nc.vector.tensor_tensor(g(7), g(0), g(3), ALU.subtract))
                    link(nc.vector.tensor_tensor(g(7), g(7), g(6), ALU.mult))
                    did(nc.vector.tensor_tensor(g(7), g(7), g(2), ALU.add))
                    dve.wait_ge(s_pe, next(npe))
                    nc.vector.tensor_copy(gate_sb[:, :], bk[0][0:UG * JG, 0:2])
                    nc.vector.tensor_copy(temps[:, :], bk[1][:, 0:2])
                    nc.vector.tensor_copy(w1t[:, :], bk[2][:, 0:8])
                    for i in range(4):
                        m = min(4, UG - 4 * i)
                        link(nc.vector.tensor_copy(gate_w[:, 4 * i:4 * i + m, :], bk[3 + i][0:UG * JG + 1, 0:m * P]))
                    link(nc.vector.memset(relu_r[:, :, :], 1.0))
                    did(nc.vector.memset(B8[:, :, :], 0.0))
                    nc.vector.memset(norms[:, 0, 0:1], 0.0).then_inc(s_go, 1)
                elif name.startswith("proj"):
                    dve.wait_ge(s_pe, next(npe))
                    s = int(name[4:])
                    link(nc.vector.tensor_copy(pt[:, 2 * s, :], bk[0][:, 0:P]))
                    did(nc.vector.tensor_copy(pt[:, 2 * s + 1, :], bk[1][:, 0:P]))
                    nc.vector.memset(norms[:, 0, 1:2], 0.0).then_inc(s_go, 1)
                elif name.startswith("qk"):
                    _, off, size = name.split()
                    off = int(off)
                    link(nc.vector.tensor_tensor(btap, ks["tap"].rearrange("p (t s) -> p t s", s=T5), bcol.unsqueeze(1).broadcast_to([P, T5, T5]), ALU.mult))
                    did(nc.vector.tensor_tensor(sparse, ks["mpair"].unsqueeze(1).broadcast_to([P, T5, 64]), w5.unsqueeze(2).broadcast_to([P, T5, 64]), ALU.mult))
                    dve.wait_ge(s_pe, next(npe))
                    dst = WBt if size == "5" else WAfull
                    for i in range(4):
                        m = min(8, T5 - 8 * i)
                        link(nc.vector.tensor_copy(dst[:, 8 * i:8 * i + m, off:off + 64], bk[i][:, 0:m * 64].rearrange("p (t o) -> p t o", o=64)))
                    did(nc.vector.tensor_copy(bias_ab[:, int(size == "5"), off:off + 64], bk[4][0:T5, 0:64]))
                    dve.wait_ge(s_ve, done[0])
                    nc.vector.memset(w5, 0.0).then_inc(s_go, 1)
                else:
                    s = int(name[3:])
                    for i in range(2):
                        dst = (WVt, WCt)[s].rearrange("p t (g i) -> p t g i", i=2)[:, :, :, i]
                        link(nc.vector.tensor_tensor(dst, ks["mgroup"].unsqueeze(1).broadcast_to([P, T5, 64]), w2[:, i, :].unsqueeze(2).broadcast_to([P, T5, 64]), ALU.mult))
                    if s == 0:
                        link(nc.vector.tensor_tensor(vtap[:, :, :], ks["tap"].rearrange("p (t s) -> p t s", s=T5), bcol.unsqueeze(1).broadcast_to([P, T5, T5]), ALU.mult))
                    nc.vector.memset(w2, 0.0).then_inc(s_go, 1)
            for i, W in enumerate((UU, WB)):
                link(nc.vector.reduce_max(small[:, 40 + i:41 + i], W, AX.X, apply_absolute_value=True))
            did(nc.vector.tensor_tensor(small[:, 40:41], small[:, 40:41], small[:, 41:42], ALU.max))
            dve.wait_ge(s_pe, next(npe))
            did(nc.vector.reduce_max(small[0:1, 42:43], bk[0][0:1, 0:P], AX.X))
            dve.wait_ge(s_pe, next(npe))
            link(nc.vector.tensor_scalar(small[:, 43:44], bk[1][:, 0:1], 1e-12, None, ALU.max))
            link(nc.vector.reciprocal(small[:, 44:45], small[:, 43:44]))
            link(nc.vector.tensor_scalar(small[:, 45:46], small[:, 44:45], WMAX, None, ALU.mult))
            link(nc.vector.tensor_scalar(small[:, 46:47], small[:, 45:46], XSCALE, None, ALU.mult))
            link(nc.vector.tensor_scalar(floor[:, :], small[:, 46:47], 1e-12, None, ALU.mult))
            for W, to in ((UU, MM), (WB, UU)):
                to = halves(to, T5)
                W = W.rearrange("p (t o) -> p t o", o=P)
                link(nc.vector.tensor_scalar(to[:, 0], W, small[:, 45:46], None, ALU.mult))
                link(nc.vector.scalar_tensor_tensor(to[:, 1], W, small[:, 45:46], to[:, 0], ALU.mult, ALU.subtract))
            link(nc.vector.tensor_scalar(bias_ab[:, :, :], bias_ab[:, :, :], small[0:T5, 46:47], None, ALU.mult))
            nc.vector.memset(norms[:, 0, 2:3], 0.0).then_inc(s_go, 1)

        @block.scalar
        def _(act):
            act.wait_ge(s_ld, ld_at[0])
            act.wait_ge(s_link, 2)
            nc.scalar.activation(par8[0:8, 5:6], par8[0:8, 5:6], ACT.Sqrt).then_inc(s_sq, 1)

        setup.close()
        TAPAT = [(t // 5, t % 5) for t in range(T5)]
        NK = 32
        sxp = [sem(f"s_x_rows_{i}") for i in range(4)]
        sxh = [sem(f"s_columns_{i}") for i in range(2)]
        syc = [sem(f"s_y_chunk_{i}") for i in range(2)]
        sxc = [sem(f"s_x_chunk_{i}") for i in range(2)]
        s_yst = [sem(f"s_y_stored_{i}") for i in range(2)]
        s_x1st = [sem(f"s_x1_stored_{i}") for i in range(2)]
        s_wl = sem("s_weights_loaded")
        s_gst = sem("s_gn_stored")
        LINKS = 115
        v = count("s_dve_link", LINKS)
        a = count("s_act_small", 7)
        m_ = count("s_pe_small", 12)
        s_xn = count("s_x_normalised", 4)
        s_xhn = count("s_columns_normalised", 8)
        s_s1 = count("s_stage1", NK)
        s_ab = count("s_stage1_copied", NK)
        s_s2 = count("s_stage2", NK)
        s_xr = count("s_real_copied", NK)
        s_xi = count("s_imag_copied", NK)
        s_gram = count("s_gram", 1)
        s_t8 = count("s_hidden", 2)
        s_t8c = count("s_hidden_copied", 2)
        s_h1 = count("s_hidden_stage1", 2)
        s_h1c = count("s_hidden_stage1_copied", 2)
        s_h2 = count("s_hidden_stage2", NUG)
        s_rel = count("s_relu", NUG)
        s_gl = count("s_gate_logits", NUG)
        s_sig = count("s_sigmoid", 2 * 4 * NUG // 2)
        s_gx = count("s_gated", 2 * NUG)
        s_i1 = count("s_inverse1", 2 * NK)
        s_z = count("s_inverse1_copied", 2 * NK)
        s_i2 = count("s_inverse2", NK)
        s_abs = count("s_abs", NK)
        s_ca = count("s_conv3", NK)
        s_cb = count("s_conv5", NK)
        s_ae = count("s_conv3_copied", 2 * NK)
        s_be = count("s_conv5_copied", 2 * NK)
        s_ta = count("s_transposed3", NK)
        s_tb = count("s_transposed5", NK)
        s_tae = count("s_transposed3_copied", NK)
        s_tbe = count("s_transposed5_copied", NK)
        s_ga = count("s_gram3", NK)
        s_gb = count("s_gram5", NK)
        s_u = count("s_u_taps", 7)
        s_uc = count("s_u_copied", 7)
        s_m = count("s_m_taps", 7)
        s_mc = count("s_m_copied", 7)
        s_bv = count("s_v_bias", 1)
        s_bvc = count("s_v_bias_copied", 1)
        s_row = count("s_rows_taken", NK)
        s_tr = count("s_rows_turned", NK)
        s_trc = count("s_rows_turned_copied", NK)
        s_sh = count("s_rows_shifted", NK)
        s_shr = count("s_shifted_real_copied", NK)
        s_shi = count("s_shifted_imag_copied", NK)
        s_o = count("s_heads_mixed", NK)
        s_os = count("s_heads_squared", 2 * NK)
        s_oa = count("s_heads_added", NK)
        s_of = count("s_heads_root", NK)
        s_hi = count("s_pixels_high", NK)
        s_lo = count("s_pixels_low", NK)
        s_px = count("s_pixels_split", NK)
        s_ms = count("s_m_split", 1)
        s_kl = [sem(f"s_shift_loaded_{i}") for i in range(2)]
        s_ofst = sem("s_heads_stored")
        sof = [sem(f"s_heads_chunk_{i}") for i in range(2)]
        s_vc = count("s_conv_out", NK)
        s_x1 = count("s_x1_ready", NK)
        s_bn = count("s_x1_stats", NK)
        s_edge = sem("s_edges_cleared")
        VL = {}
        block = ctx.enter_context(nc.Block())

        def credit(eng, *cs):
            for c in cs:
                eng.sem_inc(c.sem, c.per)

        rows4 = lambda h: bass.ds(h, 4)

        def window(kk, dh, dw):
            return xpad[:, bass.ds(kk * 4 + dh, 4), dw:dw + P]

        def window16(kk, half, dh, dw):
            return pixels16[:, bass.ds(kk * 4 + dh, 4), half, dw:dw + P]

        def chunk_loop(eng, body):
            body(0, 0, 0)
            with eng.Fori(0, NK // 2 - 1) as i:
                body(i * 2 + 1, 1, 2)
                body(i * 2 + 2, 0, 2)
            body(NK - 1, 1, 4)

        col = lambda i, n=1: small[:, i:i + n]
        xview = lambda b: x[bass.ds(b, 1), :, :, :]

        @block.vector
        def _(dve):
            credit(dve, v, s_shi, s_xhn, s_xi, s_h1c, s_gx, s_tae, s_tbe, s_lo, s_px, s_ms, s_bvc, s_oa, s_x1, s_bn)
            V = nc.vector
            n0 = [0]
            for part in (xpad[:, 0:2, :], xpad[:, WP - 2:WP, :], xpad[:, :, 0:2], xpad[:, :, WP - 2:WP]):
                V.memset(part, 0.0).then_inc(s_edge, 1)
                n0[0] += 1
                dve.wait_ge(s_edge, n0[0])
            with dve.Fori(0, B) as b:
                n, pn, an = [0], [0], [0]

                def link(op):
                    n[0] += 1
                    op.then_inc(v.sem, 1)
                    dve.wait_ge(v.sem, v.at(b, n[0]))

                def mark(name):
                    VL[name] = n[0]

                def pe_done():
                    pn[0] += 1
                    dve.wait_ge(m_.sem, m_.at(b, pn[0]))

                def act_done():
                    an[0] += 1
                    dve.wait_ge(a.sem, a.at(b, an[0]))

                def group_norm(name, st):
                    V.memset(col(20), 0.0)
                    link(V.bn_aggr(col(0, 2), st))
                    mark(name + "_mean")
                    pe_done()
                    link(V.tensor_tensor(col(2), col(0), bk[7][:, 0:1], ALU.subtract))
                    link(V.tensor_tensor(col(3), col(2), col(2), ALU.mult))
                    link(V.tensor_tensor(col(3), col(3), col(1), ALU.add))
                    link(V.tensor_copy(col(7), bk[7][:, 0:1]))
                    mark(name + "_var")
                    pe_done()
                    link(V.tensor_scalar(col(6), bk[7][:, 1:2], 1e-5, None, ALU.add))
                    mark(name + "_root")
                    act_done()
                    link(V.reciprocal(col(4), col(6)))
                    link(V.tensor_tensor(col(5), col(7), col(4), ALU.mult))
                    link(V.tensor_scalar(col(5), col(5), -1.0, None, ALU.mult))
                    mark(name + "_done")

                dve.wait_ge(s_gst, b * 16 + 16)
                for i in range(4):
                    dve.wait_ge(sxp[i], b * 16 + 16)
                    for r in range(8):
                        h = 2 + 32 * i + 4 * r
                        V.bn_stats(stats[:, 8 * i + r, :], xpad[:, h:h + 4, 2:2 + P]).then_inc(v.sem, 1)
                        n[0] += 1
                dve.wait_ge(v.sem, v.at(b, n[0]))
                group_norm("gn", stats[:, :, :])
                link(V.tensor_scalar(diag[:, 0:P], k["eye"], col(4), None, ALU.mult))
                link(V.tensor_scalar(diag[:, P:], k["eye"], col(5), None, ALU.mult))
                mark("gn_rows")
                pe_done()
                link(V.tensor_copy(rows, bk[7][:, 0:256]))

                def xi_copy(t):
                    dve.wait_ge(s_s2.sem, s_s2.at(b, t + 1))
                    V.tensor_copy(XI[:, 4 * t:4 * t + 4, :], bk[4 + t % 2][:, 0:4 * HALF].rearrange("p (c u) -> p c u", u=HALF)).then_inc(s_xi.sem, 1)

                def columns(i):
                    dve.wait_ge(sxh[i % 2], b * 128 + 32 * (i // 2) + 32)
                    t_ = xh[:, i % 2, :, :]
                    link(V.tensor_tensor(t_, t_, rows[:, 16 * i:16 * i + 16].unsqueeze(2).broadcast_to([P, 16, P]), ALU.mult))
                    V.tensor_tensor(t_, t_, rows[:, P + 16 * i:P + 16 * i + 16].unsqueeze(2).broadcast_to([P, 16, P]), ALU.add).then_inc(s_xhn.sem, 1)

                columns(0)
                columns(1)
                for i in range(8):
                    for t in range(4 * i, 4 * i + 4):
                        xi_copy(t)
                    if i + 2 < 8:
                        columns(i + 2)

                def softmax(name, width, mask):
                    L = sq[1][:, 0:width]
                    link(V.tensor_tensor(L, L, mask, ALU.mult))
                    link(V.tensor_scalar(sq[2][:, 0:width], mask, 1e30, -1e30, ALU.mult, ALU.add))
                    link(V.tensor_tensor(L, L, sq[2][:, 0:width], ALU.add))
                    link(V.reduce_max(col(15), L, AX.X))
                    link(V.tensor_scalar(col(15), col(15), -1.0, None, ALU.mult))
                    mark(name + "_max")
                    act_done()
                    link(V.reciprocal(col(17), col(16)))

                def roots(name, w_, least=1e-12):
                    mark(name + "_root")
                    for _ in range(w_):
                        act_done()
                    link(V.tensor_scalar(col(10, w_), col(10, w_), least, None, ALU.max))
                    link(V.reciprocal(col(12, w_), col(10, w_)))

                for hf in range(2):
                    dve.wait_ge(s_h1.sem, s_h1.at(b, hf + 1))
                    src = bk[2 + hf][:, :].rearrange("p (j u) -> p u j", j=4)
                    link(V.tensor_copy(A8[:, :, 4 * hf:4 * hf + 4], src[:, 0:HALF, :]))
                    V.tensor_copy(B8[:, 1:64, 4 * hf:4 * hf + 4], src[:, HALF:, :]).then_inc(s_h1c.sem, 1)
                dve.wait_ge(s_gram.sem, s_gram.at(b, 1))
                G = bk[6]
                for i in range(2):
                    link(V.tensor_copy(sq[i], G[:, (2 * i + 1) * P:(2 * i + 2) * P]))
                for o, op in ((2, ALU.subtract), (3, ALU.add)):
                    link(V.tensor_tensor(sq[o], G[:, 0:P], sq[0], op))
                    link(V.tensor_tensor(sq[4], G[:, 2 * P:3 * P], sq[1], op))
                    link(V.scalar_tensor_tensor(sq[o], sq[o], 2.0, sq[4], ALU.mult, ALU.add))
                link(V.tensor_tensor(sq[3], sq[3], k["eye"], ALU.mult))
                link(V.reduce_sum(col(8), sq[3], AX.X))
                roots("f", 1)
                link(V.tensor_scalar(diag[:, 0:P], k["eye"], col(12), None, ALU.mult))
                mark("f_rows")
                pe_done()
                link(V.tensor_tensor(col(14), col(12), temps[:, 0:1], ALU.mult))
                link(V.scalar_tensor_tensor(sq[1], sq[2], col(14), bk[7][:, 0:P], ALU.mult, ALU.mult))
                softmax("f", P, k["head"])
                link(V.tensor_scalar(sq[0], sq[0], col(17), None, ALU.mult))
                mark("f_soft")
                pe_done()
                link(V.tensor_copy(mix_t[:, 0, :], bk[7][:, 0:P]))
                link(V.tensor_tensor(mix_t[:, 1, :], bk[7][:, P:2 * P], k["mixi"], ALU.add))
                link(V.tensor_scalar(mix_t[:, 2, :], mix_t[:, 1, :], -1.0, None, ALU.mult))
                mark("f_mix")
                for g in range(NUG):
                    dve.wait_ge(s_sig.sem, s_sig.at(b, 4 * g + 4))
                    for X in (XR, XI):
                        part = X[:, :, g * UG:(g + 1) * UG]
                        V.tensor_tensor(part, part, gates.rearrange("p u c -> p c u"), ALU.mult).then_inc(s_gx.sem, 1)

                def body(kk, par, vrow):
                    dve.wait_ge(s_sh.sem, s_sh.at(b, kk + 1))
                    dve.wait_ge(s_o.sem, s_o.at(b, kk))
                    V.tensor_copy(shifted[:, 512:], bk[2][:, :]).then_inc(s_shi.sem, 1)
                    dve.wait_ge(s_os.sem, s_os.at(b, 2 * kk + 2))
                    V.tensor_tensor(sq2[0], sq2[0], sq2[1], ALU.add).then_inc(s_oa.sem, 1)
                    dve.wait_ge(s_t8.sem, s_t8.at(b, 2))
                    dve.wait_ge(s_row.sem, s_row.at(b, kk + 1))
                    dve.wait_ge(s_hi.sem, s_hi.at(b, kk + 1))
                    h4 = high[par].rearrange("p (r w) -> p r w", w=P)
                    V.scalar_tensor_tensor(window16(kk, 1, 2, 2), window(kk, 2, 2), XSCALE, h4, ALU.mult, ALU.subtract).then_inc(s_lo.sem, 1)
                    dve.wait_ge(s_lo.sem, s_lo.at(b, kk + 1))
                    V.tensor_copy(window16(kk, 0, 2, 2), h4).then_inc(s_px.sem, 1)

                chunk_loop(dve, body)

                def body(kk, par, vrow):
                    first = isinstance(kk, int) and kk == 0
                    if not first:
                        tcopy(kk - 1, 1)
                    tcopy(kk, 0)

                def tcopy(kk, s):
                    ready, done, used = ((s_ta, s_tae, s_ga), (s_tb, s_tbe, s_gb))[s]
                    dve.wait_ge(ready.sem, ready.at(b, kk + 1))
                    dve.wait_ge(used.sem, used.at(b, kk))
                    V.tensor_copy(tt[s], bk[2 + s][:, :].rearrange("p (j o) -> p j o", o=P)).then_inc(done.sem, 1)

                chunk_loop(dve, body)
                tcopy(NK - 1, 1)
                dve.wait_ge(s_gb.sem, s_gb.at(b, NK))
                dve.wait_ge(s_ae.sem, s_ae.at(b, 2 * NK))
                dve.wait_ge(s_be.sem, s_be.at(b, 2 * NK))
                pe_done()
                link(V.reduce_sum(col(8, 2), norms[:, :, :], AX.X))
                roots("s", 2, floor[:, 0:1])
                for s in range(2):
                    link(V.tensor_scalar(sq[4][:, 64 * s:64 * s + 64], k["ones"][:, 0:64], col(12 + s), None, ALU.mult))
                mark("s_rows")
                pe_done()
                link(V.tensor_tensor(col(14), bk[5][:, 0:1], temps[:, 1:2], ALU.mult))
                link(V.tensor_scalar(sq[1][:, 0:64], bk[4][:, 0:64], col(14), None, ALU.mult))
                link(V.tensor_tensor(sq[1][:, 0:64], sq[1][:, 0:64], bk[5][:, 64:P], ALU.mult))
                softmax("s", 64, k["head64"])
                link(V.memset(afull, 0.0))
                for s in range(2):
                    r = slice(64 * s, 64 * s + 64)
                    link(V.tensor_scalar(afull[r, r], sq[0][r, 0:64], small[r, 17:18], None, ALU.mult))
                mark("s_soft")
                pe_done()
                link(V.tensor_copy(ap_, bk[5][:, 0:P]))
                mark("s_mix")
                dve.wait_ge(s_mc.sem, s_mc.at(b, 7))
                link(V.reduce_max(col(21), MM, AX.X, apply_absolute_value=True))
                mark("m_rows")
                pe_done()
                link(V.reduce_max(small[0:1, 22:23], bk[5][0:1, 0:P], AX.X))
                mark("m_max")
                pe_done()
                link(V.tensor_scalar(col(22), bk[5][:, P:P + 1], 1e-12, None, ALU.max))
                link(V.reciprocal(col(23), col(22)))
                link(V.tensor_scalar(col(24), col(23), WMAX, None, ALU.mult))
                link(V.tensor_scalar(col(25), col(24), XSCALE, None, ALU.mult))
                link(V.reciprocal(col(26), col(25)))
                dve.wait_ge(s_m.sem, s_m.at(b, 7))
                dve.wait_ge(s_bv.sem, s_bv.at(b, 1))
                MT_ = MM.rearrange("p (t o) -> p t o", o=P)
                link(V.tensor_scalar(M16[:, 0], MT_, col(24), None, ALU.mult))
                V.scalar_tensor_tensor(M16[:, 1], MT_, col(24), M16[:, 0], ALU.mult, ALU.subtract).then_inc(s_ms.sem, 1)
                link(V.tensor_scalar(pt_scaled, pt[:, 0:2, :], col(25), None, ALU.mult))
                V.tensor_scalar(bias_v[:, :], bk[6][0:T5, 0:P], small[0:T5, 25:26], None, ALU.mult).then_inc(s_bvc.sem, 1)

                def body(kk, par, vrow):
                    dve.wait_ge(s_vc.sem, s_vc.at(b, kk + 1))
                    dve.wait_ge(sxc[par], b * (8 * NK) + (kk - par) * 8 + 16)
                    dve.wait_ge(s_x1st[par], b * (8 * NK) + (kk - par) * 8 + 16)
                    dve.wait_ge(s_bn.sem, s_bn.at(b, kk - 1))
                    V.scalar_tensor_tensor(x1c[par], bk[6 + par][:, :], col(26), xch[par], ALU.mult, ALU.add).then_inc(s_x1.sem, 1)
                    dve.wait_ge(s_x1.sem, s_x1.at(b, kk + 1))
                    V.bn_stats(stats[:, bass.ds(kk, 1), :], x1c[par]).then_inc(s_bn.sem, 1)

                chunk_loop(dve, body)
                dve.wait_ge(s_bn.sem, s_bn.at(b, NK))
                group_norm("gn2", stats[:, :, :])
                assert n[0] == LINKS, n

        @block.sync
        def _(sp):
            with sp.Fori(0, B) as b:
                sp.wait_ge(s_vc.sem, s_vc.at(b, 0))
                sp.wait_ge(s_bn.sem, s_bn.at(b, 0))
                for i in range(4):
                    sp.dma_start(xpad[:, 2 + 32 * i:34 + 32 * i, 2:2 + P], x[bass.ds(b, 1), :, 32 * i:32 * i + 32, :].rearrange("a c h w -> (a c) h w")).then_inc(sxp[i], 16)
                for s in range(2):
                    sp.wait_ge(s_x1st[s], b * (8 * NK) + 16)
                for i in range(8):
                    if i >= 2:
                        sp.wait_ge(s_s1.sem, s_s1.at(b, 4 * (i - 1)))
                    for hf in range(2):
                        c0 = 16 * i + 8 * hf
                        sp.dma_start(xh[:, i % 2, 8 * hf:8 * hf + 8, :], x[bass.ds(b, 1), c0:c0 + 8, :, :].rearrange("a c h w -> h (a c) w")).then_inc(sxh[i % 2], 16)
                for g in range(NK):
                    sp.wait_ge(s_abs.sem, s_abs.at(b, g + 1))
                    sp.dma_start(y_d[bass.ds(b, 1), 4 * g:4 * g + 4, :, :].rearrange("a c h w -> h (a c) w"), Yb[:, g % 2, :, :]).then_inc(s_yst[g % 2], 16)

                def body(kk, par, vrow):
                    sp.wait_ge(s_sh.sem, s_sh.at(b, kk - 1))
                    sp.dma_start(kbuf3[par], shift_d[:, rows4(kk * 4), :]).then_inc(s_kl[par], 16)

                chunk_loop(sp, body)
                sp.wait_ge(s_of.sem, s_of.at(b, NK))
                sp.dma_start(of_d[bass.ds(b, 1), :, :].rearrange("a c n -> (a c) n"), region[:, 0:HW]).then_inc(s_ofst, 16)
                sp.wait_ge(s_ofst, b * 16 + 16)
                inner = wts[:, 0:TAPS].rearrange("p (s i j o) -> p s i j o", s=2, i=5, j=5)
                inner_to = region[:, 0:9 * P].rearrange("p (s t o) -> p s t o", s=2, t=9)
                for half in range(2):
                    for i in range(3):
                        sp.dma_start(inner_to[:, half, 3 * i:3 * i + 3, :], inner[:, half, 1 + i, 1:4, :]).then_inc(s_wl, 16)
                for n, dst in enumerate((WB, WV, WC)):
                    sp.dma_start(dst, wts[:, (n + 1) * TAPS:(n + 2) * TAPS]).then_inc(s_wl, 16)
                sp.wait_ge(s_yst[0], b * (8 * NK) + 8 * NK)
                sp.wait_ge(s_yst[1], b * (8 * NK) + 8 * NK)

                def body(kk, par, vrow):
                    first = isinstance(kk, int) and kk == 0
                    if not first:
                        store(kk - 1, 1 - par)
                    sp.wait_ge(s_vc.sem, s_vc.at(b, kk - 1))
                    sp.wait_ge(s_x1.sem, s_x1.at(b, kk - 1))
                    sp.dma_start(ych[par], y_d[bass.ds(b, 1), :, rows4(kk * 4), :].rearrange("a c h w -> (a c) (h w)")).then_inc(syc[par], 16)
                    sp.dma_start(of[par], of_d[bass.ds(b, 1), :, bass.ds(kk * 512, 512)].rearrange("a c n -> (a c) n")).then_inc(sof[par], 16)
                    sp.dma_start(xch[par], x[bass.ds(b, 1), :, rows4(kk * 4), :].rearrange("a c h w -> (a c) (h w)")).then_inc(sxc[par], 16)

                def store(kk, par):
                    sp.wait_ge(s_x1.sem, s_x1.at(b, kk + 1))
                    sp.dma_start(x1[bass.ds(b, 1), :, bass.ds(kk * 512, 512)].rearrange("a c n -> (a c) n"), x1c[par]).then_inc(s_x1st[par], 16)

                chunk_loop(sp, body)
                sp.wait_ge(v.sem, v.at(b, LINKS))
                store(NK - 1, 1)
                sp.dma_start(gn2[bass.ds(b, 1), :, :].rearrange("a c n -> (a c) n"), col(4, 2)).then_inc(s_gst, 16)
            sp.wait_ge(s_gst, 16 * B + 16)
            for s in range(2):
                sp.wait_ge(s_x1st[s], B * (8 * NK) + 16)

        @block.tensor
        def _(pe):
            credit(pe, s_tr, s_sh, m_, s_s1, s_s2, s_gram, s_t8, s_h1, s_h2, s_gl, s_i1, s_i2, s_ca, s_cb, s_ta, s_tb, s_ga, s_gb, s_u, s_m, s_bv, s_o, s_vc)
            mm = lambda *args, **kw: nc.tensor.matmul(*args, skip_group_check=True, **kw)

            def conv(o, kernel, taps, kk):
                for n_, t in enumerate(taps):
                    for wh, ph in ((0, 0), (0, 1), (1, 0)):
                        mm(o, kernel[:, wh, n_, :], window16(kk, ph, *TAPAT[t]), start=(n_ == 0 and wh == 0 and ph == 0), stop=False)

            with pe.Fori(0, B) as b:
                n = [0]

                def small_mm(wait, *ops):
                    pe.wait_ge(v.sem, v.at(b, wait))
                    for o, l, r in ops:
                        x_ = mm(o, l, r, start=True, stop=True)
                    n[0] += 1
                    x_.then_inc(m_.sem, 1)

                small_mm(VL["gn_mean"], (bk[7][:, 0:1], k["four"], col(0)))
                small_mm(VL["gn_var"], (bk[7][:, 1:2], k["four"], col(3)))
                small_mm(VL["gn_rows"], (bk[7][:, 0:256], k["ones"], diag))

                def stage1(t):
                    pe.wait_ge(s_xhn.sem, s_xhn.at(b, t // 4 + 1))
                    pe.wait_ge(s_ab.sem, s_ab.at(b, t - 1))
                    for c in range(4):
                        m = mm(bk[t % 2][:, c * P:(c + 1) * P], xh[:, t // 4 % 2, 4 * (t % 4) + c, :], k["fwd"], start=True, stop=True)
                    m.then_inc(s_s1.sem, 1)

                def stage2(t):
                    pe.wait_ge(s_ab.sem, s_ab.at(b, t + 1))
                    pe.wait_ge(s_xr.sem, s_xr.at(b, t - 1))
                    pe.wait_ge(s_xi.sem, s_xi.at(b, t - 1))
                    A, Bm = AB[:, t % 2, :, 0:HALF], AB[:, t % 2, :, HALF:]
                    for o, (ca, cb_) in ((bk[2 + t % 2], (k["cs"][:, 0:P], k["cs"][:, P:])), (bk[4 + t % 2], (k["sc"][:, 0:P], k["cs"][:, 0:P]))):
                        o3 = o[:, 0:4 * HALF].rearrange("p (c u) -> p c u", u=HALF)
                        mm(o3, ca, A, start=True, stop=False)
                        m = mm(o3[:, :, 1:64], cb_, Bm, start=False, stop=True)
                    m.then_inc(s_s2.sem, 1)

                stage1(0)
                for t in range(NK):
                    if t + 1 < NK:
                        stage1(t + 1)
                    stage2(t)
                pe.wait_ge(s_xr.sem, s_xr.at(b, NK))
                pe.wait_ge(s_xi.sem, s_xi.at(b, NK))
                for i, (X, us) in enumerate(((XR, range(1, 64)), (XI, range(1, 64)), (XR, (0, 64)), (XI, (0, 64)))):
                    for u in us:
                        m = mm(bk[6][:, i * P:(i + 1) * P], X[:, :, u], X[:, :, u], start=(u == us[0]), stop=(u == us[-1]))
                m.then_inc(s_gram.sem, 1)
                pe.wait_ge(s_xn.sem, s_xn.at(b, 4))
                for hf in range(2):
                    for c in range(64 * hf, 64 * hf + 64):
                        m = mm(bk[hf][:, (c % 64) * JG:(c % 64 + 1) * JG], xpad[:, 2:2 + P, 2 + c], w1t[:, :], start=True, stop=True)
                    m.then_inc(s_t8.sem, 1)
                for hf in range(2):
                    pe.wait_ge(s_t8c.sem, s_t8c.at(b, 2))
                    for j in range(4 * hf, 4 * hf + 4):
                        m = mm(bk[2 + hf][:, (j % 4) * P:(j % 4 + 1) * P], T8[:, :, j], k["fwd"], start=True, stop=True)
                    m.then_inc(s_h1.sem, 1)
                pe.wait_ge(s_h1c.sem, s_h1c.at(b, 2))
                for g in range(NUG):
                    u0 = g * UG
                    o = bk[g // 4][0:UG * JG, (g % 4) * P:(g % 4 + 1) * P]
                    mm(o, A8[:, u0:u0 + UG, :].rearrange("p u j -> p (u j)"), k["cs"][:, 0:P], start=True, stop=False)
                    mm(o, B8[:, u0:u0 + UG, :].rearrange("p u j -> p (u j)"), k["cs"][:, P:], start=False, stop=True).then_inc(s_h2.sem, 1)
                small_mm(VL["f_rows"], (bk[7][:, 0:P], k["ones"], diag[:, 0:P]))
                pe.wait_ge(v.sem, v.at(b, VL["f_soft"]))
                mm(bk[7][:, 0:P], sq[0], k["mixc"], start=True, stop=True)
                mm(bk[7][:, P:2 * P], sq[0], k["mixs"], start=True, stop=True).then_inc(m_.sem, 1)
                gate_flat = gate_w[:, :, :].rearrange("p u c -> p (u c)")
                for g in range(NUG):
                    pe.wait_ge(s_rel.sem, s_rel.at(b, g + 1))
                    pe.wait_ge(s_sig.sem, s_sig.at(b, 4 * g))
                    for i in range(4):
                        e = min(UG * P, (i + 1) * 512)
                        m = mm(bk[2 + i][:, 0:e - i * 512], relu_r[0:UG * JG + 1, g, :], gate_flat[:, i * 512:e], start=True, stop=True)
                    m.then_inc(s_gl.sem, 1)
                pe.wait_ge(s_gx.sem, s_gx.at(b, 2 * NUG))

                def inverse1(p):
                    pe.wait_ge(s_z.sem, s_z.at(b, p - 1))
                    if p < 2:
                        pe.wait_ge(s_rel.sem, s_rel.at(b, NUG))
                    for c in range(2):
                        o = bk[p % 2][0:HALF, c * 256:(c + 1) * 256]
                        mm(o, XR[:, 2 * p + c, :], k["cs"], start=True, stop=False)
                        m = mm(o, XI[:, 2 * p + c, :], k["sc"], start=False, stop=True)
                    m.then_inc(s_i1.sem, 1)

                def inverse2(t):
                    pe.wait_ge(s_z.sem, s_z.at(b, 2 * t + 2))
                    pe.wait_ge(s_abs.sem, s_abs.at(b, t - 1))
                    mm(bk[2 + t % 2][:, :], k["back"][:, 0:P], Z[0:HALF, t % 2, :, 0:P], start=True, stop=False)
                    mm(bk[2 + t % 2][:, :], k["back"][:, P:], Z[0:HALF, t % 2, :, P:], start=False, stop=True).then_inc(s_i2.sem, 1)

                inverse1(0)
                inverse1(1)
                for t in range(NK):
                    if t + 1 < NK:
                        inverse1(2 * t + 2)
                        inverse1(2 * t + 3)
                    inverse2(t)

                def turn(kk):
                    pe.wait_ge(s_row.sem, s_row.at(b, kk + 1))
                    pe.wait_ge(s_trc.sem, s_trc.at(b, kk))
                    for j in range(4):
                        m = nc.tensor.transpose(bk[0][:, j * P:(j + 1) * P], rowbuf[:, j * P:(j + 1) * P], k["eye"])
                    m.then_inc(s_tr.sem, 1)

                def body(kk, par, vrow):
                    last = isinstance(kk, int) and kk == NK - 1
                    pe.wait_ge(s_trc.sem, s_trc.at(b, kk + 1))
                    pe.wait_ge(s_kl[par], b * (8 * NK) + (kk - par) * 8 + 16)
                    pe.wait_ge(s_shr.sem, s_shr.at(b, kk))
                    pe.wait_ge(s_shi.sem, s_shi.at(b, kk))
                    for j in range(4):
                        for s in range(2):
                            m = mm(bk[1 + s][:, j * P:(j + 1) * P], turned[:, j * P:(j + 1) * P], kbuf3[par][:, j, s * P:(s + 1) * P], start=True, stop=True)
                    m.then_inc(s_sh.sem, 1)
                    if not last:
                        turn(kk + 1)
                    pe.wait_ge(s_shr.sem, s_shr.at(b, kk + 1))
                    pe.wait_ge(s_shi.sem, s_shi.at(b, kk + 1))
                    pe.wait_ge(s_os.sem, s_os.at(b, 2 * kk))
                    re, im = shifted[:, 0:512], shifted[:, 512:]
                    mm(bk[3][:, :], mix_t[:, 0, :], re, start=True, stop=False)
                    mm(bk[3][:, :], mix_t[:, 2, :], im, start=False, stop=True)
                    mm(bk[4][:, :], mix_t[:, 0, :], im, start=True, stop=False)
                    mm(bk[4][:, :], mix_t[:, 1, :], re, start=False, stop=True).then_inc(s_o.sem, 1)

                pe.wait_ge(s_abs.sem, s_abs.at(b, NK))
                turn(0)
                chunk_loop(pe, body)
                pe.wait_ge(s_os.sem, s_os.at(b, 2 * NK))
                pe.wait_ge(s_wl, b * 144 + 144)
                pe.wait_ge(s_px.sem, s_px.at(b, NK))
                pe.wait_ge(s_i2.sem, s_i2.at(b, NK))
                pe.wait_ge(s_abs.sem, s_abs.at(b, NK))
                mm(bk[4][:, 0:64], relu_r[:, 0, :], B8[:, 0, :].unsqueeze(1).broadcast_to([P, 8, JG]), start=True, stop=True).then_inc(m_.sem, 1)
                WB16 = halves(WB, T5)

                def gram(kk, s):
                    done, ready = ((s_ga, s_tae), (s_gb, s_tbe))[s]
                    pe.wait_ge(ready.sem, ready.at(b, kk + 1))
                    for j in range(4):
                        m = mm(bk[4][64 * s:64 * s + 64, 0:64], tt[s][:, j, 0:64], tt[s][:, j, 64:P], start=False, stop=True)
                    m.then_inc(done.sem, 1)

                def flip(kk, s):
                    done, copied, read = ((s_ta, s_ae, s_tae), (s_tb, s_be, s_tbe))[s]
                    pe.wait_ge(copied.sem, copied.at(b, 2 * kk + 1))
                    pe.wait_ge(read.sem, read.at(b, kk))
                    for j in range(4):
                        m = nc.tensor.transpose(bk[2 + s][:, j * P:(j + 1) * P], qa[s][:, j * P:(j + 1) * P], k["eye"])
                    m.then_inc(done.sem, 1)

                def body(kk, par, vrow):
                    first = isinstance(kk, int) and kk == 0
                    pe.wait_ge(s_ae.sem, s_ae.at(b, 2 * kk))
                    conv(bk[0][:, :], WA, INNER, kk)
                    mm(bk[0][:, :], bias_ab[:, 0, :], valid[:, vrow:vrow + 4, :], start=False, stop=True).then_inc(s_ca.sem, 1)
                    if not first:
                        flip(kk - 1, 1)
                        gram(kk - 1, 0)
                    pe.wait_ge(s_be.sem, s_be.at(b, 2 * kk))
                    conv(bk[1][:, :], WB16, range(T5), kk)
                    mm(bk[1][:, :], bias_ab[:, 1, :], valid[:, vrow:vrow + 4, :], start=False, stop=True).then_inc(s_cb.sem, 1)
                    if not first:
                        gram(kk - 1, 1)
                    flip(kk, 0)

                chunk_loop(pe, body)
                flip(NK - 1, 1)
                gram(NK - 1, 0)
                gram(NK - 1, 1)
                pe.wait_ge(v.sem, v.at(b, VL["s_rows"]))
                for s in range(2):
                    o = bk[5][64 * s:64 * s + 64, :]
                    mm(o[:, 0:1], k["eye"][:, 0:64], col(12 + s), start=True, stop=True)
                    m = mm(o[:, 64:P], sq[4][:, 64 * s:64 * s + 64], k["shift"], start=True, stop=True)
                m.then_inc(m_.sem, 1)
                small_mm(VL["s_soft"], (bk[5][:, 0:P], afull, pt[:, 2, :]))
                pe.wait_ge(v.sem, v.at(b, VL["s_mix"]))
                WVt_, WCt_ = (W.rearrange("p (t o) -> p t o", o=P) for W in (WV, WC))
                UT = UU.rearrange("p (t o) -> p t o", o=P)
                for i in range(7):
                    e = min(T5, 4 * i + 4)
                    pe.wait_ge(s_uc.sem, s_uc.at(b, i - 1))
                    for t in range(4 * i, e):
                        m = mm(bk[i % 2][:, (t % 4) * P:(t % 4 + 1) * P], WVt_[:, t, :], ap_, start=True, stop=True)
                    m.then_inc(s_u.sem, 1)
                for i in range(7):
                    e = min(T5, 4 * i + 4)
                    pe.wait_ge(s_uc.sem, s_uc.at(b, i + 1))
                    pe.wait_ge(s_mc.sem, s_mc.at(b, i - 1))
                    mm(bk[2 + i % 2][:, 0:(e - 4 * i) * P], v1[:, :], UU[:, 4 * i * P:e * P], start=True, stop=False)
                    for t in range(4 * i, e):
                        m = mm(bk[2 + i % 2][:, (t % 4) * P:(t % 4 + 1) * P], WCt_[:, t, :], pt[:, 3, :], start=False, stop=True)
                    m.then_inc(s_m.sem, 1)
                for t in range(T5):
                    m = mm(bk[6][0:T5, 0:P], vtap[:, t, :], UT[:, t, :], start=(t == 0), stop=(t == T5 - 1))
                m.then_inc(s_bv.sem, 1)
                small_mm(VL["m_rows"], (bk[5][0:1, 0:P], col(21), k["eye"]))
                small_mm(VL["m_max"], (bk[5][:, P:P + 1], k["ones"][0:1, :], small[0:1, 22:23]))
                pe.wait_ge(s_bvc.sem, s_bvc.at(b, 1))
                pe.wait_ge(s_ms.sem, s_ms.at(b, 1))

                def body(kk, par, vrow):
                    o = bk[6 + par][:, :]
                    pe.wait_ge(s_x1.sem, s_x1.at(b, kk - 1))
                    conv(o, M16, range(T5), kk)
                    mm(o, bias_v[:, :], valid[:, vrow:vrow + 4, :], start=False, stop=False)
                    pe.wait_ge(syc[par], b * (8 * NK) + (kk - par) * 8 + 16)
                    mm(o, pt_scaled[:, 1, :], ych[par], start=False, stop=False)
                    pe.wait_ge(sof[par], b * (8 * NK) + (kk - par) * 8 + 16)
                    mm(o, pt_scaled[:, 0, :], of[par], start=False, stop=True).then_inc(s_vc.sem, 1)

                chunk_loop(pe, body)
                small_mm(VL["gn2_mean"], (bk[7][:, 0:1], k["four"], col(0)))
                small_mm(VL["gn2_var"], (bk[7][:, 1:2], k["four"], col(3)))
                assert n[0] + 3 == m_.per

        @block.scalar
        def _(act):
            credit(act, a, s_row, s_hi, s_trc, s_shr, s_xn, s_ab, s_xr, s_t8c, s_rel, s_sig, s_z, s_abs, s_ae, s_be, s_uc, s_mc, s_os, s_of)
            cp = lambda o, i, f=ACT.Copy, **kw: nc.scalar.activation(o, i, f, **kw)
            with act.Fori(0, B) as b:
                n = [0]

                def small_act(wait, o, i, f, **kw):
                    act.wait_ge(v.sem, v.at(b, wait))
                    n[0] += 1
                    cp(o, i, f, **kw).then_inc(a.sem, 1)

                small_act(VL["gn_root"], col(6), col(6), ACT.Sqrt)
                act.wait_ge(v.sem, v.at(b, VL["gn_done"]))
                def normalise(i):
                    part = xpad[:, 2 + 32 * i:34 + 32 * i, 2:2 + P]
                    cp(part, part, ACT.Identity, bias=col(5), scale=col(4)).then_inc(s_xn.sem, 1)

                for t in range(NK):
                    act.wait_ge(s_s1.sem, s_s1.at(b, t + 1))
                    act.wait_ge(s_s2.sem, s_s2.at(b, t - 1))
                    cp(AB[:, t % 2, :, :].rearrange("p c u -> p (c u)"), bk[t % 2][:, :]).then_inc(s_ab.sem, 1)
                    if t > 0:
                        act.wait_ge(s_s2.sem, s_s2.at(b, t))
                        cp(XR[:, 4 * t - 4:4 * t, :], bk[2 + (t - 1) % 2][:, 0:4 * HALF].rearrange("p (c u) -> p c u", u=HALF)).then_inc(s_xr.sem, 1)
                    if t % 8 == 4:
                        normalise(t // 8)
                act.wait_ge(s_s2.sem, s_s2.at(b, NK))
                cp(XR[:, P - 4:P, :], bk[2 + (NK - 1) % 2][:, 0:4 * HALF].rearrange("p (c u) -> p c u", u=HALF)).then_inc(s_xr.sem, 1)
                for hf in range(2):
                    act.wait_ge(s_t8.sem, s_t8.at(b, hf + 1))
                    cp(T8[:, 64 * hf:64 * hf + 64, :], bk[hf][:, :].rearrange("p (w j) -> p w j", j=JG)).then_inc(s_t8c.sem, 1)
                for g in range(NUG):
                    act.wait_ge(s_h2.sem, s_h2.at(b, min(NUG, 4 * (g // 4) + 4)))
                    cp(relu_r[0:UG * JG, g, :], bk[g // 4][0:UG * JG, (g % 4) * P:(g % 4 + 1) * P], ACT.Relu, bias=gate_sb[:, 1:2], scale=gate_sb[:, 0:1]).then_inc(s_rel.sem, 1)
                small_act(VL["f_root"], col(10), col(8), ACT.Sqrt)
                small_act(VL["f_max"], sq[0], sq[1], ACT.Exp, bias=col(15), accum_out=col(16))
                for g in range(NUG):
                    act.wait_ge(s_gl.sem, s_gl.at(b, g + 1))
                    act.wait_ge(s_gx.sem, s_gx.at(b, 2 * g))
                    for i in range(4):
                        e = min(UG, 4 * i + 4)
                        cp(gates[:, 4 * i:e, :], bk[2 + i][:, 0:(e - 4 * i) * P].rearrange("p (u c) -> p u c", c=P), ACT.Sigmoid).then_inc(s_sig.sem, 1)

                def zcopy(p):
                    act.wait_ge(s_i1.sem, s_i1.at(b, p + 1))
                    act.wait_ge(s_i2.sem, s_i2.at(b, p // 2 - 1))
                    cp(Z[0:HALF, p // 2 % 2, 2 * (p % 2):2 * (p % 2) + 2, :], bk[p % 2][0:HALF, :].rearrange("p (c n) -> p c n", c=2)).then_inc(s_z.sem, 1)

                for t in range(NK + 1):
                    if t < NK:
                        zcopy(2 * t)
                        zcopy(2 * t + 1)
                    if t > 0:
                        g = t - 1
                        act.wait_ge(s_i2.sem, s_i2.at(b, g + 1))
                        if g >= 2:
                            act.wait_ge(s_yst[g % 2], b * (8 * NK) + 16 * (g // 2))
                        cp(Yb[:, g % 2, :, :], bk[2 + g % 2][:, :].rearrange("p (c w) -> p c w", c=4), ACT.Abs).then_inc(s_abs.sem, 1)

                def take_rows(kk):
                    act.wait_ge(s_tr.sem, s_tr.at(b, kk))
                    cp(rowbuf.rearrange("p (j w) -> p j w", j=4), window(kk, 2, 2)).then_inc(s_row.sem, 1)

                act.wait_ge(s_i2.sem, s_i2.at(b, NK))
                act.wait_ge(s_gx.sem, s_gx.at(b, 2 * NUG))
                act.wait_ge(s_xn.sem, s_xn.at(b, 4))
                take_rows(0)

                def body(kk, par, vrow):
                    act.wait_ge(s_tr.sem, s_tr.at(b, kk + 1))
                    act.wait_ge(s_sh.sem, s_sh.at(b, kk))
                    cp(turned, bk[0][:, :]).then_inc(s_trc.sem, 1)
                    act.wait_ge(s_px.sem, s_px.at(b, kk - 1))
                    if not (isinstance(kk, int) and kk == NK - 1):
                        take_rows(kk + 1)
                    cp(high[par].rearrange("p (r w) -> p r w", w=P), window(kk, 2, 2), scale=XSCALE).then_inc(s_hi.sem, 1)
                    act.wait_ge(s_sh.sem, s_sh.at(b, kk + 1))
                    act.wait_ge(s_o.sem, s_o.at(b, kk))
                    cp(shifted[:, 0:512], bk[1][:, :]).then_inc(s_shr.sem, 1)
                    act.wait_ge(s_o.sem, s_o.at(b, kk + 1))
                    act.wait_ge(s_of.sem, s_of.at(b, kk))
                    for s in range(2):
                        cp(sq2[s], bk[3 + s][:, :], ACT.Square).then_inc(s_os.sem, 1)
                    act.wait_ge(s_oa.sem, s_oa.at(b, kk + 1))
                    cp(OF[:, :, bass.ds(kk * 4, 4)], sq2[0].rearrange("p (j a) -> p a j", j=4), ACT.Sqrt).then_inc(s_of.sem, 1)

                chunk_loop(act, body)
                def body(kk, par, vrow):
                    for s, (ready, done, read) in enumerate(((s_ca, s_ae, s_ta), (s_cb, s_be, s_tb))):
                        act.wait_ge(ready.sem, ready.at(b, kk + 1))
                        act.wait_ge(read.sem, read.at(b, kk))
                        cp(qa[s], bk[s][:, :]).then_inc(done.sem, 1)
                        act.wait_ge(done.sem, done.at(b, 2 * kk))
                        cp(sqa[s], bk[s][:, :], ACT.Square, accum_out=norms[:, s, bass.ds(kk, 1)]).then_inc(done.sem, 1)

                act.wait_ge(s_yst[0], b * (8 * NK) + 8 * NK)
                act.wait_ge(s_yst[1], b * (8 * NK) + 8 * NK)
                chunk_loop(act, body)
                for s in range(2):
                    small_act(VL["s_root"], col(10 + s), col(8 + s), ACT.Sqrt)
                small_act(VL["s_max"], sq[0][:, 0:64], sq[1][:, 0:64], ACT.Exp, bias=col(15), accum_out=col(16))
                for i in range(7):
                    e = min(T5, 4 * i + 4)
                    act.wait_ge(s_u.sem, s_u.at(b, i + 1))
                    cp(UU[:, 4 * i * P:e * P], bk[i % 2][:, 0:(e - 4 * i) * P]).then_inc(s_uc.sem, 1)
                for i in range(7):
                    e = min(T5, 4 * i + 4)
                    act.wait_ge(s_m.sem, s_m.at(b, i + 1))
                    cp(MM[:, 4 * i * P:e * P], bk[2 + i % 2][:, 0:(e - 4 * i) * P]).then_inc(s_mc.sem, 1)

                small_act(VL["gn2_root"], col(6), col(6), ACT.Sqrt)
                assert n[0] == a.per

        @block.gpsimd
        def _(pool):
            for s in s_x1st:
                pool.sem_inc(s, 16)
            pool.sem_inc(s_gst, 16)


class Counter:

    def __init__(self, sem, per, ahead=1):
        self.sem, self.per, self.ahead = sem, per, ahead

    def at(self, chunk, n):
        return chunk * self.per + self.ahead * self.per + n


def layer1(nc, x1, gn2, W_in, conv_w, conv_b, W_xproj, W_dt, b_dt, A_log, D_param, W_out, out, B):
    CH = 512
    NCH = HW // CH
    N = 16
    R = 8
    G = 4
    NG = N // G
    RC = 512
    K4 = 4
    ctx = ExitStack()
    with ctx:
        sb = lambda name, shape, dt=F32: ctx.enter_context(nc.sbuf_tensor(name, shape, dt))
        pb = lambda name, shape: ctx.enter_context(nc.psum_tensor(name, shape, F32))
        sem = lambda name: ctx.enter_context(nc.semaphore(name))

        w_in = sb("w_in", [P, 4 * P])
        w_conv = sb("w_conv", [P, 2, K4])
        v_convb = sb("v_convb", [P, 2])
        w_bc = sb("w_bc", [P, 2, 3 * 2 * N])
        w_xdt = sb("w_xdt", [P, 2, R])
        w_dt = sb("w_dt", [R, 2 * P])
        v_bdt = sb("v_bdt", [P, 2])
        v_alog = sb("v_alog", [P, 2, N])
        v_aexp = sb("v_aexp", [P, 2, N])
        v_a = sb("v_a", [P, 2, N])
        v_d = sb("v_d", [P, 2])
        w_out = sb("w_out", [P, 2, P])
        ident = sb("ident", [P, P])
        pick = sb("pick", [96, 2 * N, P], BF16)
        gnb = sb("gnb", [P, 2])
        xin = sb("xin", [P, 2, CH])
        xn = sb("xn", [P, CH])
        xs = sb("xs", [P, 2, K4 - 1 + CH])
        conv = sb("conv", [P, 2, CH])
        silu_z = sb("silu_z", [P, 2, 2, CH])
        xc = sb("xc", [P, 2, 2, CH])
        delta = sb("delta", [P, 2, 2, CH])
        du = sb("du", [P, 2, 2, CH])
        parts = sb("parts", [96, 2, CH], BF16)
        rest = sb("rest", [96, CH])
        dt8 = sb("dt8", [R, CH])
        lin = conv
        soft = sb("soft", [P, 2, CH])
        mid = soft[0:96, 0, 0:CH // 2].bitcast(BF16)
        da = sb("da", [P, 4, NG, CH + 1])
        hid = sb("hid", [P, 4, NG, CH + 1])
        carry = sb("carry", [P, 2, N])
        cs = sb("cs", [P, 2, NG, CH])
        y = sb("y", [P, 2, CH])
        img = sb("img", [P, P, P])
        img_flat = img[:, :, :].rearrange("p i j -> p (i j)")
        rbuf = sb("rbuf", [P, 2, RC])

        bb = pb("bb", [P, 2, CH])
        cb = pb("cb", [P, 2, CH])
        yp = pb("yp", [P, 2, CH])
        pj = [pb(f"pj{i}", [P, CH]) for i in range(2)]

        s_w = sem("s_weights_loaded")
        s_cst = sem("s_constants_built")
        s_ap = sem("s_a_ready")
        s_gn = sem("s_gn_loaded")
        s_reset = sem("s_state_reset")
        s_x = [sem(f"s_x_loaded_{q}") for q in range(2)]
        s_xn = Counter(sem("s_xn_ready"), 1, 2)
        s_inp = Counter(sem("s_inproj_done"), 4)
        s_xs = Counter(sem("s_xs_ready"), 2)
        s_conv = Counter(sem("s_conv_step"), 9)
        s_silu = Counter(sem("s_silu_done"), 4)
        s_xp = Counter(sem("s_xproj_done"), 2)
        s_hi = Counter(sem("s_hi_ready"), 2)
        s_rest = Counter(sem("s_rest_ready"), 1)
        s_mid = Counter(sem("s_mid_ready"), 2)
        s_low = Counter(sem("s_low_ready"), 1)
        s_dt = Counter(sem("s_dtproj_done"), 2)
        s_lin = Counter(sem("s_lin_ready"), 2)
        s_neg = Counter(sem("s_neg_ready"), 2)
        s_exp = Counter(sem("s_softexp_ready"), 2)
        s_ln = Counter(sem("s_softln_ready"), 2)
        s_delta = Counter(sem("s_delta_ready"), 2)
        s_du = Counter(sem("s_du_ready"), 2, 2)
        s_da = Counter(sem("s_da_ready"), 2 * G, 2)
        s_bb = Counter(sem("s_b_spread"), 2 * G, 2)
        s_cb = Counter(sem("s_c_spread"), 2 * G, 2)
        s_cs = Counter(sem("s_c_copied"), 2 * G)
        s_m1 = Counter(sem("s_input_ready"), 4 * G, 2)
        s_c0 = Counter(sem("s_carry_in"), 2 * G)
        s_scan = Counter(sem("s_scanned"), 2 * G)
        s_cout = Counter(sem("s_carry_out"), 2 * G)
        s_hc = Counter(sem("s_hc_ready"), 2 * G)
        s_ysum = Counter(sem("s_y_summed"), 2 * G)
        s_yd = Counter(sem("s_y_skip"), 2)
        s_yg = Counter(sem("s_y_gated"), 2, 2)
        s_op = Counter(sem("s_outproj_done"), 1)
        s_img = Counter(sem("s_image_written"), 1, 2)
        s_r = [sem(f"s_residual_loaded_{r}") for r in range(2)]
        s_add = sem("s_residual_added")
        s_st = sem("s_stored")
        block = ctx.enter_context(nc.Block())

        def chunks(eng, body, image_start, image_end):
            with eng.Fori(0, B) as b:
                first, pair = b * NCH, b * (NCH // 2)
                image_start(b)
                body(None, None, first, 0, b, 0, pair)
                body(None, first, first + 1, 1, b, 1, pair)
                with eng.Fori(1, NCH // 2) as i:
                    f = first + i * 2
                    body(f - 2, f - 1, f, 0, b, i * 2, pair + i)
                    body(f - 1, f, f + 1, 1, b, i * 2 + 1, pair + i)
                body(first + NCH - 2, first + NCH - 1, None, 0, b, NCH, None)
                body(first + NCH - 1, None, None, 1, b, NCH + 1, None)
                image_end(b)

        def credit(eng, *counters):
            for s in counters:
                eng.sem_inc(s.sem, s.per * s.ahead)

        NR = HW // RC

        @block.sync
        def _(sp):
            for dst, src in (
                (w_in[:, :], W_in), (w_conv[:, :, :], conv_w.rearrange("(h p) k -> p h k", p=P)),
                (v_convb[:, :], conv_b.rearrange("(h p) -> p h", p=P)),
                (w_xdt[:, :, :], W_xproj[:, 0:R].rearrange("(h p) r -> p h r", p=P)),
                (w_dt[:, :], W_dt), (v_bdt[:, :], b_dt.rearrange("(h p) -> p h", p=P)),
                (v_alog[:, :, :], A_log.rearrange("(h p) n -> p h n", p=P)),
                (v_d[:, :], D_param.rearrange("(h p) -> p h", p=P)),
                (w_out[:, :, :], W_out.rearrange("(h p) o -> p h o", p=P)),
                *((w_bc[:, :, 2 * N * j:2 * N * (j + 1)], W_xproj[:, R:].rearrange("(h p) r -> p h r", p=P)) for j in range(3)),
            ):
                sp.dma_start(dst, src, allow_slow_non_contiguous=True).then_inc(s_w, 16)

            def start(b):
                sp.wait_ge(s_xn.sem, s_xn.at(b * NCH, 0))
                sp.dma_start(gnb[:, :], gn2[bass.ds(b, 1), :, :].rearrange("a p t -> p (a t)")).then_inc(s_gn, 16)

            def body(t, c, front, q, b, k, m):
                if front is None:
                    return
                sp.wait_ge(s_xn.sem, s_xn.at(front, -1))
                sp.dma_start(xin[:, q, :], x1[bass.ds(b, 1), :, bass.ds(k * CH, CH)].rearrange("a p n -> p (a n)")).then_inc(s_x[q], 16)

            def end(b):
                for r in range(NR + 1):
                    if r:
                        sp.wait_ge(s_add, b * NR + r + 2)
                        sp.dma_start(out[bass.ds(b, 1), :, (r - 1) * RC:r * RC].rearrange("a p n -> p (a n)"), img_flat[:, (r - 1) * RC:r * RC]).then_inc(s_st, 16)
                    if r == NR:
                        break
                    sp.dma_start(rbuf[:, r % 2, :], x1[bass.ds(b, 1), :, r * RC:(r + 1) * RC].rearrange("a p n -> p (a n)")).then_inc(s_r[r % 2], 16)

            sp.sem_inc(s_st, 16)
            chunks(sp, body, start, end)
            sp.wait_ge(s_st, 16 * (NR * B + 1))

        @block.tensor
        def _(pe):
            credit(pe, s_inp, s_xp, s_dt, s_bb, s_cb, s_ysum, s_op)
            pe.wait_ge(s_w, 16 * 12)
            pe.wait_ge(s_cst, 5)

            def front_a(f, first, pieces):
                if 0 in pieces:
                    pe.wait_ge(s_xn.sem, s_xn.at(f, 1))
                for i in pieces:
                    if i < 2:
                        pe.wait_ge(s_lin.sem, s_lin.at(f, i - 1))
                    if i == 1 and first:
                        pe.wait_ge(s_img.sem, s_img.at(f, 0))
                    if i >= 2:
                        pe.wait_ge(s_xs.sem, s_xs.at(f, i - 1))
                    nc.tensor.matmul(pj[i % 2][:, :], w_in[:, i * P:(i + 1) * P], xn[:, :], start=True, stop=True).then_inc(s_inp.sem, 1)

            def front_b(f, q):
                pe.wait_ge(s_silu.sem, s_silu.at(f, 4))
                for h in range(2):
                    m = nc.tensor.matmul(pj[0][0:96, :], w_bc[:, h, :], xc[:, q, h, :], start=(h == 0), stop=(h == 1))
                m.then_inc(s_xp.sem, 1)
                for h in range(2):
                    m = nc.tensor.matmul(pj[1][0:R, :], w_xdt[:, h, :], xc[:, q, h, :], start=(h == 0), stop=(h == 1))
                m.then_inc(s_xp.sem, 1)

            def front_c(f, q, t):
                pe.wait_ge(s_hi.sem, s_hi.at(f, 2))
                pe.wait_ge(s_rest.sem, s_rest.at(f, 1))
                for h in range(2):
                    if h == 1 and t is not None:
                        pe.wait_ge(s_img.sem, s_img.at(t, 1))
                    nc.tensor.matmul(pj[h][:, :], w_dt[:, h * P:(h + 1) * P], dt8[:, :], start=True, stop=True).then_inc(s_dt.sem, 1)

            def spread_b(c, q, u):
                pe.wait_ge(s_m1.sem, s_m1.at(c, 2 * u))
                for j in range(2):
                    m = nc.tensor.matmul(bb[:, j, :], pick[:, 2 * u + j, :], parts[:, q, :], start=True, stop=True)
                m.then_inc(s_bb.sem, 1)

            def spread_c(c, q, p):
                pe.wait_ge(s_cs.sem, s_cs.at(c, p))
                for j in range(2):
                    m = nc.tensor.matmul(cb[:, j, :], pick[:, N + 2 * p + j, :], parts[:, q, :], start=True, stop=True)
                m.then_inc(s_cb.sem, 1)

            def sum_y(c, g, h, states):
                if 0 in states:
                    if g == 0:
                        pe.wait_ge(s_yd.sem, s_yd.at(c, h - 1))
                    pe.wait_ge(s_hc.sem, s_hc.at(c, 2 * g + h + 1))
                for n in states:
                    m = nc.tensor.matmul(yp[:, h, :], ident[:, :], hid[:, (2 * g + h) % 4, n, 1:], start=(g == 0 and n == 0), stop=(g == G - 1 and n == NG - 1), skip_group_check=True)
                if NG - 1 in states:
                    m.then_inc(s_ysum.sem, 1)

            def out_proj(t, c, f):
                if f is not None:
                    pe.wait_ge(s_hi.sem, s_hi.at(f, 2))
                elif c is not None:
                    pe.wait_ge(s_lin.sem, s_lin.at(c, 2))
                else:
                    pe.wait_ge(s_img.sem, s_img.at(t, 0))
                for h in range(2):
                    pe.wait_ge(s_yg.sem, s_yg.at(t, h + 1))
                    m = nc.tensor.matmul(pj[1][:, :], w_out[:, h, :], y[:, h, :], start=(h == 0), stop=(h == 1))
                m.then_inc(s_op.sem, 1)

            def body(t, c, f, qf, b, k, m):
                q = 1 - qf
                for g in range(G):
                    sc, sg = (c, g - 1) if g else (t, G - 1)
                    nxt, nq, ng = (c, q, g + 1) if g < G - 1 else (f, qf, 0)
                    if f is not None and g == 0:
                        front_a(f, c is None, (0, 1))
                    if sc is not None and g == 1:
                        sum_y(sc, sg, 0, (0, 1))
                    if c is not None:
                        spread_b(c, q, 2 * g + 1)
                        spread_c(c, q, 2 * g + 1)
                    if t is not None and g == 2:
                        out_proj(t, c, f)
                    if sc is not None:
                        sum_y(sc, sg, 0, (2, 3) if g == 1 else (0, 1, 2, 3))
                    if f is not None and g == 0:
                        front_a(f, c is None, (2, 3))
                    if f is not None and g == 2:
                        front_c(f, qf, t)
                    if nxt is not None:
                        if g == G - 1:
                            pe.wait_ge(s_low.sem, s_low.at(f, 1))
                            pe.wait_ge(s_mid.sem, s_mid.at(f, 2))
                        spread_b(nxt, nq, 2 * ng)
                        spread_c(nxt, nq, 2 * ng)
                    if f is not None and g == 1:
                        front_b(f, qf)
                    if sc is not None:
                        sum_y(sc, sg, 1, (0, 1, 2, 3))

            chunks(pe, body, lambda b: None, lambda b: None)

        @block.scalar
        def _(act):
            credit(act, s_xn, s_xs, s_silu, s_hi, s_mid, s_lin, s_exp, s_ln, s_da, s_cs, s_img)
            act.wait_ge(s_w, 16 * 12)
            nc.scalar.activation(v_aexp[:, :, :], v_alog[:, :, :], ACT.Exp).then_inc(s_ap, 1)
            act.wait_ge(s_ap, 2)
            act.wait_ge(s_cst, 5)

            def exps(c, q, g, h):
                act.wait_ge(s_scan.sem, s_scan.at(c, 2 * g + h - 3))
                if g == 0:
                    act.wait_ge(s_delta.sem, s_delta.at(c, h + 1))
                for n in range(NG):
                    m = nc.scalar.activation(da[:, (2 * g + h) % 4, n, 1:], delta[:, q, h, :], ACT.Exp, scale=v_a[:, h, NG * g + n:NG * g + n + 1])
                    if n == NG - 1:
                        m.then_inc(s_da.sem, 1)
                copy_c(c, g, h)

            def copy_c(c, g, h):
                if h == 0:
                    act.wait_ge(s_hc.sem, s_hc.at(c, 2 * (g - 1)))
                act.wait_ge(s_cb.sem, s_cb.at(c, 2 * g + h + 1))
                nc.scalar.activation(cs[:, g % 2, 2 * h:2 * h + 2, :], cb[:, :, :], ACT.Copy).then_inc(s_cs.sem, 1)

            def front_a(f, q, m):
                act.wait_ge(s_x[q], m * 16 + 16)
                act.wait_ge(s_inp.sem, s_inp.at(f, 0))
                nc.scalar.activation(xn[:, :], xin[:, q, :], ACT.Identity, bias=gnb[:, 1:2], scale=gnb[:, 0:1]).then_inc(s_xn.sem, 1)

            def front_xs(f):
                for h in range(2):
                    act.wait_ge(s_inp.sem, s_inp.at(f, h + 1))
                    act.wait_ge(s_conv.sem, s_conv.at(f, 0))
                    nc.scalar.activation(xs[:, h, K4 - 1:], pj[h][:, :], ACT.Copy).then_inc(s_xs.sem, 1)

            def front_b(f, q, m):
                for h in range(2):
                    act.wait_ge(s_inp.sem, s_inp.at(f, h + 3))
                    act.wait_ge(s_yg.sem, s_yg.at(f, -2))
                    nc.scalar.activation(silu_z[:, q, h, :], pj[h][:, :], ACT.Silu).then_inc(s_silu.sem, 1)
                for h in range(2):
                    act.wait_ge(s_conv.sem, s_conv.at(f, 7 + h))
                    nc.scalar.activation(xc[:, q, h, :], conv[:, h, :], ACT.Silu).then_inc(s_silu.sem, 1)

            def front_parts(f, q):
                act.wait_ge(s_xp.sem, s_xp.at(f, 1))
                act.wait_ge(s_cb.sem, s_cb.at(f, -2 * G))
                act.wait_ge(s_bb.sem, s_bb.at(f, -2 * G))
                nc.scalar.activation(parts[:, q, :], pj[0][0:96, :], ACT.Copy).then_inc(s_hi.sem, 1)
                act.wait_ge(s_xp.sem, s_xp.at(f, 2))
                act.wait_ge(s_dt.sem, s_dt.at(f, 0))
                nc.scalar.activation(dt8[:, :], pj[1][0:R, :], ACT.Copy).then_inc(s_hi.sem, 1)

            def front_mid(f, q):
                act.wait_ge(s_rest.sem, s_rest.at(f, 1))
                act.wait_ge(s_hi.sem, s_hi.at(f, 1))
                nc.scalar.activation(parts[32:64, q, :], rest[32:64, :], ACT.Copy).then_inc(s_mid.sem, 1)
                act.wait_ge(s_delta.sem, s_delta.at(f, 0))
                nc.scalar.activation(mid[64:96, :], rest[64:96, :], ACT.Copy).then_inc(s_mid.sem, 1)

            def front_c(f, q, m):
                for h in range(2):
                    act.wait_ge(s_dt.sem, s_dt.at(f, h + 1))
                    act.wait_ge(s_delta.sem, s_delta.at(f, h - 1))
                    nc.scalar.activation(lin[:, h, :], pj[h][:, :], ACT.Identity, bias=v_bdt[:, h:h + 1]).then_inc(s_lin.sem, 1)

            def front_soft(f):
                for h in range(2):
                    act.wait_ge(s_neg.sem, s_neg.at(f, h + 1))
                    nc.scalar.activation(soft[:, h, :], soft[:, h, :], ACT.Exp).then_inc(s_exp.sem, 1)
                for h in range(2):
                    act.wait_ge(s_exp.sem, s_exp.at(f, h + 1))
                    nc.scalar.activation(soft[:, h, :], soft[:, h, :], ACT.Ln, bias=1.0).then_inc(s_ln.sem, 1)

            def image(t, b, k):
                act.wait_ge(s_op.sem, s_op.at(t, 1))
                act.wait_ge(s_st, b * (NR * 16) + 16)
                nc.scalar.activation(img[:, :, bass.ds((k - 2) * 4, 4)], pj[1][:, :].rearrange("p (j i) -> p i j", j=4), ACT.Copy).then_inc(s_img.sem, 1)

            def body(t, c, f, qf, b, k, m):
                q = 1 - qf
                for g in range(G):
                    if f is not None and g == 0:
                        front_a(f, qf, m)
                    if f is not None and g == 3:
                        front_c(f, qf, m)
                    if c is not None:
                        exps(c, q, g, 0)
                    if f is not None:
                        if g == 0:
                            front_xs(f)
                        if g == 2:
                            front_parts(f, qf)
                        if g == 3:
                            front_soft(f)
                    if c is not None:
                        exps(c, q, g, 1)
                    if f is not None:
                        if g == 1:
                            front_b(f, qf, m)
                    if t is not None and g == 2:
                        image(t, b, k)
                    if f is not None and g == 2:
                        front_mid(f, qf)

            def start(b):
                act.wait_ge(s_gn, b * 16 + 16)

            chunks(act, body, start, lambda b: None)

        @block.vector
        def _(dve):
            credit(dve, s_conv, s_rest, s_low, s_neg, s_delta, s_m1, s_c0, s_scan, s_cout, s_yd)
            dve.sem_inc(s_reset, 2)
            nc.vector.memset(ident[:, :], 0.0).then_inc(s_cst, 1)
            nc.vector.memset(da[:, :, :, 0:1], 0.0).then_inc(s_cst, 1)
            dve.wait_ge(s_ap, 1)
            nc.vector.tensor_scalar(v_a[:, :, :], v_aexp[:, :, :], -1.0, None, ALU.mult).then_inc(s_ap, 1)
            dve.wait_ge(s_w, 16 * 12)
            dve.wait_ge(s_cst, 5)

            def front_a(f, q):
                for h in range(2):
                    dve.wait_ge(s_xs.sem, s_xs.at(f, h + 1))
                    dve.wait_ge(s_silu.sem, s_silu.at(f, 0))
                    dve.wait_ge(s_delta.sem, s_delta.at(f, 0))
                    nc.vector.tensor_scalar(conv[:, h, :], xs[:, h, K4 - 1:], w_conv[:, h, K4 - 1:K4], v_convb[:, h:h + 1], ALU.mult, ALU.add).then_inc(s_conv.sem, 1)
                for t in range(K4 - 2, -1, -1):
                    for h in range(2):
                        dve.wait_ge(s_conv.sem, s_conv.at(f, 2 * (K4 - 2 - t) + h + 1))
                        nc.vector.scalar_tensor_tensor(conv[:, h, :], xs[:, h, t:t + CH], w_conv[:, h, t:t + 1], conv[:, h, :], ALU.mult, ALU.add).then_inc(s_conv.sem, 1)
                dve.wait_ge(s_conv.sem, s_conv.at(f, 8))
                nc.vector.tensor_copy(xs[:, :, 0:K4 - 1], xs[:, :, CH:CH + K4 - 1]).then_inc(s_conv.sem, 1)

            def front_b(f, q):
                dve.wait_ge(s_hi.sem, s_hi.at(f, 1))
                dve.wait_ge(s_mid.sem, s_mid.at(f, 0))
                dve.wait_ge(s_low.sem, s_low.at(f, 0))
                nc.vector.tensor_tensor(rest[:, :], pj[0][0:96, :], parts[:, q, :], ALU.subtract).then_inc(s_rest.sem, 1)

            def front_c(f, q):
                dve.wait_ge(s_mid.sem, s_mid.at(f, 2))
                nc.vector.tensor_tensor(parts[64:96, q, :], rest[64:96, :], mid[64:96, :], ALU.subtract).then_inc(s_low.sem, 1)

            def front_neg(f):
                for h in range(2):
                    dve.wait_ge(s_lin.sem, s_lin.at(f, h + 1))
                    dve.wait_ge(s_low.sem, s_low.at(f, 1))
                    nc.vector.scalar_tensor_tensor(soft[:, h, :], lin[:, h, :], -1.0, lin[:, h, :], ALU.mult, ALU.min).then_inc(s_neg.sem, 1)

            def front_d(f, q):
                for h in range(2):
                    dve.wait_ge(s_ln.sem, s_ln.at(f, h + 1))
                    dve.wait_ge(s_da.sem, s_da.at(f, -2 * G))
                    dve.wait_ge(s_du.sem, s_du.at(f, -2))
                    nc.vector.scalar_tensor_tensor(delta[:, q, h, :], lin[:, h, :], 0.0, soft[:, h, :], ALU.max, ALU.add).then_inc(s_delta.sem, 1)

            def inputs(c, q, u):
                g = u // 2
                dve.wait_ge(s_bb.sem, s_bb.at(c, u + 1))
                for h in range(2):
                    slot = (2 * g + h) % 4
                    if u % 2 == 0:
                        dve.wait_ge(s_ysum.sem, s_ysum.at(c, 2 * g + h - 3))
                    if u == 0:
                        dve.wait_ge(s_du.sem, s_du.at(c, h + 1))
                    o = hid[:, slot, 2 * (u % 2):2 * (u % 2) + 2, 1:]
                    nc.vector.tensor_tensor(o, bb[:, :, :], du[:, q, h, :].unsqueeze(1).broadcast_to([P, 2, CH]), ALU.mult).then_inc(s_m1.sem, 1)

            def carry_in(c, g, h):
                dve.wait_ge(s_cout.sem, s_cout.at(c, 2 * g + h - 3))
                nc.vector.tensor_copy(hid[:, (2 * g + h) % 4, :, 0:1], carry[:, h, NG * g:NG * (g + 1)].unsqueeze(2)).then_inc(s_c0.sem, 1)

            def scan(c, g, h):
                slot = (2 * g + h) % 4
                dve.wait_ge(s_c0.sem, s_c0.at(c, 2 * g + h + 1))
                dve.wait_ge(s_m1.sem, s_m1.at(c, 4 * g + h + 3))
                dve.wait_ge(s_da.sem, s_da.at(c, 2 * g + h + 1))
                flat = hid[:, slot, :, :].rearrange("p n t -> p (n t)")
                nc.vector.tensor_tensor_scan(flat, da[:, slot, :, :].rearrange("p n t -> p (n t)"), flat, 0.0, ALU.mult, ALU.add).then_inc(s_scan.sem, 1)
                dve.wait_ge(s_scan.sem, s_scan.at(c, 2 * g + h + 1))
                nc.vector.tensor_copy(carry[:, h, NG * g:NG * (g + 1)].unsqueeze(2), hid[:, slot, :, CH:CH + 1]).then_inc(s_cout.sem, 1)

            def skip(t, q, h):
                dve.wait_ge(s_ysum.sem, s_ysum.at(t, 2 * G - 1 + h))
                dve.wait_ge(s_op.sem, s_op.at(t, 0))
                nc.vector.scalar_tensor_tensor(y[:, h, :], xc[:, q, h, :], v_d[:, h:h + 1], yp[:, h, :], ALU.mult, ALU.add).then_inc(s_yd.sem, 1)

            def body(t, c, f, qf, b, k, m):
                q = 1 - qf
                for g in range(G):
                    sc, sg = (c, g - 1) if g else (t, G - 1)
                    if sc is not None:
                        carry_in(sc, sg, 1)
                    if c is not None:
                        inputs(c, q, 2 * g)
                    if t is not None and g == 1:
                        skip(t, qf, 1)
                    if f is not None and g == 2:
                        front_b(f, qf)
                    if sc is not None:
                        scan(sc, sg, 1)
                    if f is not None and g == 2:
                        front_c(f, qf)
                    if c is not None:
                        carry_in(c, g, 0)
                        inputs(c, q, 2 * g + 1)
                    if f is not None and g == 2:
                        front_neg(f)
                    if f is not None and g == 3:
                        front_d(f, qf)
                    if c is not None:
                        scan(c, g, 0)
                    if t is not None and g == 0:
                        skip(t, qf, 0)
                    if f is not None and g == 0:
                        front_a(f, qf)

            def start(b):
                dve.wait_ge(s_cout.sem, s_cout.at(b * NCH, 0))
                dve.wait_ge(s_conv.sem, s_conv.at(b * NCH, 0))
                nc.vector.memset(carry[:, :, :], 0.0).then_inc(s_reset, 1)
                nc.vector.memset(xs[:, :, 0:K4 - 1], 0.0).then_inc(s_reset, 1)
                dve.wait_ge(s_reset, b * 2 + 4)

            chunks(dve, body, start, lambda b: None)

        @block.gpsimd
        def _(pool):
            credit(pool, s_du, s_hc, s_yg)
            pool.sem_inc(s_add, 2)
            pool.wait_ge(s_cst, 2)
            nc.gpsimd.affine_select(out=ident[:, :], in_=ident[:, :], compare_op=ALU.not_equal, fill=1.0, base=0, pattern=[[-1, P]], channel_multiplier=1).then_inc(s_cst, 1)
            nc.gpsimd.memset(pick[:, :, :], 0.0).then_inc(s_cst, 1)
            pool.wait_ge(s_cst, 4)
            for j in range(3):
                part = pick[32 * j:32 * (j + 1), :, :]
                m = nc.gpsimd.affine_select(out=part, in_=part, compare_op=ALU.not_equal, fill=1.0, base=0, pattern=[[-1, 2 * N], [0, P]], channel_multiplier=1)
            m.then_inc(s_cst, 1)

            def weigh(c, g, h):
                pool.wait_ge(s_cs.sem, s_cs.at(c, 2 * (g + 1)))
                pool.wait_ge(s_cout.sem, s_cout.at(c, 2 * g + h + 1))
                slot = (2 * g + h) % 4
                nc.gpsimd.tensor_tensor(hid[:, slot, :, 1:], hid[:, slot, :, 1:], cs[:, g % 2, :, :], ALU.mult).then_inc(s_hc.sem, 1)

            def gate(t, q):
                for h in range(2):
                    pool.wait_ge(s_yd.sem, s_yd.at(t, h + 1))
                    nc.gpsimd.tensor_tensor(y[:, h, :], y[:, h, :], silu_z[:, q, h, :], ALU.mult).then_inc(s_yg.sem, 1)

            def body(t, c, f, qf, b, k, m):
                for g in range(G):
                    sc, sg = (c, g - 1) if g else (t, G - 1)
                    if sc is not None:
                        weigh(sc, sg, 1)
                    if f is not None and g == 3:
                        for h in range(2):
                            pool.wait_ge(s_delta.sem, s_delta.at(f, h + 1))
                            pool.wait_ge(s_silu.sem, s_silu.at(f, h + 3))
                            pool.wait_ge(s_m1.sem, s_m1.at(f, -4 * G))
                            nc.gpsimd.tensor_tensor(du[:, qf, h, :], delta[:, qf, h, :], xc[:, qf, h, :], ALU.mult).then_inc(s_du.sem, 1)
                    if c is not None:
                        weigh(c, g, 0)
                    if t is not None and g == 0:
                        gate(t, qf)

            def end(b):
                pool.wait_ge(s_img.sem, s_img.at(b * NCH + NCH - 1, 1))
                for r in range(NR):
                    part = img_flat[:, r * RC:(r + 1) * RC]
                    pool.wait_ge(s_r[r % 2], b * (8 * NR) + 16 * (r // 2 + 1))
                    nc.gpsimd.tensor_tensor(part, part, rbuf[:, r % 2, :], ALU.add).then_inc(s_add, 1)

            chunks(pool, body, lambda b: None, end)


_L0 = ['temp_f', 'w1', 'b1', 'bn_gamma', 'bn_beta', 'bn_mean', 'bn_var', 'w2', 'b2', 'projf_w', 'temp_s', 'q1_w', 'q1_b', 'k1_w', 'k1_b', 'v1_w', 'v1_b', 'q3_w', 'q5_w', 'k3_w', 'k5_w', 'v3_w', 'v5_w', 'c3_w', 'c5_w', 'projs_w']
_L1 = ["W_in", "conv_w", "conv_b", "W_xproj", "W_dt", "b_dt", "A_log", "D_param", "W_out"]


def build(nc, x, out, table, shift_d, l0, l1):
    B = x.shape[0]

    def scratch(name, shape):
        return nc.dram_tensor(name, shape, F32, kind="Internal").ap()

    x1, gn2 = scratch("x1", (B, P, HW)), scratch("gn2", (B, P, 2))
    layer0(nc, B, x, table, shift_d, l0, scratch("kernels", (P, 4 * TAPS)), scratch("gated", (B, P, P, P)),
           scratch("heads", (B, P, HW)), x1, gn2)
    layer1(nc, x1, gn2, *(l1[n] for n in _L1), out.rearrange("b c i j -> b c (i j)"), B)


def kernel(**inputs):
    import numpy as _np
    import concourse.bacc as _bacc
    from concourse import mybir as _mybir
    from concourse.bass_utils import run_bass_kernel_spmd as _run

    nc = _bacc.Bacc("TRN2", target_bir_lowering=False, num_devices=1, dynamic_dma_scratch_size=1024)
    arrays, aps = {}, {}

    def feed(name, a):
        a = _np.ascontiguousarray(a)
        arrays[f"in_{name}"] = a
        aps[name] = nc.dram_tensor(f"in_{name}", a.shape, _mybir.dt.from_np(a.dtype), kind="ExternalInput").ap()

    for name, a in inputs.items():
        feed(name, a)
    feed("table", constants()[0])
    feed("shift_d", shifts())
    x = inputs["x"]
    out = nc.dram_tensor("out", x.shape, _mybir.dt.float32, kind="ExternalOutput").ap()
    build(nc, aps["x"], out, aps["table"], aps["shift_d"], {n: aps["L0_conv_" + n] for n in _L0}, {n: aps["L1_conv_" + n] for n in _L1})
    r = _run(nc, [arrays], core_ids=[0])
    return r.results[0]["out"]
```

```python
from contextlib import ExitStack
from typing import Any, NamedTuple
import numpy as np
import concourse.bass as bass
from concourse import mybir

F32 = mybir.dt.float32
BF16 = mybir.dt.bfloat16
F16 = mybir.dt.float16
ALU = mybir.AluOpType
ACT = mybir.ActivationFunctionType
AX = mybir.AxisListType

P = 128
HW = 16384
HALF = 65
UG, JG = 13, 8
NUG = HALF // UG
T5 = 25
INNER = [5 * i + j for i in (1, 2, 3) for j in (1, 2, 3)]
WP = P + 4
TAPS = T5 * P
XSCALE, WMAX = 128.0, 16384.0


def constants():
    i = np.arange(P)
    cos, sin = (f(2 * np.pi * (np.outer(i, i) % P) / P) for f in (np.cos, np.sin))
    wt = np.where((i[:HALF] == 0) | (i[:HALF] == 64), 1.0, 2.0)[:, None] / HW
    o64 = np.arange(64)
    head = (i[:, None] // 16 == i // 16) * 1.0
    valid = np.zeros((T5, 8, P))
    for t in range(T5):
        dh, dw = t // 5 - 2, t % 5 - 2
        for n, h in enumerate((0, 1, 64, 64, 64, 64, 126, 127)):
            valid[t, n] = (0 <= h + dh < P) * ((0 <= i + dw) & (i + dw < P))
    spread = np.zeros((9, UG, UG * JG + 1))
    for u in range(UG):
        spread[8, u, UG * JG] = 1
        for j in range(JG):
            spread[j, u, u * JG + j] = 1
    parts = {
        "fwd": np.concatenate([cos[:, :HALF], sin[:, 1:64]], 1),
        "cs": np.concatenate([cos, -sin], 1), "sc": np.concatenate([sin, cos], 1),
        "back": np.concatenate([wt * cos[:HALF], wt * sin[:HALF]], 1),
        "eye": np.eye(P), "ones": np.ones((P, P)),
        "head": head, "head64": ((i[:, None] // 16) % 4 == o64 // 16),
        "four": (i[:, None] // 4 == i // 4) / 4,
        "mixc": head * np.cos(2 * np.pi * np.outer(i, i) / 16) / 16, "mixs": head * np.sin(2 * np.pi * np.outer(i, i) / 16) / 16,
        "mixi": head * (i % 16 == 0) / 16,
        "shift": (i[:, None] == 64 + o64), "valid": valid.reshape(T5, -1),
        "heads": (np.arange(8)[:, None] == i // 16), "rep8": (np.arange(8)[:, None] == np.arange(UG * JG) % JG),
        "mpair": (i[:, None] // 2 == o64), "mgroup": (i[:, None] % 64 == o64),
        "spread": spread.reshape(9, -1), "tap": np.broadcast_to(np.eye(T5).reshape(1, -1), (P, T5 * T5)),
    }
    at, cols = {}, 0
    for k, v in parts.items():
        at[k] = (cols, v.shape[0], v.shape[1])
        cols += v.shape[1]
    packed = np.zeros((P, cols), np.float32)
    for k, v in parts.items():
        packed[:v.shape[0], at[k][0]:at[k][0] + v.shape[1]] = v
    return packed, at


def shifts():
    i = np.arange(P)
    t = i[None, None, :] - i[:, None, None] + i[None, :, None] / P
    whole = t == np.round(t)
    safe = np.where(whole, 0.5, t)
    series = (np.exp(2j * np.pi * safe) - 1) / (np.exp(2j * np.pi * safe / P) - 1) / P
    d = np.where(whole, (t % P == 0) * (1.0 + 0j), series)
    return np.concatenate([d.real, d.imag], 2).astype(np.float32)


class Count:

    def __init__(self, sem, per):
        self.sem, self.per = sem, per

    def at(self, b, n):
        return b * self.per + self.per + n


def layer0(nc, B, x, table, shift_d, w, wts, y_d, of_d, x1, gn2):
    _, at = constants()
    ctx = ExitStack()
    with ctx:
        sb = lambda name, shape, dt=F32: ctx.enter_context(nc.sbuf_tensor(name, shape, dt))
        sem = lambda name: ctx.enter_context(nc.semaphore(name))
        counters = []

        def count(name, per):
            counters.append(Count(sem(name), per))
            return counters[-1]

        setup_from = at["mpair"][0]
        ncols = at["tap"][0] + at["tap"][2]
        ctab = sb("ctab", [P, setup_from])
        xpad = sb("xpad", [P, WP, WP])
        xpad_flat = xpad[:, :, :].rearrange("p h w -> p (h w)")
        region = sb("region", [P, 17408])
        work = sb("work", [P, 11264])
        k = {n: ctab[:r, c0:c0 + n_] for n, (c0, r, n_) in at.items() if c0 < setup_from}
        stab = xpad_flat[:, 0:ncols - setup_from]
        ks = {n: stab[:r, c0 - setup_from:c0 - setup_from + n_] for n, (c0, r, n_) in at.items() if c0 >= setup_from}
        valid = k["valid"].rearrange("t (r n) -> t r n", n=P)
        XR = region[:, 0:P * HALF].rearrange("p (c u) -> p c u", u=HALF)
        XI = region[:, P * HALF:2 * P * HALF].rearrange("p (c u) -> p c u", u=HALF)
        halves = lambda v, n: v.bitcast(F16).rearrange("p (s t o) -> p s t o", s=2, t=n)
        pixels16 = xpad[:, :, :].bitcast(F16).rearrange("p h (w s) -> p h s w", s=2)
        WA = halves(region[:, 0:9 * P], 9)
        cut = [9 * P + i * TAPS for i in range(6)]
        WB, WV, WC, UU, MM = (region[:, cut[i]:cut[i + 1]] for i in range(5))
        M16 = halves(UU, T5)

        pt = sb("pt", [P, 4, P])
        v1 = sb("v1", [P, P])
        floor = sb("floor", [P, 1])
        w1t = sb("w1t", [P, JG])
        gate_w = sb("gate_w", [UG * JG + 1, UG, P])
        gate_sb = sb("gate_sb", [UG * JG, 2])
        temps = sb("temps", [P, 2])
        vtap = sb("vtap", [P, T5, T5])
        bias_ab = sb("bias_ab", [T5, 2, P])
        bias_v = sb("bias_v", [T5, P])
        small = sb("small", [P, 64])
        stats = sb("stats", [P, 32, 6])
        mix_t = sb("mix_t", [P, 3, P])
        relu_r = sb("relu_r", [P, NUG, P])
        A8 = sb("A8", [P, HALF, JG])
        B8 = sb("B8", [P, HALF, JG])
        norms = sb("norms", [P, 2, 32])

        wk = lambda o, n: work[:, o:o + n]
        xh = wk(0, 4096).rearrange("p (s c w) -> p s c w", s=2, w=P)
        AB = wk(4096, 1024).rearrange("p (s c u) -> p s c u", s=2, u=P)
        T8 = wk(5120, 1024).rearrange("p (w j) -> p w j", j=JG)
        gates = wk(0, UG * P).rearrange("p (u c) -> p u c", c=P)
        Z = wk(2048, 2048).rearrange("p (s c n) -> p s c n", s=2, c=4)
        Yb = wk(4096, 1024).rearrange("p (s c w) -> p s c w", s=2, w=P)
        rows = wk(6144, 256)
        diag = wk(6400, 256)
        sq = [wk(6656 + P * i, P) for i in range(6)]
        rowbuf = wk(0, 512)
        turned = wk(512, 512)
        shifted = wk(1024, 1024)
        sq2 = [wk(2048 + 512 * i, 512) for i in range(2)]
        kbuf = [wk(7424 + 1024 * i, 1024) for i in range(2)]
        kbuf3 = [v_.rearrange("p (j n) -> p j n", j=4) for v_ in kbuf]
        high = [wk(3072 + 256 * i, 256).bitcast(F16) for i in range(2)]
        OF = region[:, 0:HW].rearrange("p (a h) -> p a h", h=P)
        qa = [wk(512 * i, 512) for i in range(2)]
        tt = [wk(1024 + 512 * i, 512).rearrange("p (j o) -> p j o", o=P) for i in range(2)]
        pt_scaled = wk(6144, 2 * P).rearrange("p (i o) -> p i o", i=2)
        of = [wk(2048 + 512 * i, 512) for i in range(2)]
        sqa = [wk(3072 + 512 * i, 512) for i in range(2)]
        ych = [wk(4096 + 512 * i, 512) for i in range(2)]
        xch = [wk(5120 + 512 * i, 512) for i in range(2)]
        x1c = [wk(7424 + 512 * i, 512) for i in range(2)]
        afull = wk(8448, P)
        ap_ = wk(8576, P)
        sparse = wk(0, T5 * 64).rearrange("p (t o) -> p t o", o=64)
        btap = wk(1600, T5 * T5).rearrange("p (t s) -> p t s", s=T5)
        wq = wk(2304, P)
        w5 = wk(2432, T5)
        w2 = wk(2464, 50).rearrange("p (i t) -> p i t", i=2)
        bcol = wk(2520, 1)
        wproj = wk(2528, 256)
        w1n = wk(2784, P)
        w2b = wk(2912, P)
        par8 = wk(3040, 8)
        tin = wk(3048, 2)

        bk = [ctx.enter_context(nc.psum_tensor(f"bk{i}", [P, 512], F32)) for i in range(8)]

        setup = ExitStack()
        s_ld = setup.enter_context(nc.semaphore("s_setup_load"))
        s_pe = setup.enter_context(nc.semaphore("s_setup_pe"))
        s_ve = setup.enter_context(nc.semaphore("s_setup_dve"))
        s_go = setup.enter_context(nc.semaphore("s_setup_next"))
        s_wr = setup.enter_context(nc.semaphore("s_setup_store"))
        s_link = setup.enter_context(nc.semaphore("s_setup_link"))
        s_sq = setup.enter_context(nc.semaphore("s_setup_sqrt"))
        qk = [("q", 0), ("k", 64)]

        def put(dst, src):
            return lambda sp: sp.dma_start(dst, src, allow_slow_non_contiguous=True).then_inc(s_ld, 16)

        conv_flat = lambda a: a.rearrange("o i a b -> (o i) (a b)")
        W5 = w5.rearrange("p (a b) -> p a b", b=5)
        table_loads = [put(ctab[:, :], table[:, 0:setup_from]), put(stab, table[:, setup_from:])]
        small_loads = [
            put(w1n[0:8, :], w["w1"].rearrange("o i a b -> o (i a b)")),
            put(w2b[0:8, :], w["w2"].rearrange("o i a b -> (i a b) o")), put(w2b[8:9, :], w["b2"].unsqueeze(0)),
            *(put(par8[0:8, n:n + 1], w[name].unsqueeze(1)) for n, name in enumerate(("b1", "bn_gamma", "bn_beta", "bn_mean", "bn_var"))),
            put(tin[0:8, 0:1], w["temp_f"].rearrange("h a b -> h (a b)")), put(tin[0:8, 1:2], w["temp_s"].rearrange("h a b -> h (a b)")),
            put(v1[:, :], w["v1_w"].rearrange("o i a b -> o (i a b)")),
        ]
        flats = [w["projf_w"].rearrange("o i a b -> o (i a b)"), w["projs_w"].rearrange("o i a b -> o (i a b)")]
        WBt = WB.rearrange("p (t o) -> p t o", o=P)
        WAfull = UU.rearrange("p (t o) -> p t o", o=P)
        WVt = WV.rearrange("p (t m) -> p t m", m=P)
        WCt = WC.rearrange("p (t m) -> p t m", m=P)

        block = setup.enter_context(nc.Block())
        loads_done, pe_done, ve_done, go = [0], [0], [0], [0]

        plan = []
        plan.append(("first", table_loads + small_loads))
        for n in range(2):
            plan.append((f"proj{n}", [put(wproj, flats[n])]))
        for nm, off in qk:
            for size in (3, 5):
                ld = [put(wq, w[nm + "1_w"].rearrange("o i a b -> o (i a b)")), put(bcol, w[nm + "1_b"].unsqueeze(1))]
                if size == 5:
                    ld.append(put(w5, conv_flat(w[nm + "5_w"])))
                else:
                    ld += [put(W5[:, 1 + a, 1:4], w[nm + "3_w"].rearrange("o i a b -> (o i) a b")[:, a, :]) for a in range(3)]
                plan.append((f"qk {off} {size}", ld))
        for n, nm in enumerate("vc"):
            ld = [put(w2[64:128, :, :], w[nm + "5_w"].rearrange("o i a b -> o i (a b)"))]
            ld += [put(w2[0:64, i, :].rearrange("p (a b) -> p a b", b=5)[:, 1 + a, 1:4], w[nm + "3_w"][:, i, a, :]) for i in range(2) for a in range(3)]
            if n == 0:
                ld.append(put(bcol, w["v1_b"].unsqueeze(1)))
            plan.append((f"vc {n}", ld))
        ld_at, total = [], 0
        for _, ld in plan:
            total += len(ld)
            ld_at.append(total * 16)
        NSTEP = len(plan)

        @block.sync
        def _(sp):
            for n, (_, loads) in enumerate(plan):
                sp.wait_ge(s_go, n + 1)
                for ld in loads:
                    ld(sp)
            sp.wait_ge(s_go, NSTEP + 2)
            for n, dst in enumerate((MM, UU, WV, WC)):
                sp.dma_start(wts[:, n * TAPS:(n + 1) * TAPS], dst).then_inc(s_wr, 16)
            sp.wait_ge(s_wr, 64)

        @block.tensor
        def _(pe):
            c = [0]

            def after(n):
                pe.wait_ge(s_ve, n)

            ve = iter(range(1, 1000))
            for n, (name, _) in enumerate(plan):
                pe.wait_ge(s_ld, ld_at[n])
                if name == "first":
                    after(next(ve))
                    nc.tensor.matmul(bk[0][0:UG * JG, 0:2], k["rep8"], par8[0:8, 6:8], start=True, stop=True)
                    nc.tensor.matmul(bk[1][:, 0:2], k["heads"], tin[0:8, :], start=True, stop=True)
                    nc.tensor.transpose(bk[2][:, 0:8], w1n[0:8, :], k["eye"][0:8, 0:8])
                    for u in range(UG):
                        m = nc.tensor.matmul(bk[3 + u // 4][0:UG * JG + 1, (u % 4) * P:(u % 4 + 1) * P], ks["spread"].rearrange("p (u m) -> p u m", u=UG)[:, u, :], w2b[0:9, :], start=True, stop=True)
                    m.then_inc(s_pe, 1)
                elif name.startswith("proj"):
                    for i in range(2):
                        m = nc.tensor.transpose(bk[i][:, 0:P], wproj[:, i * P:(i + 1) * P], k["eye"])
                    m.then_inc(s_pe, 1)
                elif name.startswith("qk"):
                    after(next(ve))
                    for t in range(0, T5, 8):
                        e = min(T5, t + 8)
                        nc.tensor.matmul(bk[t // 8][:, 0:(e - t) * 64], wq, sparse[:, t:e, :], start=True, stop=True)
                    for t in range(T5):
                        m = nc.tensor.matmul(bk[4][0:T5, 0:64], btap[:, t, :], sparse[:, t, :], start=(t == 0), stop=(t == T5 - 1))
                    m.then_inc(s_pe, 1)
                if name != "" and not name.startswith("vc"):
                    after(next(ve))
            after(next(ve))
            nc.tensor.matmul(bk[0][0:1, 0:P], small[:, 40:41], k["eye"], start=True, stop=True).then_inc(s_pe, 1)
            after(next(ve))
            nc.tensor.matmul(bk[1][:, 0:1], k["ones"][0:1, :], small[0:1, 42:43], start=True, stop=True).then_inc(s_pe, 1)

        @block.vector
        def _(dve):
            done = [0]

            def did(op):
                done[0] += 1
                op.then_inc(s_ve, 1)

            s_ch = [0]

            def link(op):
                s_ch[0] += 1
                op.then_inc(s_link, 1)
                dve.wait_ge(s_link, s_ch[0])

            link(nc.vector.memset(w5, 0.0))
            nc.vector.memset(w2, 0.0).then_inc(s_go, 1)
            npe = iter(range(1, 1000))
            for n, (name, _) in enumerate(plan):
                dve.wait_ge(s_ld, ld_at[n])
                if name == "first":
                    g = lambda i: par8[0:8, i:i + 1]
                    link(nc.vector.tensor_scalar(g(5), g(4), 1e-5, None, ALU.add))
                    dve.wait_ge(s_sq, 1)
                    link(nc.vector.reciprocal(g(5), g(5)))
                    link(nc.vector.tensor_tensor(g(6), g(1), g(5), ALU.mult))
                    link(nc.vector.tensor_tensor(g(7), g(0), g(3), ALU.subtract))
                    link(nc.vector.tensor_tensor(g(7), g(7), g(6), ALU.mult))
                    did(nc.vector.tensor_tensor(g(7), g(7), g(2), ALU.add))
                    dve.wait_ge(s_pe, next(npe))
                    nc.vector.tensor_copy(gate_sb[:, :], bk[0][0:UG * JG, 0:2])
                    nc.vector.tensor_copy(temps[:, :], bk[1][:, 0:2])
                    nc.vector.tensor_copy(w1t[:, :], bk[2][:, 0:8])
                    for i in range(4):
                        m = min(4, UG - 4 * i)
                        link(nc.vector.tensor_copy(gate_w[:, 4 * i:4 * i + m, :], bk[3 + i][0:UG * JG + 1, 0:m * P]))
                    link(nc.vector.memset(relu_r[:, :, :], 1.0))
                    did(nc.vector.memset(B8[:, :, :], 0.0))
                    nc.vector.memset(norms[:, 0, 0:1], 0.0).then_inc(s_go, 1)
                elif name.startswith("proj"):
                    dve.wait_ge(s_pe, next(npe))
                    s = int(name[4:])
                    link(nc.vector.tensor_copy(pt[:, 2 * s, :], bk[0][:, 0:P]))
                    did(nc.vector.tensor_copy(pt[:, 2 * s + 1, :], bk[1][:, 0:P]))
                    nc.vector.memset(norms[:, 0, 1:2], 0.0).then_inc(s_go, 1)
                elif name.startswith("qk"):
                    _, off, size = name.split()
                    off = int(off)
                    link(nc.vector.tensor_tensor(btap, ks["tap"].rearrange("p (t s) -> p t s", s=T5), bcol.unsqueeze(1).broadcast_to([P, T5, T5]), ALU.mult))
                    did(nc.vector.tensor_tensor(sparse, ks["mpair"].unsqueeze(1).broadcast_to([P, T5, 64]), w5.unsqueeze(2).broadcast_to([P, T5, 64]), ALU.mult))
                    dve.wait_ge(s_pe, next(npe))
                    dst = WBt if size == "5" else WAfull
                    for i in range(4):
                        m = min(8, T5 - 8 * i)
                        link(nc.vector.tensor_copy(dst[:, 8 * i:8 * i + m, off:off + 64], bk[i][:, 0:m * 64].rearrange("p (t o) -> p t o", o=64)))
                    did(nc.vector.tensor_copy(bias_ab[:, int(size == "5"), off:off + 64], bk[4][0:T5, 0:64]))
                    dve.wait_ge(s_ve, done[0])
                    nc.vector.memset(w5, 0.0).then_inc(s_go, 1)
                else:
                    s = int(name[3:])
                    for i in range(2):
                        dst = (WVt, WCt)[s].rearrange("p t (g i) -> p t g i", i=2)[:, :, :, i]
                        link(nc.vector.tensor_tensor(dst, ks["mgroup"].unsqueeze(1).broadcast_to([P, T5, 64]), w2[:, i, :].unsqueeze(2).broadcast_to([P, T5, 64]), ALU.mult))
                    if s == 0:
                        link(nc.vector.tensor_tensor(vtap[:, :, :], ks["tap"].rearrange("p (t s) -> p t s", s=T5), bcol.unsqueeze(1).broadcast_to([P, T5, T5]), ALU.mult))
                    nc.vector.memset(w2, 0.0).then_inc(s_go, 1)
            for i, W in enumerate((UU, WB)):
                link(nc.vector.reduce_max(small[:, 40 + i:41 + i], W, AX.X, apply_absolute_value=True))
            did(nc.vector.tensor_tensor(small[:, 40:41], small[:, 40:41], small[:, 41:42], ALU.max))
            dve.wait_ge(s_pe, next(npe))
            did(nc.vector.reduce_max(small[0:1, 42:43], bk[0][0:1, 0:P], AX.X))
            dve.wait_ge(s_pe, next(npe))
            link(nc.vector.tensor_scalar(small[:, 43:44], bk[1][:, 0:1], 1e-12, None, ALU.max))
            link(nc.vector.reciprocal(small[:, 44:45], small[:, 43:44]))
            link(nc.vector.tensor_scalar(small[:, 45:46], small[:, 44:45], WMAX, None, ALU.mult))
            link(nc.vector.tensor_scalar(small[:, 46:47], small[:, 45:46], XSCALE, None, ALU.mult))
            link(nc.vector.tensor_scalar(floor[:, :], small[:, 46:47], 1e-12, None, ALU.mult))
            for W, to in ((UU, MM), (WB, UU)):
                to = halves(to, T5)
                W = W.rearrange("p (t o) -> p t o", o=P)
                link(nc.vector.tensor_scalar(to[:, 0], W, small[:, 45:46], None, ALU.mult))
                link(nc.vector.scalar_tensor_tensor(to[:, 1], W, small[:, 45:46], to[:, 0], ALU.mult, ALU.subtract))
            link(nc.vector.tensor_scalar(bias_ab[:, :, :], bias_ab[:, :, :], small[0:T5, 46:47], None, ALU.mult))
            nc.vector.memset(norms[:, 0, 2:3], 0.0).then_inc(s_go, 1)

        @block.scalar
        def _(act):
            act.wait_ge(s_ld, ld_at[0])
            act.wait_ge(s_link, 2)
            nc.scalar.activation(par8[0:8, 5:6], par8[0:8, 5:6], ACT.Sqrt).then_inc(s_sq, 1)

        setup.close()
        TAPAT = [(t // 5, t % 5) for t in range(T5)]
        NK = 32
        sxp = [sem(f"s_x_rows_{i}") for i in range(4)]
        sxh = [sem(f"s_columns_{i}") for i in range(2)]
        syc = [sem(f"s_y_chunk_{i}") for i in range(2)]
        sxc = [sem(f"s_x_chunk_{i}") for i in range(2)]
        s_yst = [sem(f"s_y_stored_{i}") for i in range(2)]
        s_x1st = [sem(f"s_x1_stored_{i}") for i in range(2)]
        s_wl = sem("s_qk_kernels_loaded")
        s_vl = sem("s_v_kernels_loaded")
        s_gst = sem("s_gn_stored")
        LINKS = 115
        v = count("s_dve_link", LINKS)
        a = count("s_act_small", 7)
        m_ = count("s_pe_small", 12)
        s_xn = count("s_x_normalised", 4)
        s_xhn = count("s_columns_normalised", 8)
        s_s1 = count("s_stage1", NK)
        s_ab = count("s_stage1_copied", NK)
        s_s2 = count("s_stage2", NK)
        s_xr = count("s_real_copied", NK)
        s_xi = count("s_imag_copied", NK)
        s_gram = count("s_gram", 1)
        s_t8 = count("s_hidden", 2)
        s_t8c = count("s_hidden_copied", 2)
        s_h1 = count("s_hidden_stage1", 2)
        s_h1c = count("s_hidden_stage1_copied", 2)
        s_h2 = count("s_hidden_stage2", NUG)
        s_rel = count("s_relu", NUG)
        s_gl = count("s_gate_logits", NUG)
        s_sig = count("s_sigmoid", 2 * 4 * NUG // 2)
        s_gx = count("s_gated", 2 * NUG)
        s_i1 = count("s_inverse1", 2 * NK)
        s_z = count("s_inverse1_copied", 2 * NK)
        s_i2 = count("s_inverse2", NK)
        s_abs = count("s_abs", NK)
        s_ca = count("s_conv3", NK)
        s_cb = count("s_conv5", NK)
        s_ae = count("s_conv3_copied", 2 * NK)
        s_be = count("s_conv5_copied", 2 * NK)
        s_ta = count("s_transposed3", NK)
        s_tb = count("s_transposed5", NK)
        s_tae = count("s_transposed3_copied", NK)
        s_tbe = count("s_transposed5_copied", NK)
        s_ga = count("s_gram3", NK)
        s_gb = count("s_gram5", NK)
        s_u = count("s_u_taps", 7)
        s_uc = count("s_u_copied", 7)
        s_m = count("s_m_taps", 7)
        s_mc = count("s_m_copied", 7)
        s_bv = count("s_v_bias", 1)
        s_bvc = count("s_v_bias_copied", 1)
        s_row = count("s_rows_taken", NK)
        s_tr = count("s_rows_turned", NK)
        s_trc = count("s_rows_turned_copied", NK)
        s_sh = count("s_rows_shifted", NK)
        s_shr = count("s_shifted_real_copied", NK)
        s_shi = count("s_shifted_imag_copied", NK)
        s_o = count("s_heads_mixed", NK)
        s_os = count("s_heads_squared", 2 * NK)
        s_oa = count("s_heads_added", NK)
        s_of = count("s_heads_root", NK)
        s_hi = count("s_pixels_high", NK)
        s_lo = count("s_pixels_low", NK)
        s_px = count("s_pixels_split", NK)
        s_ms = count("s_m_split", 1)
        s_kl = [sem(f"s_shift_loaded_{i}") for i in range(2)]
        s_ofst = [sem(f"s_heads_stored_{i}") for i in range(2)]
        sof = [sem(f"s_heads_chunk_{i}") for i in range(2)]
        s_vc = count("s_conv_out", NK)
        s_x1 = count("s_x1_ready", NK)
        s_bn = count("s_x1_stats", NK)
        s_edge = sem("s_edges_cleared")
        VL = {}
        block = ctx.enter_context(nc.Block())

        def credit(eng, *cs):
            for c in cs:
                eng.sem_inc(c.sem, c.per)

        rows4 = lambda h: bass.ds(h, 4)

        def window(kk, dh, dw):
            return xpad[:, bass.ds(kk * 4 + dh, 4), dw:dw + P]

        def window16(kk, half, dh, dw):
            return pixels16[:, bass.ds(kk * 4 + dh, 4), half, dw:dw + P]

        def chunk_loop(eng, body):
            body(0, 0, 0)
            with eng.Fori(0, NK // 2 - 1) as i:
                body(i * 2 + 1, 1, 2)
                body(i * 2 + 2, 0, 2)
            body(NK - 1, 1, 4)

        col = lambda i, n=1: small[:, i:i + n]
        xview = lambda b: x[bass.ds(b, 1), :, :, :]

        @block.vector
        def _(dve):
            credit(dve, v, s_shi, s_xhn, s_xi, s_h1c, s_gx, s_tae, s_tbe, s_lo, s_px, s_ms, s_bvc, s_oa, s_x1, s_bn)
            V = nc.vector
            n0 = [0]
            for part in (xpad[:, 0:2, :], xpad[:, WP - 2:WP, :], xpad[:, :, 0:2], xpad[:, :, WP - 2:WP]):
                V.memset(part, 0.0).then_inc(s_edge, 1)
                n0[0] += 1
                dve.wait_ge(s_edge, n0[0])
            with dve.Fori(0, B) as b:
                n, pn, an = [0], [0], [0]

                def link(op):
                    n[0] += 1
                    op.then_inc(v.sem, 1)
                    dve.wait_ge(v.sem, v.at(b, n[0]))

                def mark(name):
                    VL[name] = n[0]

                def pe_done():
                    pn[0] += 1
                    dve.wait_ge(m_.sem, m_.at(b, pn[0]))

                def act_done():
                    an[0] += 1
                    dve.wait_ge(a.sem, a.at(b, an[0]))

                def group_norm(name, st):
                    V.memset(col(20), 0.0)
                    link(V.bn_aggr(col(0, 2), st))
                    mark(name + "_mean")
                    pe_done()
                    link(V.tensor_tensor(col(2), col(0), bk[7][:, 0:1], ALU.subtract))
                    link(V.tensor_tensor(col(3), col(2), col(2), ALU.mult))
                    link(V.tensor_tensor(col(3), col(3), col(1), ALU.add))
                    link(V.tensor_copy(col(7), bk[7][:, 0:1]))
                    mark(name + "_var")
                    pe_done()
                    link(V.tensor_scalar(col(6), bk[7][:, 1:2], 1e-5, None, ALU.add))
                    mark(name + "_root")
                    act_done()
                    link(V.reciprocal(col(4), col(6)))
                    link(V.tensor_tensor(col(5), col(7), col(4), ALU.mult))
                    link(V.tensor_scalar(col(5), col(5), -1.0, None, ALU.mult))
                    mark(name + "_done")

                dve.wait_ge(s_gst, b * 16 + 16)
                for i in range(4):
                    dve.wait_ge(sxp[i], b * 16 + 16)
                    for r in range(8):
                        h = 2 + 32 * i + 4 * r
                        V.bn_stats(stats[:, 8 * i + r, :], xpad[:, h:h + 4, 2:2 + P]).then_inc(v.sem, 1)
                        n[0] += 1
                dve.wait_ge(v.sem, v.at(b, n[0]))
                group_norm("gn", stats[:, :, :])
                link(V.tensor_scalar(diag[:, 0:P], k["eye"], col(4), None, ALU.mult))
                link(V.tensor_scalar(diag[:, P:], k["eye"], col(5), None, ALU.mult))
                mark("gn_rows")
                pe_done()
                link(V.tensor_copy(rows, bk[7][:, 0:256]))

                def xi_copy(t):
                    dve.wait_ge(s_s2.sem, s_s2.at(b, t + 1))
                    V.tensor_copy(XI[:, 4 * t:4 * t + 4, :], bk[4 + t % 2][:, 0:4 * HALF].rearrange("p (c u) -> p c u", u=HALF)).then_inc(s_xi.sem, 1)

                def columns(i):
                    dve.wait_ge(sxh[i % 2], b * 128 + 32 * (i // 2) + 32)
                    t_ = xh[:, i % 2, :, :]
                    link(V.tensor_tensor(t_, t_, rows[:, 16 * i:16 * i + 16].unsqueeze(2).broadcast_to([P, 16, P]), ALU.mult))
                    V.tensor_tensor(t_, t_, rows[:, P + 16 * i:P + 16 * i + 16].unsqueeze(2).broadcast_to([P, 16, P]), ALU.add).then_inc(s_xhn.sem, 1)

                columns(0)
                columns(1)
                for i in range(8):
                    for t in range(4 * i, 4 * i + 4):
                        xi_copy(t)
                    if i + 2 < 8:
                        columns(i + 2)

                def softmax(name, width, mask):
                    L = sq[1][:, 0:width]
                    link(V.tensor_tensor(L, L, mask, ALU.mult))
                    link(V.tensor_scalar(sq[2][:, 0:width], mask, 1e30, -1e30, ALU.mult, ALU.add))
                    link(V.tensor_tensor(L, L, sq[2][:, 0:width], ALU.add))
                    link(V.reduce_max(col(15), L, AX.X))
                    link(V.tensor_scalar(col(15), col(15), -1.0, None, ALU.mult))
                    mark(name + "_max")
                    act_done()
                    link(V.reciprocal(col(17), col(16)))

                def roots(name, w_, least=1e-12):
                    mark(name + "_root")
                    for _ in range(w_):
                        act_done()
                    link(V.tensor_scalar(col(10, w_), col(10, w_), least, None, ALU.max))
                    link(V.reciprocal(col(12, w_), col(10, w_)))

                for hf in range(2):
                    dve.wait_ge(s_h1.sem, s_h1.at(b, hf + 1))
                    src = bk[2 + hf][:, :].rearrange("p (j u) -> p u j", j=4)
                    link(V.tensor_copy(A8[:, :, 4 * hf:4 * hf + 4], src[:, 0:HALF, :]))
                    V.tensor_copy(B8[:, 1:64, 4 * hf:4 * hf + 4], src[:, HALF:, :]).then_inc(s_h1c.sem, 1)
                dve.wait_ge(s_gram.sem, s_gram.at(b, 1))
                G = bk[6]
                for i in range(2):
                    link(V.tensor_copy(sq[i], G[:, (2 * i + 1) * P:(2 * i + 2) * P]))
                for o, op in ((2, ALU.subtract), (3, ALU.add)):
                    link(V.tensor_tensor(sq[o], G[:, 0:P], sq[0], op))
                    link(V.tensor_tensor(sq[4], G[:, 2 * P:3 * P], sq[1], op))
                    link(V.scalar_tensor_tensor(sq[o], sq[o], 2.0, sq[4], ALU.mult, ALU.add))
                link(V.tensor_tensor(sq[3], sq[3], k["eye"], ALU.mult))
                link(V.reduce_sum(col(8), sq[3], AX.X))
                roots("f", 1)
                link(V.tensor_scalar(diag[:, 0:P], k["eye"], col(12), None, ALU.mult))
                mark("f_rows")
                pe_done()
                link(V.tensor_tensor(col(14), col(12), temps[:, 0:1], ALU.mult))
                link(V.scalar_tensor_tensor(sq[1], sq[2], col(14), bk[7][:, 0:P], ALU.mult, ALU.mult))
                softmax("f", P, k["head"])
                link(V.tensor_scalar(sq[0], sq[0], col(17), None, ALU.mult))
                mark("f_soft")
                pe_done()
                link(V.tensor_copy(mix_t[:, 0, :], bk[7][:, 0:P]))
                link(V.tensor_tensor(mix_t[:, 1, :], bk[7][:, P:2 * P], k["mixi"], ALU.add))
                link(V.tensor_scalar(mix_t[:, 2, :], mix_t[:, 1, :], -1.0, None, ALU.mult))
                mark("f_mix")
                for g in range(NUG):
                    dve.wait_ge(s_sig.sem, s_sig.at(b, 4 * g + 4))
                    for X in (XR, XI):
                        part = X[:, :, g * UG:(g + 1) * UG]
                        V.tensor_tensor(part, part, gates.rearrange("p u c -> p c u"), ALU.mult).then_inc(s_gx.sem, 1)

                def add_squares(kk):
                    dve.wait_ge(s_os.sem, s_os.at(b, 2 * kk + 2))
                    V.tensor_tensor(sq2[0], sq2[0], sq2[1], ALU.add).then_inc(s_oa.sem, 1)

                def body(kk, par, vrow):
                    first = isinstance(kk, int) and kk == 0
                    dve.wait_ge(s_sh.sem, s_sh.at(b, kk + 1))
                    dve.wait_ge(s_o.sem, s_o.at(b, kk))
                    V.tensor_copy(shifted[:, 512:], bk[2][:, :]).then_inc(s_shi.sem, 1)
                    if not first:
                        add_squares(kk - 1)
                    dve.wait_ge(s_t8.sem, s_t8.at(b, 2))
                    dve.wait_ge(s_row.sem, s_row.at(b, kk + 1))
                    dve.wait_ge(s_hi.sem, s_hi.at(b, kk + 1))
                    h4 = high[par].rearrange("p (r w) -> p r w", w=P)
                    V.scalar_tensor_tensor(window16(kk, 1, 2, 2), window(kk, 2, 2), XSCALE, h4, ALU.mult, ALU.subtract).then_inc(s_lo.sem, 1)
                    dve.wait_ge(s_lo.sem, s_lo.at(b, kk + 1))
                    V.tensor_copy(window16(kk, 0, 2, 2), h4).then_inc(s_px.sem, 1)

                chunk_loop(dve, body)
                add_squares(NK - 1)

                def body(kk, par, vrow):
                    first = isinstance(kk, int) and kk == 0
                    if not first:
                        tcopy(kk - 1, 1)
                    tcopy(kk, 0)

                def tcopy(kk, s):
                    ready, done, used = ((s_ta, s_tae, s_ga), (s_tb, s_tbe, s_gb))[s]
                    dve.wait_ge(ready.sem, ready.at(b, kk + 1))
                    dve.wait_ge(used.sem, used.at(b, kk))
                    V.tensor_copy(tt[s], bk[2 + s][:, :].rearrange("p (j o) -> p j o", o=P)).then_inc(done.sem, 1)

                chunk_loop(dve, body)
                tcopy(NK - 1, 1)
                dve.wait_ge(s_gb.sem, s_gb.at(b, NK))
                dve.wait_ge(s_ae.sem, s_ae.at(b, 2 * NK))
                dve.wait_ge(s_be.sem, s_be.at(b, 2 * NK))
                pe_done()
                link(V.reduce_sum(col(8, 2), norms[:, :, :], AX.X))
                roots("s", 2, floor[:, 0:1])
                for s in range(2):
                    link(V.tensor_scalar(sq[4][:, 64 * s:64 * s + 64], k["ones"][:, 0:64], col(12 + s), None, ALU.mult))
                mark("s_rows")
                pe_done()
                link(V.tensor_tensor(col(14), bk[5][:, 0:1], temps[:, 1:2], ALU.mult))
                link(V.tensor_scalar(sq[1][:, 0:64], bk[4][:, 0:64], col(14), None, ALU.mult))
                link(V.tensor_tensor(sq[1][:, 0:64], sq[1][:, 0:64], bk[5][:, 64:P], ALU.mult))
                softmax("s", 64, k["head64"])
                link(V.memset(afull, 0.0))
                for s in range(2):
                    r = slice(64 * s, 64 * s + 64)
                    link(V.tensor_scalar(afull[r, r], sq[0][r, 0:64], small[r, 17:18], None, ALU.mult))
                mark("s_soft")
                pe_done()
                link(V.tensor_copy(ap_, bk[5][:, 0:P]))
                mark("s_mix")
                dve.wait_ge(s_mc.sem, s_mc.at(b, 7))
                link(V.reduce_max(col(21), MM, AX.X, apply_absolute_value=True))
                mark("m_rows")
                pe_done()
                link(V.reduce_max(small[0:1, 22:23], bk[5][0:1, 0:P], AX.X))
                mark("m_max")
                pe_done()
                link(V.tensor_scalar(col(22), bk[5][:, P:P + 1], 1e-12, None, ALU.max))
                link(V.reciprocal(col(23), col(22)))
                link(V.tensor_scalar(col(24), col(23), WMAX, None, ALU.mult))
                link(V.tensor_scalar(col(25), col(24), XSCALE, None, ALU.mult))
                link(V.reciprocal(col(26), col(25)))
                dve.wait_ge(s_m.sem, s_m.at(b, 7))
                dve.wait_ge(s_bv.sem, s_bv.at(b, 1))
                MT_ = MM.rearrange("p (t o) -> p t o", o=P)
                link(V.tensor_scalar(M16[:, 0], MT_, col(24), None, ALU.mult))
                V.scalar_tensor_tensor(M16[:, 1], MT_, col(24), M16[:, 0], ALU.mult, ALU.subtract).then_inc(s_ms.sem, 1)
                link(V.tensor_scalar(pt_scaled, pt[:, 0:2, :], col(25), None, ALU.mult))
                V.tensor_scalar(bias_v[:, :], bk[6][0:T5, 0:P], small[0:T5, 25:26], None, ALU.mult).then_inc(s_bvc.sem, 1)

                def body(kk, par, vrow):
                    dve.wait_ge(s_vc.sem, s_vc.at(b, kk + 1))
                    dve.wait_ge(sxc[par], b * (8 * NK) + (kk - par) * 8 + 16)
                    dve.wait_ge(s_x1st[par], b * (8 * NK) + (kk - par) * 8 + 16)
                    dve.wait_ge(s_bn.sem, s_bn.at(b, kk - 1))
                    V.scalar_tensor_tensor(x1c[par], bk[6 + par][:, :], col(26), xch[par], ALU.mult, ALU.add).then_inc(s_x1.sem, 1)
                    dve.wait_ge(s_x1.sem, s_x1.at(b, kk + 1))
                    V.bn_stats(stats[:, bass.ds(kk, 1), :], x1c[par]).then_inc(s_bn.sem, 1)

                chunk_loop(dve, body)
                dve.wait_ge(s_bn.sem, s_bn.at(b, NK))
                group_norm("gn2", stats[:, :, :])
                assert n[0] == LINKS, n

        @block.sync
        def _(sp):
            with sp.Fori(0, B) as b:
                sp.wait_ge(s_vc.sem, s_vc.at(b, 0))
                sp.wait_ge(s_bn.sem, s_bn.at(b, 0))
                for i in range(4):
                    sp.dma_start(xpad[:, 2 + 32 * i:34 + 32 * i, 2:2 + P], x[bass.ds(b, 1), :, 32 * i:32 * i + 32, :].rearrange("a c h w -> (a c) h w")).then_inc(sxp[i], 16)
                for s in range(2):
                    sp.wait_ge(s_x1st[s], b * (8 * NK) + 16)
                for i in range(8):
                    if i >= 2:
                        sp.wait_ge(s_s1.sem, s_s1.at(b, 4 * (i - 1)))
                    for hf in range(2):
                        c0 = 16 * i + 8 * hf
                        sp.dma_start(xh[:, i % 2, 8 * hf:8 * hf + 8, :], x[bass.ds(b, 1), c0:c0 + 8, :, :].rearrange("a c h w -> h (a c) w")).then_inc(sxh[i % 2], 16)
                for g in range(NK):
                    sp.wait_ge(s_abs.sem, s_abs.at(b, g + 1))
                    sp.dma_start(y_d[bass.ds(b, 1), 4 * g:4 * g + 4, :, :].rearrange("a c h w -> h (a c) w"), Yb[:, g % 2, :, :]).then_inc(s_yst[g % 2], 16)

                def body(kk, par, vrow):
                    sp.wait_ge(s_sh.sem, s_sh.at(b, kk - 1))
                    sp.dma_start(kbuf3[par], shift_d[:, rows4(kk * 4), :]).then_inc(s_kl[par], 16)

                chunk_loop(sp, body)
                sp.wait_ge(s_of.sem, s_of.at(b, NK))
                for i, (c0, c1) in enumerate(((0, cut[1]), (cut[1], HW))):
                    sp.dma_start(of_d[bass.ds(b, 1), :, c0:c1].rearrange("a c n -> (a c) n"), region[:, c0:c1]).then_inc(s_ofst[i], 16)
                sp.wait_ge(s_ofst[0], b * 16 + 16)
                inner = wts[:, 0:TAPS].rearrange("p (s i j o) -> p s i j o", s=2, i=5, j=5)
                inner_to = region[:, 0:9 * P].rearrange("p (s t o) -> p s t o", s=2, t=9)
                for half in range(2):
                    for i in range(3):
                        sp.dma_start(inner_to[:, half, 3 * i:3 * i + 3, :], inner[:, half, 1 + i, 1:4, :]).then_inc(s_wl, 16)
                for n, dst in enumerate((WB, WV, WC)):
                    if n == 1:
                        sp.wait_ge(s_ofst[1], b * 16 + 16)
                    sp.dma_start(dst, wts[:, (n + 1) * TAPS:(n + 2) * TAPS]).then_inc((s_wl, s_vl, s_vl)[n], 16)
                sp.wait_ge(s_yst[0], b * (8 * NK) + 8 * NK)
                sp.wait_ge(s_yst[1], b * (8 * NK) + 8 * NK)

                def body(kk, par, vrow):
                    first = isinstance(kk, int) and kk == 0
                    if not first:
                        store(kk - 1, 1 - par)
                    sp.wait_ge(s_vc.sem, s_vc.at(b, kk - 1))
                    sp.wait_ge(s_x1.sem, s_x1.at(b, kk - 1))
                    sp.dma_start(ych[par], y_d[bass.ds(b, 1), :, rows4(kk * 4), :].rearrange("a c h w -> (a c) (h w)")).then_inc(syc[par], 16)
                    sp.dma_start(of[par], of_d[bass.ds(b, 1), :, bass.ds(kk * 512, 512)].rearrange("a c n -> (a c) n")).then_inc(sof[par], 16)
                    sp.dma_start(xch[par], x[bass.ds(b, 1), :, rows4(kk * 4), :].rearrange("a c h w -> (a c) (h w)")).then_inc(sxc[par], 16)

                def store(kk, par):
                    sp.wait_ge(s_x1.sem, s_x1.at(b, kk + 1))
                    sp.dma_start(x1[bass.ds(b, 1), :, bass.ds(kk * 512, 512)].rearrange("a c n -> (a c) n"), x1c[par]).then_inc(s_x1st[par], 16)

                chunk_loop(sp, body)
                sp.wait_ge(v.sem, v.at(b, LINKS))
                store(NK - 1, 1)
                sp.dma_start(gn2[bass.ds(b, 1), :, :].rearrange("a c n -> (a c) n"), col(4, 2)).then_inc(s_gst, 16)
            sp.wait_ge(s_gst, 16 * B + 16)
            for s in range(2):
                sp.wait_ge(s_x1st[s], B * (8 * NK) + 16)

        @block.tensor
        def _(pe):
            credit(pe, s_tr, s_sh, m_, s_s1, s_s2, s_gram, s_t8, s_h1, s_h2, s_gl, s_i1, s_i2, s_ca, s_cb, s_ta, s_tb, s_ga, s_gb, s_u, s_m, s_bv, s_o, s_vc)
            mm = lambda *args, **kw: nc.tensor.matmul(*args, skip_group_check=True, **kw)

            def conv(o, kernel, taps, kk):
                for n_, t in enumerate(taps):
                    for wh, ph in ((0, 0), (0, 1), (1, 0)):
                        mm(o, kernel[:, wh, n_, :], window16(kk, ph, *TAPAT[t]), start=(n_ == 0 and wh == 0 and ph == 0), stop=False)

            with pe.Fori(0, B) as b:
                n = [0]

                def small_mm(wait, *ops):
                    pe.wait_ge(v.sem, v.at(b, wait))
                    for o, l, r in ops:
                        x_ = mm(o, l, r, start=True, stop=True)
                    n[0] += 1
                    x_.then_inc(m_.sem, 1)

                small_mm(VL["gn_mean"], (bk[7][:, 0:1], k["four"], col(0)))
                small_mm(VL["gn_var"], (bk[7][:, 1:2], k["four"], col(3)))
                small_mm(VL["gn_rows"], (bk[7][:, 0:256], k["ones"], diag))

                def stage1(t):
                    pe.wait_ge(s_xhn.sem, s_xhn.at(b, t // 4 + 1))
                    pe.wait_ge(s_ab.sem, s_ab.at(b, t - 1))
                    for c in range(4):
                        m = mm(bk[t % 2][:, c * P:(c + 1) * P], xh[:, t // 4 % 2, 4 * (t % 4) + c, :], k["fwd"], start=True, stop=True)
                    m.then_inc(s_s1.sem, 1)

                def stage2(t):
                    pe.wait_ge(s_ab.sem, s_ab.at(b, t + 1))
                    pe.wait_ge(s_xr.sem, s_xr.at(b, t - 1))
                    pe.wait_ge(s_xi.sem, s_xi.at(b, t - 1))
                    A, Bm = AB[:, t % 2, :, 0:HALF], AB[:, t % 2, :, HALF:]
                    for o, (ca, cb_) in ((bk[2 + t % 2], (k["cs"][:, 0:P], k["cs"][:, P:])), (bk[4 + t % 2], (k["sc"][:, 0:P], k["cs"][:, 0:P]))):
                        o3 = o[:, 0:4 * HALF].rearrange("p (c u) -> p c u", u=HALF)
                        mm(o3, ca, A, start=True, stop=False)
                        m = mm(o3[:, :, 1:64], cb_, Bm, start=False, stop=True)
                    m.then_inc(s_s2.sem, 1)

                stage1(0)
                for t in range(NK):
                    if t + 1 < NK:
                        stage1(t + 1)
                    stage2(t)
                pe.wait_ge(s_xr.sem, s_xr.at(b, NK))
                pe.wait_ge(s_xi.sem, s_xi.at(b, NK))
                for i, (X, us) in enumerate(((XR, range(1, 64)), (XI, range(1, 64)), (XR, (0, 64)), (XI, (0, 64)))):
                    for u in us:
                        m = mm(bk[6][:, i * P:(i + 1) * P], X[:, :, u], X[:, :, u], start=(u == us[0]), stop=(u == us[-1]))
                m.then_inc(s_gram.sem, 1)
                pe.wait_ge(s_xn.sem, s_xn.at(b, 4))
                for hf in range(2):
                    for c in range(64 * hf, 64 * hf + 64):
                        m = mm(bk[hf][:, (c % 64) * JG:(c % 64 + 1) * JG], xpad[:, 2:2 + P, 2 + c], w1t[:, :], start=True, stop=True)
                    m.then_inc(s_t8.sem, 1)
                for hf in range(2):
                    pe.wait_ge(s_t8c.sem, s_t8c.at(b, 2))
                    for j in range(4 * hf, 4 * hf + 4):
                        m = mm(bk[2 + hf][:, (j % 4) * P:(j % 4 + 1) * P], T8[:, :, j], k["fwd"], start=True, stop=True)
                    m.then_inc(s_h1.sem, 1)
                pe.wait_ge(s_h1c.sem, s_h1c.at(b, 2))
                for g in range(NUG):
                    u0 = g * UG
                    o = bk[g // 4][0:UG * JG, (g % 4) * P:(g % 4 + 1) * P]
                    mm(o, A8[:, u0:u0 + UG, :].rearrange("p u j -> p (u j)"), k["cs"][:, 0:P], start=True, stop=False)
                    mm(o, B8[:, u0:u0 + UG, :].rearrange("p u j -> p (u j)"), k["cs"][:, P:], start=False, stop=True).then_inc(s_h2.sem, 1)
                small_mm(VL["f_rows"], (bk[7][:, 0:P], k["ones"], diag[:, 0:P]))
                pe.wait_ge(v.sem, v.at(b, VL["f_soft"]))
                mm(bk[7][:, 0:P], sq[0], k["mixc"], start=True, stop=True)
                mm(bk[7][:, P:2 * P], sq[0], k["mixs"], start=True, stop=True).then_inc(m_.sem, 1)
                gate_flat = gate_w[:, :, :].rearrange("p u c -> p (u c)")
                for g in range(NUG):
                    pe.wait_ge(s_rel.sem, s_rel.at(b, g + 1))
                    pe.wait_ge(s_sig.sem, s_sig.at(b, 4 * g))
                    for i in range(4):
                        e = min(UG * P, (i + 1) * 512)
                        m = mm(bk[2 + i][:, 0:e - i * 512], relu_r[0:UG * JG + 1, g, :], gate_flat[:, i * 512:e], start=True, stop=True)
                    m.then_inc(s_gl.sem, 1)
                pe.wait_ge(s_gx.sem, s_gx.at(b, 2 * NUG))

                def inverse1(p):
                    pe.wait_ge(s_z.sem, s_z.at(b, p - 1))
                    if p < 2:
                        pe.wait_ge(s_rel.sem, s_rel.at(b, NUG))
                    for c in range(2):
                        o = bk[p % 2][0:HALF, c * 256:(c + 1) * 256]
                        mm(o, XR[:, 2 * p + c, :], k["cs"], start=True, stop=False)
                        m = mm(o, XI[:, 2 * p + c, :], k["sc"], start=False, stop=True)
                    m.then_inc(s_i1.sem, 1)

                def inverse2(t):
                    pe.wait_ge(s_z.sem, s_z.at(b, 2 * t + 2))
                    pe.wait_ge(s_abs.sem, s_abs.at(b, t - 1))
                    mm(bk[2 + t % 2][:, :], k["back"][:, 0:P], Z[0:HALF, t % 2, :, 0:P], start=True, stop=False)
                    mm(bk[2 + t % 2][:, :], k["back"][:, P:], Z[0:HALF, t % 2, :, P:], start=False, stop=True).then_inc(s_i2.sem, 1)

                inverse1(0)
                inverse1(1)
                for t in range(NK):
                    if t + 1 < NK:
                        inverse1(2 * t + 2)
                        inverse1(2 * t + 3)
                    inverse2(t)

                def turn(kk):
                    pe.wait_ge(s_row.sem, s_row.at(b, kk + 1))
                    pe.wait_ge(s_trc.sem, s_trc.at(b, kk))
                    for j in range(4):
                        m = nc.tensor.transpose(bk[0][:, j * P:(j + 1) * P], rowbuf[:, j * P:(j + 1) * P], k["eye"])
                    m.then_inc(s_tr.sem, 1)

                def body(kk, par, vrow):
                    last = isinstance(kk, int) and kk == NK - 1
                    pe.wait_ge(s_trc.sem, s_trc.at(b, kk + 1))
                    pe.wait_ge(s_kl[par], b * (8 * NK) + (kk - par) * 8 + 16)
                    pe.wait_ge(s_shr.sem, s_shr.at(b, kk))
                    pe.wait_ge(s_shi.sem, s_shi.at(b, kk))
                    for j in range(4):
                        for s in range(2):
                            m = mm(bk[1 + s][:, j * P:(j + 1) * P], turned[:, j * P:(j + 1) * P], kbuf3[par][:, j, s * P:(s + 1) * P], start=True, stop=True)
                    m.then_inc(s_sh.sem, 1)
                    if not last:
                        turn(kk + 1)
                    pe.wait_ge(s_shr.sem, s_shr.at(b, kk + 1))
                    pe.wait_ge(s_shi.sem, s_shi.at(b, kk + 1))
                    pe.wait_ge(s_os.sem, s_os.at(b, 2 * kk - 2))
                    o_re, o_im = bk[3 + 2 * par][:, :], bk[4 + 2 * par][:, :]
                    re, im = shifted[:, 0:512], shifted[:, 512:]
                    mm(o_re, mix_t[:, 0, :], re, start=True, stop=False)
                    mm(o_re, mix_t[:, 2, :], im, start=False, stop=True)
                    mm(o_im, mix_t[:, 0, :], im, start=True, stop=False)
                    mm(o_im, mix_t[:, 1, :], re, start=False, stop=True).then_inc(s_o.sem, 1)

                pe.wait_ge(s_abs.sem, s_abs.at(b, NK))
                turn(0)
                chunk_loop(pe, body)
                pe.wait_ge(s_os.sem, s_os.at(b, 2 * NK))
                pe.wait_ge(s_wl, b * 112 + 112)
                pe.wait_ge(s_px.sem, s_px.at(b, NK))
                pe.wait_ge(s_i2.sem, s_i2.at(b, NK))
                pe.wait_ge(s_abs.sem, s_abs.at(b, NK))
                mm(bk[4][:, 0:64], relu_r[:, 0, :], B8[:, 0, :].unsqueeze(1).broadcast_to([P, 8, JG]), start=True, stop=True).then_inc(m_.sem, 1)
                WB16 = halves(WB, T5)

                def gram(kk, s):
                    done, ready = ((s_ga, s_tae), (s_gb, s_tbe))[s]
                    pe.wait_ge(ready.sem, ready.at(b, kk + 1))
                    for j in range(4):
                        m = mm(bk[4][64 * s:64 * s + 64, 0:64], tt[s][:, j, 0:64], tt[s][:, j, 64:P], start=False, stop=True)
                    m.then_inc(done.sem, 1)

                def flip(kk, s):
                    done, copied, read = ((s_ta, s_ae, s_tae), (s_tb, s_be, s_tbe))[s]
                    pe.wait_ge(copied.sem, copied.at(b, 2 * kk + 1))
                    pe.wait_ge(read.sem, read.at(b, kk))
                    for j in range(4):
                        m = nc.tensor.transpose(bk[2 + s][:, j * P:(j + 1) * P], qa[s][:, j * P:(j + 1) * P], k["eye"])
                    m.then_inc(done.sem, 1)

                def body(kk, par, vrow):
                    first = isinstance(kk, int) and kk == 0
                    pe.wait_ge(s_ae.sem, s_ae.at(b, 2 * kk))
                    conv(bk[0][:, :], WA, INNER, kk)
                    mm(bk[0][:, :], bias_ab[:, 0, :], valid[:, vrow:vrow + 4, :], start=False, stop=True).then_inc(s_ca.sem, 1)
                    if not first:
                        flip(kk - 1, 1)
                        gram(kk - 1, 0)
                    pe.wait_ge(s_be.sem, s_be.at(b, 2 * kk))
                    conv(bk[1][:, :], WB16, range(T5), kk)
                    mm(bk[1][:, :], bias_ab[:, 1, :], valid[:, vrow:vrow + 4, :], start=False, stop=True).then_inc(s_cb.sem, 1)
                    if not first:
                        gram(kk - 1, 1)
                    flip(kk, 0)

                chunk_loop(pe, body)
                flip(NK - 1, 1)
                gram(NK - 1, 0)
                gram(NK - 1, 1)
                pe.wait_ge(v.sem, v.at(b, VL["s_rows"]))
                for s in range(2):
                    o = bk[5][64 * s:64 * s + 64, :]
                    mm(o[:, 0:1], k["eye"][:, 0:64], col(12 + s), start=True, stop=True)
                    m = mm(o[:, 64:P], sq[4][:, 64 * s:64 * s + 64], k["shift"], start=True, stop=True)
                m.then_inc(m_.sem, 1)
                small_mm(VL["s_soft"], (bk[5][:, 0:P], afull, pt[:, 2, :]))
                pe.wait_ge(v.sem, v.at(b, VL["s_mix"]))
                pe.wait_ge(s_vl, b * 32 + 32)
                WVt_, WCt_ = (W.rearrange("p (t o) -> p t o", o=P) for W in (WV, WC))
                UT = UU.rearrange("p (t o) -> p t o", o=P)
                for i in range(7):
                    e = min(T5, 4 * i + 4)
                    pe.wait_ge(s_uc.sem, s_uc.at(b, i - 1))
                    for t in range(4 * i, e):
                        m = mm(bk[i % 2][:, (t % 4) * P:(t % 4 + 1) * P], WVt_[:, t, :], ap_, start=True, stop=True)
                    m.then_inc(s_u.sem, 1)
                for i in range(7):
                    e = min(T5, 4 * i + 4)
                    pe.wait_ge(s_uc.sem, s_uc.at(b, i + 1))
                    pe.wait_ge(s_mc.sem, s_mc.at(b, i - 1))
                    mm(bk[2 + i % 2][:, 0:(e - 4 * i) * P], v1[:, :], UU[:, 4 * i * P:e * P], start=True, stop=False)
                    for t in range(4 * i, e):
                        m = mm(bk[2 + i % 2][:, (t % 4) * P:(t % 4 + 1) * P], WCt_[:, t, :], pt[:, 3, :], start=False, stop=True)
                    m.then_inc(s_m.sem, 1)
                for t in range(T5):
                    m = mm(bk[6][0:T5, 0:P], vtap[:, t, :], UT[:, t, :], start=(t == 0), stop=(t == T5 - 1))
                m.then_inc(s_bv.sem, 1)
                small_mm(VL["m_rows"], (bk[5][0:1, 0:P], col(21), k["eye"]))
                small_mm(VL["m_max"], (bk[5][:, P:P + 1], k["ones"][0:1, :], small[0:1, 22:23]))
                pe.wait_ge(s_bvc.sem, s_bvc.at(b, 1))
                pe.wait_ge(s_ms.sem, s_ms.at(b, 1))

                def body(kk, par, vrow):
                    o = bk[6 + par][:, :]
                    pe.wait_ge(s_x1.sem, s_x1.at(b, kk - 1))
                    conv(o, M16, range(T5), kk)
                    mm(o, bias_v[:, :], valid[:, vrow:vrow + 4, :], start=False, stop=False)
                    pe.wait_ge(syc[par], b * (8 * NK) + (kk - par) * 8 + 16)
                    mm(o, pt_scaled[:, 1, :], ych[par], start=False, stop=False)
                    pe.wait_ge(sof[par], b * (8 * NK) + (kk - par) * 8 + 16)
                    mm(o, pt_scaled[:, 0, :], of[par], start=False, stop=True).then_inc(s_vc.sem, 1)

                chunk_loop(pe, body)
                small_mm(VL["gn2_mean"], (bk[7][:, 0:1], k["four"], col(0)))
                small_mm(VL["gn2_var"], (bk[7][:, 1:2], k["four"], col(3)))
                assert n[0] + 3 == m_.per

        @block.scalar
        def _(act):
            credit(act, a, s_row, s_hi, s_trc, s_shr, s_xn, s_ab, s_xr, s_t8c, s_rel, s_sig, s_z, s_abs, s_ae, s_be, s_uc, s_mc, s_os, s_of)
            cp = lambda o, i, f=ACT.Copy, **kw: nc.scalar.activation(o, i, f, **kw)
            with act.Fori(0, B) as b:
                n = [0]

                def small_act(wait, o, i, f, **kw):
                    act.wait_ge(v.sem, v.at(b, wait))
                    n[0] += 1
                    cp(o, i, f, **kw).then_inc(a.sem, 1)

                small_act(VL["gn_root"], col(6), col(6), ACT.Sqrt)
                act.wait_ge(v.sem, v.at(b, VL["gn_done"]))
                def normalise(i):
                    part = xpad[:, 2 + 32 * i:34 + 32 * i, 2:2 + P]
                    cp(part, part, ACT.Identity, bias=col(5), scale=col(4)).then_inc(s_xn.sem, 1)

                for t in range(NK):
                    act.wait_ge(s_s1.sem, s_s1.at(b, t + 1))
                    act.wait_ge(s_s2.sem, s_s2.at(b, t - 1))
                    cp(AB[:, t % 2, :, :].rearrange("p c u -> p (c u)"), bk[t % 2][:, :]).then_inc(s_ab.sem, 1)
                    if t > 0:
                        act.wait_ge(s_s2.sem, s_s2.at(b, t))
                        cp(XR[:, 4 * t - 4:4 * t, :], bk[2 + (t - 1) % 2][:, 0:4 * HALF].rearrange("p (c u) -> p c u", u=HALF)).then_inc(s_xr.sem, 1)
                    if t % 8 == 4:
                        normalise(t // 8)
                act.wait_ge(s_s2.sem, s_s2.at(b, NK))
                cp(XR[:, P - 4:P, :], bk[2 + (NK - 1) % 2][:, 0:4 * HALF].rearrange("p (c u) -> p c u", u=HALF)).then_inc(s_xr.sem, 1)
                for hf in range(2):
                    act.wait_ge(s_t8.sem, s_t8.at(b, hf + 1))
                    cp(T8[:, 64 * hf:64 * hf + 64, :], bk[hf][:, :].rearrange("p (w j) -> p w j", j=JG)).then_inc(s_t8c.sem, 1)
                for g in range(NUG):
                    act.wait_ge(s_h2.sem, s_h2.at(b, min(NUG, 4 * (g // 4) + 4)))
                    cp(relu_r[0:UG * JG, g, :], bk[g // 4][0:UG * JG, (g % 4) * P:(g % 4 + 1) * P], ACT.Relu, bias=gate_sb[:, 1:2], scale=gate_sb[:, 0:1]).then_inc(s_rel.sem, 1)
                small_act(VL["f_root"], col(10), col(8), ACT.Sqrt)
                small_act(VL["f_max"], sq[0], sq[1], ACT.Exp, bias=col(15), accum_out=col(16))
                for g in range(NUG):
                    act.wait_ge(s_gl.sem, s_gl.at(b, g + 1))
                    act.wait_ge(s_gx.sem, s_gx.at(b, 2 * g))
                    for i in range(4):
                        e = min(UG, 4 * i + 4)
                        cp(gates[:, 4 * i:e, :], bk[2 + i][:, 0:(e - 4 * i) * P].rearrange("p (u c) -> p u c", c=P), ACT.Sigmoid).then_inc(s_sig.sem, 1)

                def zcopy(p):
                    act.wait_ge(s_i1.sem, s_i1.at(b, p + 1))
                    act.wait_ge(s_i2.sem, s_i2.at(b, p // 2 - 1))
                    cp(Z[0:HALF, p // 2 % 2, 2 * (p % 2):2 * (p % 2) + 2, :], bk[p % 2][0:HALF, :].rearrange("p (c n) -> p c n", c=2)).then_inc(s_z.sem, 1)

                for t in range(NK + 1):
                    if t < NK:
                        zcopy(2 * t)
                        zcopy(2 * t + 1)
                    if t > 0:
                        g = t - 1
                        act.wait_ge(s_i2.sem, s_i2.at(b, g + 1))
                        if g >= 2:
                            act.wait_ge(s_yst[g % 2], b * (8 * NK) + 16 * (g // 2))
                        cp(Yb[:, g % 2, :, :], bk[2 + g % 2][:, :].rearrange("p (c w) -> p c w", c=4), ACT.Abs).then_inc(s_abs.sem, 1)

                def take_rows(kk):
                    act.wait_ge(s_tr.sem, s_tr.at(b, kk))
                    cp(rowbuf.rearrange("p (j w) -> p j w", j=4), window(kk, 2, 2)).then_inc(s_row.sem, 1)

                act.wait_ge(s_i2.sem, s_i2.at(b, NK))
                act.wait_ge(s_gx.sem, s_gx.at(b, 2 * NUG))
                act.wait_ge(s_xn.sem, s_xn.at(b, 4))

                def turned_rows(kk):
                    act.wait_ge(s_tr.sem, s_tr.at(b, kk + 1))
                    act.wait_ge(s_sh.sem, s_sh.at(b, kk))
                    cp(turned, bk[0][:, :]).then_inc(s_trc.sem, 1)

                def squares(kk, par):
                    act.wait_ge(s_o.sem, s_o.at(b, kk + 1))
                    act.wait_ge(s_of.sem, s_of.at(b, kk))
                    act.wait_ge(s_oa.sem, s_oa.at(b, kk))
                    for s in range(2):
                        cp(sq2[s], bk[3 + 2 * par + s][:, :], ACT.Square).then_inc(s_os.sem, 1)

                def root(kk):
                    act.wait_ge(s_oa.sem, s_oa.at(b, kk + 1))
                    cp(OF[:, :, bass.ds(kk * 4, 4)], sq2[0].rearrange("p (j a) -> p a j", j=4), ACT.Sqrt).then_inc(s_of.sem, 1)

                def body(kk, par, vrow):
                    first, last = (isinstance(kk, int) and kk == i for i in (0, NK - 1))
                    if not last:
                        take_rows(kk + 1)
                    act.wait_ge(s_sh.sem, s_sh.at(b, kk + 1))
                    act.wait_ge(s_o.sem, s_o.at(b, kk))
                    cp(shifted[:, 0:512], bk[1][:, :]).then_inc(s_shr.sem, 1)
                    if not last:
                        turned_rows(kk + 1)
                    act.wait_ge(s_px.sem, s_px.at(b, kk - 1))
                    if not first:
                        squares(kk - 1, 1 - par)
                    cp(high[par].rearrange("p (r w) -> p r w", w=P), window(kk, 2, 2), scale=XSCALE).then_inc(s_hi.sem, 1)
                    if not first:
                        root(kk - 1)

                take_rows(0)
                turned_rows(0)
                chunk_loop(act, body)
                squares(NK - 1, 1)
                root(NK - 1)

                def body(kk, par, vrow):
                    for s, (ready, done, read) in enumerate(((s_ca, s_ae, s_ta), (s_cb, s_be, s_tb))):
                        act.wait_ge(ready.sem, ready.at(b, kk + 1))
                        act.wait_ge(read.sem, read.at(b, kk))
                        cp(qa[s], bk[s][:, :]).then_inc(done.sem, 1)
                        act.wait_ge(done.sem, done.at(b, 2 * kk))
                        cp(sqa[s], bk[s][:, :], ACT.Square, accum_out=norms[:, s, bass.ds(kk, 1)]).then_inc(done.sem, 1)

                act.wait_ge(s_yst[0], b * (8 * NK) + 8 * NK)
                act.wait_ge(s_yst[1], b * (8 * NK) + 8 * NK)
                chunk_loop(act, body)
                for s in range(2):
                    small_act(VL["s_root"], col(10 + s), col(8 + s), ACT.Sqrt)
                small_act(VL["s_max"], sq[0][:, 0:64], sq[1][:, 0:64], ACT.Exp, bias=col(15), accum_out=col(16))
                for i in range(7):
                    e = min(T5, 4 * i + 4)
                    act.wait_ge(s_u.sem, s_u.at(b, i + 1))
                    cp(UU[:, 4 * i * P:e * P], bk[i % 2][:, 0:(e - 4 * i) * P]).then_inc(s_uc.sem, 1)
                for i in range(7):
                    e = min(T5, 4 * i + 4)
                    act.wait_ge(s_m.sem, s_m.at(b, i + 1))
                    cp(MM[:, 4 * i * P:e * P], bk[2 + i % 2][:, 0:(e - 4 * i) * P]).then_inc(s_mc.sem, 1)

                small_act(VL["gn2_root"], col(6), col(6), ACT.Sqrt)
                assert n[0] == a.per

        @block.gpsimd
        def _(pool):
            for s in s_x1st:
                pool.sem_inc(s, 16)
            pool.sem_inc(s_gst, 16)


class Step(NamedTuple):
    tail: Any
    core: Any
    front: Any
    par: int
    front_image: Any
    front_at: Any
    front_pair: Any
    tail_image: Any
    tail_at: Any
    fresh_front: bool = False
    fresh_core: bool = False


class Counter:

    def __init__(self, sem, per, ahead=1):
        self.sem, self.per, self.ahead = sem, per, ahead

    def at(self, chunk, n):
        return chunk * self.per + self.ahead * self.per + n


def layer1(nc, x1, gn2, W_in, conv_w, conv_b, W_xproj, W_dt, b_dt, A_log, D_param, W_out, out, B):
    CH = 512
    NCH = HW // CH
    N = 16
    R = 8
    G = 4
    NG = N // G
    IP = 4
    K4 = 4
    ctx = ExitStack()
    with ctx:
        sb = lambda name, shape, dt=F32: ctx.enter_context(nc.sbuf_tensor(name, shape, dt))
        pb = lambda name, shape: ctx.enter_context(nc.psum_tensor(name, shape, F32))
        sem = lambda name: ctx.enter_context(nc.semaphore(name))

        w_in = sb("w_in", [P, 4 * P])
        w_conv = sb("w_conv", [P, 2, K4])
        v_convb = sb("v_convb", [P, 2])
        w_bc = sb("w_bc", [P, 2, 3 * 2 * N])
        w_xdt = sb("w_xdt", [P, 2, R])
        w_dt = sb("w_dt", [R, 2 * P])
        v_bdt = sb("v_bdt", [P, 2])
        v_alog = sb("v_alog", [P, 2, N])
        v_aexp = sb("v_aexp", [P, 2, N])
        v_a = sb("v_a", [P, 2, N])
        v_d = sb("v_d", [P, 2])
        w_out = sb("w_out", [P, 2, P])
        ident = sb("ident", [P, P])
        pick = sb("pick", [96, 2 * N, P], BF16)
        gnb = sb("gnb", [P, 2])
        mid = sb("mid", [96, CH], BF16)
        xin = sb("xin", [P, 2, CH])
        xn = sb("xn", [P, CH])
        xs = sb("xs", [P, 2, K4 - 1 + CH])
        conv = sb("conv", [P, 2, CH])
        silu_z = sb("silu_z", [P, 2, 2, CH])
        xc = sb("xc", [P, 2, 2, CH])
        delta = sb("delta", [P, 2, 2, CH])
        du = sb("du", [P, 2, 2, CH])
        parts = sb("parts", [96, 2, CH], BF16)
        rest = sb("rest", [96, CH])
        dt8 = sb("dt8", [R, CH])
        lin = conv
        soft = sb("soft", [P, 2, CH])
        da = sb("da", [P, 4, NG, CH + 1])
        hid = sb("hid", [P, 4, NG, CH + 1])
        carry = sb("carry", [P, 2, N])
        cs = sb("cs", [P, 2, NG, CH])
        y = sb("y", [P, 2, CH])
        img = sb("img", [P, P, P])
        img_flat = img[:, :, :].rearrange("p i j -> p (i j)")

        bb = pb("bb", [P, 2, CH])
        cb = pb("cb", [P, 2, CH])
        yp = pb("yp", [P, 2, CH])
        pj = [pb(f"pj{i}", [P, CH]) for i in range(2)]

        s_w = sem("s_weights_loaded")
        s_cst = sem("s_constants_built")
        s_ap = sem("s_a_ready")
        s_gn = sem("s_gn_loaded")
        s_reset = sem("s_state_reset")
        s_x = [sem(f"s_x_loaded_{q}") for q in range(2)]
        s_xn = Counter(sem("s_xn_ready"), 1, 2)
        s_inp = Counter(sem("s_inproj_done"), 4)
        s_xs = Counter(sem("s_xs_ready"), 2)
        s_conv = Counter(sem("s_conv_step"), 9)
        s_silu = Counter(sem("s_silu_done"), 4)
        s_xp = Counter(sem("s_xproj_done"), 2)
        s_hi = Counter(sem("s_hi_ready"), 2)
        s_rest = Counter(sem("s_rest_ready"), 1)
        s_mid = Counter(sem("s_mid_ready"), 2)
        s_low = Counter(sem("s_low_ready"), 1)
        s_dt = Counter(sem("s_dtproj_done"), 2)
        s_lin = Counter(sem("s_lin_ready"), 2)
        s_abs = Counter(sem("s_abs_ready"), 2)
        s_exp = Counter(sem("s_softexp_ready"), 2)
        s_ln = Counter(sem("s_softln_ready"), 2)
        s_delta = Counter(sem("s_delta_ready"), 2)
        s_du = Counter(sem("s_du_ready"), 2, 2)
        s_da = Counter(sem("s_da_ready"), 2 * G, 2)
        s_bb = Counter(sem("s_b_spread"), 2 * G, 2)
        s_cb = Counter(sem("s_c_spread"), 2 * G, 2)
        s_cs = Counter(sem("s_c_copied"), 2 * G)
        s_m1 = Counter(sem("s_input_ready"), 4 * G, 2)
        s_c0 = Counter(sem("s_carry_in"), 2 * G)
        s_scan = Counter(sem("s_scanned"), 2 * G)
        s_cout = Counter(sem("s_carry_out"), 2 * G)
        s_hc = Counter(sem("s_hc_ready"), 2 * G)
        s_ysum = Counter(sem("s_y_summed"), 2 * G)
        s_yd = Counter(sem("s_y_skip"), 2)
        s_yg = Counter(sem("s_y_gated"), 2, 2)
        s_op = Counter(sem("s_outproj_done"), 1)
        s_img = Counter(sem("s_image_summed"), 1, 2)
        s_il = sem("s_image_loaded")
        s_st = sem("s_stored")
        block = ctx.enter_context(nc.Block())

        PAIRS = NCH // 2

        def chunks(eng, body):
            def within(b):
                with eng.Fori(1, PAIRS) as i:
                    f = b * NCH + i * 2
                    pair = b * PAIRS + i
                    body(Step(f - 2, f - 1, f, 0, b, i * 2, pair, b, i * 2 - 2))
                    body(Step(f - 1, f, f + 1, 1, b, i * 2 + 1, pair, b, i * 2 - 1))

            body(Step(None, None, 0, 0, 0, 0, 0, None, None, fresh_front=True))
            body(Step(None, 0, 1, 1, 0, 1, 0, None, None, fresh_core=True))
            with eng.Fori(0, B - 1) as b:
                within(b)
                f = b * NCH + NCH
                body(Step(f - 2, f - 1, f, 0, b + 1, 0, b * PAIRS + PAIRS, b, NCH - 2, fresh_front=True))
                body(Step(f - 1, f, f + 1, 1, b + 1, 1, b * PAIRS + PAIRS, b, NCH - 1, fresh_core=True))
            within(B - 1)
            body(Step(B * NCH - 2, B * NCH - 1, None, 0, None, None, None, B - 1, NCH - 2))
            body(Step(B * NCH - 1, None, None, 1, None, None, None, B - 1, NCH - 1))

        def credit(eng, *counters):
            for s in counters:
                eng.sem_inc(s.sem, s.per * s.ahead)

        @block.sync
        def _(sp):
            for dst, src in (
                (w_in[:, :], W_in), (w_conv[:, :, :], conv_w.rearrange("(h p) k -> p h k", p=P)),
                (v_convb[:, :], conv_b.rearrange("(h p) -> p h", p=P)),
                (w_xdt[:, :, :], W_xproj[:, 0:R].rearrange("(h p) r -> p h r", p=P)),
                (w_dt[:, :], W_dt), (v_bdt[:, :], b_dt.rearrange("(h p) -> p h", p=P)),
                (v_alog[:, :, :], A_log.rearrange("(h p) n -> p h n", p=P)),
                (v_d[:, :], D_param.rearrange("(h p) -> p h", p=P)),
                (w_out[:, :, :], W_out.rearrange("(h p) o -> p h o", p=P)),
                *((w_bc[:, :, 2 * N * j:2 * N * (j + 1)], W_xproj[:, R:].rearrange("(h p) r -> p h r", p=P)) for j in range(3)),
            ):
                sp.dma_start(dst, src, allow_slow_non_contiguous=True).then_inc(s_w, 16)

            def load_pixels(c, par, b, at):
                sp.wait_ge(s_xn.sem, s_xn.at(c, -1))
                sp.dma_start(xin[:, par, :], x1[bass.ds(b, 1), :, bass.ds(at * CH, CH)].rearrange("a p n -> p (a n)")).then_inc(s_x[par], 16)

            def load_image(b):
                for i in range(IP):
                    c0 = i * (HW // IP)
                    sp.dma_start(img_flat[:, c0:c0 + HW // IP], x1[bass.ds(b, 1), :, c0:c0 + HW // IP].rearrange("a p n -> p (a n)")).then_inc(s_il, 16)

            def store_image(b):
                sp.wait_ge(s_img.sem, s_img.at(b * NCH + NCH, 0))
                for i in range(IP):
                    c0 = i * (HW // IP)
                    sp.dma_start(out[bass.ds(b, 1), :, c0:c0 + HW // IP].rearrange("a p n -> p (a n)"), img_flat[:, c0:c0 + HW // IP]).then_inc(s_st, 16)
                sp.wait_ge(s_st, b * (16 * IP) + 16 * IP)

            def image(b, before):
                sp.wait_ge(s_xn.sem, s_xn.at(b * NCH, 0))
                sp.dma_start(gnb[:, :], gn2[bass.ds(b, 1), :, :].rearrange("a p t -> p (a t)")).then_inc(s_gn, 16)
                for at in range(4):
                    load_pixels(b * NCH + at, at % 2, b, at)
                if before:
                    store_image(b - 1)
                load_image(b)
                with sp.Fori(2, PAIRS) as i:
                    for par in range(2):
                        load_pixels(b * NCH + i * 2 + par, par, b, i * 2 + par)

            image(0, False)
            with sp.Fori(1, B) as b:
                image(b, True)
            store_image(B - 1)

        @block.tensor
        def _(pe):
            credit(pe, s_inp, s_xp, s_dt, s_bb, s_cb, s_ysum, s_op)
            pe.wait_ge(s_w, 16 * 12)
            pe.wait_ge(s_cst, 5)

            def front_a(f, pieces):
                if f is None:
                    return
                if 0 in pieces:
                    pe.wait_ge(s_xn.sem, s_xn.at(f, 1))
                for i in pieces:
                    if i < 2:
                        pe.wait_ge(s_lin.sem, s_lin.at(f, i - 1))
                    if i >= 2:
                        pe.wait_ge(s_xs.sem, s_xs.at(f, i - 1))
                    nc.tensor.matmul(pj[i % 2][:, :], w_in[:, i * P:(i + 1) * P], xn[:, :], start=True, stop=True).then_inc(s_inp.sem, 1)

            def front_bc(f, q):
                if f is None:
                    return
                pe.wait_ge(s_silu.sem, s_silu.at(f, 4))
                for h in range(2):
                    m = nc.tensor.matmul(pj[0][0:96, :], w_bc[:, h, :], xc[:, q, h, :], start=(h == 0), stop=(h == 1))
                m.then_inc(s_xp.sem, 1)

            def front_dt(f, q):
                if f is None:
                    return
                pe.wait_ge(s_silu.sem, s_silu.at(f, 4))
                for h in range(2):
                    m = nc.tensor.matmul(pj[1][0:R, :], w_xdt[:, h, :], xc[:, q, h, :], start=(h == 0), stop=(h == 1))
                m.then_inc(s_xp.sem, 1)

            def front_c(f, q, t):
                if f is None:
                    return
                pe.wait_ge(s_hi.sem, s_hi.at(f, 2))
                pe.wait_ge(s_rest.sem, s_rest.at(f, 1))
                for h in range(2):
                    if h == 1 and t is not None:
                        pe.wait_ge(s_img.sem, s_img.at(t, 1))
                    nc.tensor.matmul(pj[h][:, :], w_dt[:, h * P:(h + 1) * P], dt8[:, :], start=True, stop=True).then_inc(s_dt.sem, 1)

            def spread_b(c, q, u):
                if c is None:
                    return
                pe.wait_ge(s_low.sem, s_low.at(c, 1))
                pe.wait_ge(s_mid.sem, s_mid.at(c, 2))
                pe.wait_ge(s_m1.sem, s_m1.at(c, 2 * u))
                for j in range(2):
                    m = nc.tensor.matmul(bb[:, j, :], pick[:, 2 * u + j, :], parts[:, q, :], start=True, stop=True)
                m.then_inc(s_bb.sem, 1)

            def spread_c(c, q, p):
                if c is None:
                    return
                pe.wait_ge(s_low.sem, s_low.at(c, 1))
                pe.wait_ge(s_mid.sem, s_mid.at(c, 2))
                pe.wait_ge(s_cs.sem, s_cs.at(c, p))
                for j in range(2):
                    m = nc.tensor.matmul(cb[:, j, :], pick[:, N + 2 * p + j, :], parts[:, q, :], start=True, stop=True)
                m.then_inc(s_cb.sem, 1)

            def sum_y(c, g, h, states):
                if c is None:
                    return
                if 0 in states:
                    if g == 0:
                        pe.wait_ge(s_yd.sem, s_yd.at(c, h - 1))
                    pe.wait_ge(s_hc.sem, s_hc.at(c, 2 * g + h + 1))
                for n in states:
                    m = nc.tensor.matmul(yp[:, h, :], ident[:, :], hid[:, (2 * g + h) % 4, n, 1:], start=(g == 0 and n == 0), stop=(g == G - 1 and n == NG - 1), skip_group_check=True)
                if NG - 1 in states:
                    m.then_inc(s_ysum.sem, 1)

            def out_proj(t, c, f):
                if t is None:
                    return
                if f is not None:
                    pe.wait_ge(s_hi.sem, s_hi.at(f, 2))
                elif c is not None:
                    pe.wait_ge(s_lin.sem, s_lin.at(c, 2))
                else:
                    pe.wait_ge(s_img.sem, s_img.at(t, 0))
                for h in range(2):
                    pe.wait_ge(s_yg.sem, s_yg.at(t, h + 1))
                    m = nc.tensor.matmul(pj[1][:, :], w_out[:, h, :], y[:, h, :], start=(h == 0), stop=(h == 1))
                m.then_inc(s_op.sem, 1)

            def body(s):
                t, c, f, qf = s[:4]
                q = 1 - qf
                front_a(f, (0, 1))
                spread_b(c, q, 1)
                sum_y(t, 3, 0, (0, 1))
                spread_c(c, q, 1)
                sum_y(t, 3, 0, (2, 3))
                spread_c(c, q, 2)
                spread_b(c, q, 2)
                sum_y(t, 3, 1, (0, 1, 2, 3))
                front_a(f, (2, 3))
                spread_c(c, q, 3)
                sum_y(c, 0, 0, (0, 1))
                spread_b(c, q, 3)
                spread_c(c, q, 4)
                sum_y(c, 0, 0, (2, 3))
                front_bc(f, qf)
                front_dt(f, qf)
                spread_b(c, q, 4)
                sum_y(c, 0, 1, (0, 1, 2, 3))
                spread_c(c, q, 5)
                spread_b(c, q, 5)
                out_proj(t, c, f)
                sum_y(c, 1, 0, (0, 1))
                spread_c(c, q, 6)
                sum_y(c, 1, 0, (2, 3))
                front_c(f, qf, t)
                spread_b(c, q, 6)
                sum_y(c, 1, 1, (0, 1, 2, 3))
                spread_c(c, q, 7)
                spread_b(c, q, 7)
                sum_y(c, 2, 0, (0, 1, 2, 3))
                spread_b(f, qf, 0)
                sum_y(c, 2, 1, (0, 1))
                spread_c(f, qf, 0)
                sum_y(c, 2, 1, (2, 3))

            chunks(pe, body)

        @block.scalar
        def _(act):
            credit(act, s_xn, s_xs, s_silu, s_hi, s_mid, s_lin, s_abs, s_exp, s_ln, s_da, s_cs)
            act.wait_ge(s_w, 16 * 12)
            nc.scalar.activation(v_aexp[:, :, :], v_alog[:, :, :], ACT.Exp).then_inc(s_ap, 1)
            act.wait_ge(s_ap, 2)
            act.wait_ge(s_cst, 5)

            def exps(c, q, g, h):
                if c is None:
                    return
                act.wait_ge(s_scan.sem, s_scan.at(c, 2 * g + h - 3))
                if g == 0:
                    act.wait_ge(s_delta.sem, s_delta.at(c, h + 1))
                for n in range(NG):
                    m = nc.scalar.activation(da[:, (2 * g + h) % 4, n, 1:], delta[:, q, h, :], ACT.Exp, scale=v_a[:, h, NG * g + n:NG * g + n + 1])
                    if n == NG - 1:
                        m.then_inc(s_da.sem, 1)

            def copy_c(c, g, h):
                if c is None:
                    return
                if h == 0:
                    act.wait_ge(s_hc.sem, s_hc.at(c, 2 * (g - 1)))
                act.wait_ge(s_cb.sem, s_cb.at(c, 2 * g + h + 1))
                nc.scalar.activation(cs[:, g % 2, 2 * h:2 * h + 2, :], cb[:, :, :], ACT.Copy).then_inc(s_cs.sem, 1)

            def front_xn(s):
                if s.front is None:
                    return
                f, q = s.front, s.par
                act.wait_ge(s_x[q], s.front_pair * 16 + 16)
                if s.fresh_front:
                    act.wait_ge(s_gn, s.front_image * 16 + 16)
                act.wait_ge(s_inp.sem, s_inp.at(f, 0))
                nc.scalar.activation(xn[:, :], xin[:, q, :], ACT.Identity, bias=gnb[:, 1:2], scale=gnb[:, 0:1]).then_inc(s_xn.sem, 1)

            def front_xs(f):
                if f is None:
                    return
                for h in range(2):
                    act.wait_ge(s_inp.sem, s_inp.at(f, h + 1))
                    act.wait_ge(s_conv.sem, s_conv.at(f, 0))
                    nc.scalar.activation(xs[:, h, K4 - 1:], pj[h][:, :], ACT.Copy).then_inc(s_xs.sem, 1)

            def front_silu(f, q):
                if f is None:
                    return
                for h in range(2):
                    act.wait_ge(s_inp.sem, s_inp.at(f, h + 3))
                    act.wait_ge(s_yg.sem, s_yg.at(f, -2))
                    nc.scalar.activation(silu_z[:, q, h, :], pj[h][:, :], ACT.Silu).then_inc(s_silu.sem, 1)
                for h in range(2):
                    act.wait_ge(s_conv.sem, s_conv.at(f, 7 + h))
                    nc.scalar.activation(xc[:, q, h, :], conv[:, h, :], ACT.Silu).then_inc(s_silu.sem, 1)

            def front_parts(f, q):
                if f is None:
                    return
                act.wait_ge(s_xp.sem, s_xp.at(f, 1))
                act.wait_ge(s_cb.sem, s_cb.at(f, -2 * G))
                act.wait_ge(s_bb.sem, s_bb.at(f, -2 * G))
                nc.scalar.activation(parts[:, q, :], pj[0][0:96, :], ACT.Copy).then_inc(s_hi.sem, 1)

            def front_dt8(f):
                if f is None:
                    return
                act.wait_ge(s_xp.sem, s_xp.at(f, 2))
                act.wait_ge(s_dt.sem, s_dt.at(f, 0))
                nc.scalar.activation(dt8[:, :], pj[1][0:R, :], ACT.Copy).then_inc(s_hi.sem, 1)

            def front_mid(f, q):
                if f is None:
                    return
                act.wait_ge(s_rest.sem, s_rest.at(f, 1))
                act.wait_ge(s_hi.sem, s_hi.at(f, 1))
                nc.scalar.activation(parts[32:64, q, :], rest[32:64, :], ACT.Copy).then_inc(s_mid.sem, 1)
                act.wait_ge(s_low.sem, s_low.at(f, 0))
                nc.scalar.activation(mid[64:96, :], rest[64:96, :], ACT.Copy).then_inc(s_mid.sem, 1)

            def front_lin(f):
                if f is None:
                    return
                for h in range(2):
                    act.wait_ge(s_dt.sem, s_dt.at(f, h + 1))
                    act.wait_ge(s_delta.sem, s_delta.at(f, h - 1))
                    nc.scalar.activation(soft[:, h, :], pj[h][:, :], ACT.Abs, bias=v_bdt[:, h:h + 1]).then_inc(s_abs.sem, 1)
                    nc.scalar.activation(lin[:, h, :], pj[h][:, :], ACT.Identity, bias=v_bdt[:, h:h + 1]).then_inc(s_lin.sem, 1)

            def front_exp(f):
                if f is None:
                    return
                for h in range(2):
                    act.wait_ge(s_abs.sem, s_abs.at(f, h + 1))
                    nc.scalar.activation(soft[:, h, :], soft[:, h, :], ACT.Exp, scale=-1.0).then_inc(s_exp.sem, 1)

            def front_ln(f):
                if f is None:
                    return
                for h in range(2):
                    act.wait_ge(s_exp.sem, s_exp.at(f, h + 1))
                    nc.scalar.activation(soft[:, h, :], soft[:, h, :], ACT.Ln, bias=1.0).then_inc(s_ln.sem, 1)

            def body(s):
                t, c, f, qf = s[:4]
                q = 1 - qf
                front_xn(s)
                copy_c(c, 0, 0)
                exps(c, q, 0, 0)
                exps(c, q, 0, 1)
                copy_c(c, 0, 1)
                front_xs(f)
                exps(c, q, 1, 0)
                exps(c, q, 1, 1)
                copy_c(c, 1, 0)
                copy_c(c, 1, 1)
                front_silu(f, qf)
                exps(c, q, 2, 0)
                front_parts(f, qf)
                front_dt8(f)
                copy_c(c, 2, 0)
                copy_c(c, 2, 1)
                exps(c, q, 2, 1)
                exps(c, q, 3, 0)
                copy_c(c, 3, 0)
                front_mid(f, qf)
                front_lin(f)
                exps(c, q, 3, 1)
                front_exp(f)
                front_ln(f)
                copy_c(c, 3, 1)

            chunks(act, body)

        @block.vector
        def _(dve):
            credit(dve, s_conv, s_rest, s_low, s_delta, s_m1, s_c0, s_scan, s_cout, s_yd, s_img)
            nc.vector.memset(ident[:, :], 0.0).then_inc(s_cst, 1)
            nc.vector.memset(da[:, :, :, 0:1], 0.0).then_inc(s_cst, 1)
            dve.wait_ge(s_ap, 1)
            nc.vector.tensor_scalar(v_a[:, :, :], v_aexp[:, :, :], -1.0, None, ALU.mult).then_inc(s_ap, 1)
            dve.wait_ge(s_w, 16 * 12)
            dve.wait_ge(s_cst, 5)

            def front_conv(s):
                if s.front is None:
                    return
                f = s.front
                if s.fresh_front:
                    dve.wait_ge(s_conv.sem, s_conv.at(f, 0))
                    nc.vector.memset(xs[:, :, 0:K4 - 1], 0.0).then_inc(s_reset, 1)
                    dve.wait_ge(s_reset, s.front_image * 2 + 1)
                for h in range(2):
                    dve.wait_ge(s_xs.sem, s_xs.at(f, h + 1))
                    dve.wait_ge(s_silu.sem, s_silu.at(f, 0))
                    dve.wait_ge(s_delta.sem, s_delta.at(f, 0))
                    nc.vector.tensor_scalar(conv[:, h, :], xs[:, h, K4 - 1:], w_conv[:, h, K4 - 1:K4], v_convb[:, h:h + 1], ALU.mult, ALU.add).then_inc(s_conv.sem, 1)
                for t in range(K4 - 2, -1, -1):
                    for h in range(2):
                        dve.wait_ge(s_conv.sem, s_conv.at(f, 2 * (K4 - 2 - t) + h + 1))
                        nc.vector.scalar_tensor_tensor(conv[:, h, :], xs[:, h, t:t + CH], w_conv[:, h, t:t + 1], conv[:, h, :], ALU.mult, ALU.add).then_inc(s_conv.sem, 1)
                dve.wait_ge(s_conv.sem, s_conv.at(f, 8))
                nc.vector.tensor_copy(xs[:, :, 0:K4 - 1], xs[:, :, CH:CH + K4 - 1]).then_inc(s_conv.sem, 1)

            def front_rest(f, q):
                if f is None:
                    return
                dve.wait_ge(s_hi.sem, s_hi.at(f, 1))
                dve.wait_ge(s_mid.sem, s_mid.at(f, 0))
                dve.wait_ge(s_low.sem, s_low.at(f, 0))
                nc.vector.tensor_tensor(rest[:, :], pj[0][0:96, :], parts[:, q, :], ALU.subtract).then_inc(s_rest.sem, 1)

            def front_low(f, q):
                if f is None:
                    return
                dve.wait_ge(s_mid.sem, s_mid.at(f, 2))
                nc.vector.tensor_tensor(parts[64:96, q, :], rest[64:96, :], mid[64:96, :], ALU.subtract).then_inc(s_low.sem, 1)

            def front_delta(f, q):
                if f is None:
                    return
                for h in range(2):
                    dve.wait_ge(s_ln.sem, s_ln.at(f, h + 1))
                    dve.wait_ge(s_da.sem, s_da.at(f, -2 * G))
                    dve.wait_ge(s_du.sem, s_du.at(f, -2))
                    nc.vector.scalar_tensor_tensor(delta[:, q, h, :], lin[:, h, :], 0.0, soft[:, h, :], ALU.max, ALU.add).then_inc(s_delta.sem, 1)

            def inputs(c, q, u):
                if c is None:
                    return
                g = u // 2
                dve.wait_ge(s_bb.sem, s_bb.at(c, u + 1))
                for h in range(2):
                    slot = (2 * g + h) % 4
                    if u % 2 == 0:
                        dve.wait_ge(s_ysum.sem, s_ysum.at(c, 2 * g + h - 3))
                    if u == 0:
                        dve.wait_ge(s_du.sem, s_du.at(c, h + 1))
                    o = hid[:, slot, 2 * (u % 2):2 * (u % 2) + 2, 1:]
                    nc.vector.tensor_tensor(o, bb[:, :, :], du[:, q, h, :].unsqueeze(1).broadcast_to([P, 2, CH]), ALU.mult).then_inc(s_m1.sem, 1)

            def carry_in(c, g, h, fresh):
                if c is None:
                    return
                dve.wait_ge(s_cout.sem, s_cout.at(c, 2 * g + h - 3))
                first = hid[:, (2 * g + h) % 4, :, 0:1]
                if fresh:
                    nc.vector.memset(first, 0.0).then_inc(s_c0.sem, 1)
                else:
                    nc.vector.tensor_copy(first, carry[:, h, NG * g:NG * (g + 1)].unsqueeze(2)).then_inc(s_c0.sem, 1)

            def clear_last(s):
                if not s.fresh_core:
                    return
                dve.wait_ge(s_cout.sem, s_cout.at(s.core, 0))
                nc.vector.memset(carry[:, 1, N - NG:N], 0.0).then_inc(s_reset, 1)
                dve.wait_ge(s_reset, s.front_image * 2 + 2)

            def scan(c, g, h):
                if c is None:
                    return
                slot = (2 * g + h) % 4
                dve.wait_ge(s_c0.sem, s_c0.at(c, 2 * g + h + 1))
                dve.wait_ge(s_m1.sem, s_m1.at(c, 4 * g + h + 3))
                dve.wait_ge(s_da.sem, s_da.at(c, 2 * g + h + 1))
                flat = hid[:, slot, :, :].rearrange("p n t -> p (n t)")
                nc.vector.tensor_tensor_scan(flat, da[:, slot, :, :].rearrange("p n t -> p (n t)"), flat, 0.0, ALU.mult, ALU.add).then_inc(s_scan.sem, 1)
                dve.wait_ge(s_scan.sem, s_scan.at(c, 2 * g + h + 1))
                nc.vector.tensor_copy(carry[:, h, NG * g:NG * (g + 1)].unsqueeze(2), hid[:, slot, :, CH:CH + 1]).then_inc(s_cout.sem, 1)

            def image(s):
                if s.tail is None:
                    return
                dve.wait_ge(s_op.sem, s_op.at(s.tail, 1))
                dve.wait_ge(s_il, s.tail_image * (16 * IP) + 16 * IP)
                to = img[:, :, bass.ds(s.tail_at * 4, 4)]
                nc.vector.tensor_tensor(to, to, pj[1][:, :].rearrange("p (j i) -> p i j", j=4), ALU.add).then_inc(s_img.sem, 1)

            def skip(t, q, h):
                if t is None:
                    return
                dve.wait_ge(s_ysum.sem, s_ysum.at(t, 2 * G - 1 + h))
                dve.wait_ge(s_op.sem, s_op.at(t, 0))
                nc.vector.scalar_tensor_tensor(y[:, h, :], xc[:, q, h, :], v_d[:, h:h + 1], yp[:, h, :], ALU.mult, ALU.add).then_inc(s_yd.sem, 1)

            def body(s):
                t, c, f, qf = s[:4]
                q = 1 - qf
                carry_in(t, 3, 1, False)
                inputs(c, q, 0)
                scan(t, 3, 1)
                clear_last(s)
                carry_in(c, 0, 0, s.fresh_core)
                inputs(c, q, 1)
                scan(c, 0, 0)
                carry_in(c, 0, 1, s.fresh_core)
                skip(t, qf, 0)
                front_conv(s)
                skip(t, qf, 1)
                carry_in(c, 1, 0, s.fresh_core)
                inputs(c, q, 2)
                scan(c, 0, 1)
                carry_in(c, 1, 1, s.fresh_core)
                inputs(c, q, 3)
                scan(c, 1, 0)
                scan(c, 1, 1)
                carry_in(c, 2, 0, s.fresh_core)
                inputs(c, q, 4)
                front_rest(f, qf)
                inputs(c, q, 5)
                scan(c, 2, 0)
                carry_in(c, 2, 1, s.fresh_core)
                image(s)
                scan(c, 2, 1)
                carry_in(c, 3, 0, s.fresh_core)
                front_low(f, qf)
                inputs(c, q, 6)
                inputs(c, q, 7)
                front_delta(f, qf)
                scan(c, 3, 0)

            chunks(dve, body)

        @block.gpsimd
        def _(pool):
            credit(pool, s_du, s_hc, s_yg)
            pool.wait_ge(s_cst, 2)
            nc.gpsimd.affine_select(out=ident[:, :], in_=ident[:, :], compare_op=ALU.not_equal, fill=1.0, base=0, pattern=[[-1, P]], channel_multiplier=1).then_inc(s_cst, 1)
            nc.gpsimd.memset(pick[:, :, :], 0.0).then_inc(s_cst, 1)
            pool.wait_ge(s_cst, 4)
            for j in range(3):
                part = pick[32 * j:32 * (j + 1), :, :]
                m = nc.gpsimd.affine_select(out=part, in_=part, compare_op=ALU.not_equal, fill=1.0, base=0, pattern=[[-1, 2 * N], [0, P]], channel_multiplier=1)
            m.then_inc(s_cst, 1)

            def weigh(c, g, h):
                if c is None:
                    return
                pool.wait_ge(s_cs.sem, s_cs.at(c, 2 * (g + 1)))
                pool.wait_ge(s_cout.sem, s_cout.at(c, 2 * g + h + 1))
                slot = (2 * g + h) % 4
                nc.gpsimd.tensor_tensor(hid[:, slot, :, 1:], hid[:, slot, :, 1:], cs[:, g % 2, :, :], ALU.mult).then_inc(s_hc.sem, 1)

            def input_du(f, qf):
                if f is None:
                    return
                for h in range(2):
                    pool.wait_ge(s_delta.sem, s_delta.at(f, h + 1))
                    pool.wait_ge(s_silu.sem, s_silu.at(f, h + 3))
                    pool.wait_ge(s_m1.sem, s_m1.at(f, -4 * G))
                    nc.gpsimd.tensor_tensor(du[:, qf, h, :], delta[:, qf, h, :], xc[:, qf, h, :], ALU.mult).then_inc(s_du.sem, 1)

            def gate(t, q, h):
                if t is None:
                    return
                pool.wait_ge(s_yd.sem, s_yd.at(t, h + 1))
                nc.gpsimd.tensor_tensor(y[:, h, :], y[:, h, :], silu_z[:, q, h, :], ALU.mult).then_inc(s_yg.sem, 1)

            def body(s):
                t, c, f, qf = s[:4]
                weigh(t, 3, 1)
                weigh(c, 0, 0)
                gate(t, qf, 0)
                gate(t, qf, 1)
                weigh(c, 0, 1)
                weigh(c, 1, 0)
                weigh(c, 1, 1)
                weigh(c, 2, 0)
                weigh(c, 2, 1)
                input_du(f, qf)
                weigh(c, 3, 0)

            chunks(pool, body)


_L0 = ['temp_f', 'w1', 'b1', 'bn_gamma', 'bn_beta', 'bn_mean', 'bn_var', 'w2', 'b2', 'projf_w', 'temp_s', 'q1_w', 'q1_b', 'k1_w', 'k1_b', 'v1_w', 'v1_b', 'q3_w', 'q5_w', 'k3_w', 'k5_w', 'v3_w', 'v5_w', 'c3_w', 'c5_w', 'projs_w']
_L1 = ["W_in", "conv_w", "conv_b", "W_xproj", "W_dt", "b_dt", "A_log", "D_param", "W_out"]


def build(nc, x, out, table, shift_d, l0, l1):
    B = x.shape[0]

    def scratch(name, shape):
        return nc.dram_tensor(name, shape, F32, kind="Internal").ap()

    x1, gn2 = scratch("x1", (B, P, HW)), scratch("gn2", (B, P, 2))
    layer0(nc, B, x, table, shift_d, l0, scratch("kernels", (P, 4 * TAPS)), scratch("gated", (B, P, P, P)),
           scratch("heads", (B, P, HW)), x1, gn2)
    layer1(nc, x1, gn2, *(l1[n] for n in _L1), out.rearrange("b c i j -> b c (i j)"), B)


def kernel(**inputs):
    import numpy as _np
    import concourse.bacc as _bacc
    from concourse import mybir as _mybir
    from concourse.bass_utils import run_bass_kernel_spmd as _run

    nc = _bacc.Bacc("TRN2", target_bir_lowering=False, num_devices=1, dynamic_dma_scratch_size=1024)
    arrays, aps = {}, {}

    def feed(name, a):
        a = _np.ascontiguousarray(a)
        arrays[f"in_{name}"] = a
        aps[name] = nc.dram_tensor(f"in_{name}", a.shape, _mybir.dt.from_np(a.dtype), kind="ExternalInput").ap()

    for name, a in inputs.items():
        feed(name, a)
    feed("table", constants()[0])
    feed("shift_d", shifts())
    x = inputs["x"]
    out = nc.dram_tensor("out", x.shape, _mybir.dt.float32, kind="ExternalOutput").ap()
    build(nc, aps["x"], out, aps["table"], aps["shift_d"], {n: aps["L0_conv_" + n] for n in _L0}, {n: aps["L1_conv_" + n] for n in _L1})
    r = _run(nc, [arrays], core_ids=[0])
    return r.results[0]["out"]
```
